# Optimizing a Trainium2 kernel written in Bass

```python
import numpy as np
import jax
import jax.numpy as jnp

def _softmax(x, axis=-1):
    return jax.nn.softmax(x, axis=axis)

def _gelu(x):
    return jax.nn.gelu(x, approximate=True)

def _silu(x):
    return jax.nn.silu(x)

def _sigmoid(x):
    return jax.nn.sigmoid(x)

def _layernorm(x, axis=-1, eps=1e-05):
    m = jnp.mean(x, axis=axis, keepdims=True)
    v = jnp.var(x, axis=axis, keepdims=True)
    return (x - m) / jnp.sqrt(v + eps)

def _scatter_add(tgt, idx, src, axis=0):
    return tgt.at[idx].add(src)

def _segment_sum(src, seg, n):
    return jax.ops.segment_sum(src, seg, n)
kernel_name = 'mk_gnn_resnorm_d4_gnn_r32_541000'

def setup_inputs(seed: int=0):
    np.random.seed(seed)
    _w = jnp.asarray

    def _rec_inputs():
        import jax
        import jax.numpy as jnp
        _gk = jax.random.key(seed)
        x = -0.000202 + 1 * jax.random.normal(jax.random.fold_in(_gk, 1), (3125, 64), jnp.float32)
        _s = jax.random.randint(jax.random.fold_in(_gk, 2), (50000,), 0, 3125, jnp.int32)
        _d = jax.random.randint(jax.random.fold_in(_gk, 3), (50000,), 0, 3125, jnp.int32)
        _loop = jnp.arange(3125, dtype=jnp.int32)
        src = jnp.concatenate([_s, _d, _loop])
        dst = jnp.concatenate([_d, _s, _loop])
        _o = jnp.argsort(dst, stable=True)
        src = src[_o]
        dst = dst[_o]
        edge_attr_64 = 1.36993e-05 + 0.999972 * jax.random.normal(jax.random.fold_in(_gk, 12), (103125, 64), jnp.float32)
        edge_attr_9 = 0.000739051 + 0.999958 * jax.random.normal(jax.random.fold_in(_gk, 13), (103125, 9), jnp.float32)
        return (x, src, dst, edge_attr_64, edge_attr_9)
    x, src, dst, edge_attr_64, edge_attr_9 = _rec_inputs()

    def _L0_gnn_setup():
        import jax, jax.numpy as jnp
        import numpy as np
        N_NODES = 3125
        N_EDGES = 50000
        IN_C = 64
        OUT_C = 64
        BN_EPS = 1e-05
        key = jax.random.key(seed)
        ks = jax.random.split(key, 5)
        x = jax.random.normal(ks[0], (N_NODES, IN_C), dtype=jnp.float32)
        edge_index = jax.random.randint(ks[1], (2, N_EDGES), 0, N_NODES, dtype=jnp.int32)
        s = 1.0 / np.sqrt(IN_C)
        W_l = jax.random.normal(ks[2], (IN_C, OUT_C), dtype=jnp.float32) * s
        b_l = jnp.zeros((OUT_C,), dtype=jnp.float32)
        W_r = jax.random.normal(ks[3], (IN_C, OUT_C), dtype=jnp.float32) * s
        gamma = jnp.ones((OUT_C,), dtype=jnp.float32)
        beta = jnp.zeros((OUT_C,), dtype=jnp.float32)
        return {'x': x, 'edge_index': edge_index, 'W_l': W_l, 'b_l': b_l, 'W_r': W_r, 'gamma': gamma, 'beta': beta}
    _L0_gnn_all = _L0_gnn_setup()
    _L0_gnn_in = {k: v for k, v in _L0_gnn_all.items() if k in ('W_l', 'b_l', 'W_r', 'gamma', 'beta')}
    del _L0_gnn_all

    def _L1_gnn_setup():
        import jax, jax.numpy as jnp
        import numpy as np
        N_NODES = 3125
        N_EDGES = 50000
        D_IN = 64
        D_OUT = 64
        key = jax.random.key(seed)
        k_x, k_s, k_d, k_w = jax.random.split(key, 4)
        x = jax.random.normal(k_x, (N_NODES, D_IN), dtype=jnp.float32)
        src = jax.random.randint(k_s, (N_EDGES,), 0, N_NODES, dtype=jnp.int32)
        dst = jax.random.randint(k_d, (N_EDGES,), 0, N_NODES, dtype=jnp.int32)
        limit = float(np.sqrt(6.0 / (D_IN + D_OUT)))
        W = jax.random.uniform(k_w, (D_IN, D_OUT), dtype=jnp.float32, minval=-limit, maxval=limit)
        b = jnp.zeros((D_OUT,), dtype=jnp.float32)
        return {'x': x, 'src': src, 'dst': dst, 'W': W, 'b': b}
    _L1_gnn_all = _L1_gnn_setup()
    _L1_gnn_in = {k: v for k, v in _L1_gnn_all.items() if k in ('W', 'b')}
    del _L1_gnn_all

    def _L2_gnn_setup():
        import jax, jax.numpy as jnp
        import numpy as np
        N, E = (10000, 10000)
        D, S, HE = (64, 9, 64)
        H, DQK, DV = (8, 16, 16)
        OK, OV = (H * DQK, H * DV)
        EPS_BN = 1e-05

        def tensor_product(x_e, sh, w, C):
            acc = sh[:, 0:1] * (x_e @ C[:, 0, :])
            for s in range(1, S):
                acc = acc + sh[:, s:s + 1] * (x_e @ C[:, s, :])
            return acc * w

        def mlp2(x, w1, b1, w2, b2):
            return jax.nn.relu(x @ w1 + b1) @ w2 + b2
        key = jax.random.key(seed)
        ks = jax.random.split(key, 20)
        g = lambda k, shape, fan: jax.random.normal(k, shape, jnp.float32) / np.float32(np.sqrt(fan))
        return {'tfn_features': jax.random.normal(ks[0], (N, D), jnp.float32), 'edge_features': jax.random.normal(ks[1], (E, HE), jnp.float32), 'edge_sh': jax.random.normal(ks[2], (E, S), jnp.float32), 'Wq': g(ks[3], (D, OK), D), 'Cqk': g(ks[4], (D, S, OK), D * S), 'Cv': g(ks[5], (D, S, OV), D * S), 'k_w1': g(ks[6], (HE, HE), HE), 'k_b1': jnp.zeros((HE,), jnp.float32), 'k_w2': g(ks[7], (HE, OK), HE), 'k_b2': jnp.zeros((OK,), jnp.float32), 'v_w1': g(ks[8], (HE, HE), HE), 'v_b1': jnp.zeros((HE,), jnp.float32), 'v_w2': g(ks[9], (HE, OV), HE), 'v_b2': jnp.zeros((OV,), jnp.float32), 'W_out': g(ks[10], (OV, D), OV), 'W_self': g(ks[11], (D, D), D), 'gamma': jnp.ones((D,), jnp.float32), 'beta': jnp.zeros((D,), jnp.float32), 'edge_index': jax.random.randint(ks[12], (2, E), 0, N, dtype=jnp.int32)}
    _L2_gnn_all = _L2_gnn_setup()
    _L2_gnn_in = {k: v for k, v in _L2_gnn_all.items() if k in ('Wq', 'Cqk', 'Cv', 'k_w1', 'k_b1', 'k_w2', 'k_b2', 'v_w1', 'v_b1', 'v_w2', 'v_b2', 'W_out', 'W_self', 'gamma', 'beta')}
    del _L2_gnn_all

    def _L3_gnn_setup():
        import jax, jax.numpy as jnp
        import numpy as np
        N_NODES = 3125
        N_EDGES = 50000
        IN_DIM = 64
        OUT_DIM = 64
        key = jax.random.key(seed)
        k_x, k_e, k_wm, k_bm, k_wu, k_bu = jax.random.split(key, 6)
        x = jax.random.normal(k_x, (N_NODES, IN_DIM), dtype=jnp.float32)
        edge_index = jax.random.randint(k_e, (2, N_EDGES), 0, N_NODES, dtype=jnp.int64)
        lim_m = 1.0 / np.sqrt(2 * IN_DIM)
        lim_u = 1.0 / np.sqrt(IN_DIM + OUT_DIM)
        W_msg = jax.random.uniform(k_wm, (2 * IN_DIM, OUT_DIM), jnp.float32, -lim_m, lim_m)
        b_msg = jax.random.uniform(k_bm, (OUT_DIM,), jnp.float32, -lim_m, lim_m)
        W_upd = jax.random.uniform(k_wu, (IN_DIM + OUT_DIM, OUT_DIM), jnp.float32, -lim_u, lim_u)
        b_upd = jax.random.uniform(k_bu, (OUT_DIM,), jnp.float32, -lim_u, lim_u)
        return {'x': x, 'edge_index': edge_index, 'W_msg': W_msg, 'b_msg': b_msg, 'W_upd': W_upd, 'b_upd': b_upd}
    _L3_gnn_all = _L3_gnn_setup()
    _L3_gnn_in = {k: v for k, v in _L3_gnn_all.items() if k in ('W_msg', 'b_msg', 'W_upd', 'b_upd')}
    del _L3_gnn_all
    return {'x': x, 'src': src, 'dst': dst, 'edge_attr_64': edge_attr_64, 'edge_attr_9': edge_attr_9, 'L0_gnn_W_l': _L0_gnn_in['W_l'], 'L0_gnn_b_l': _L0_gnn_in['b_l'], 'L0_gnn_W_r': _L0_gnn_in['W_r'], 'L0_gnn_gamma': _L0_gnn_in['gamma'], 'L0_gnn_beta': _L0_gnn_in['beta'], 'L1_gnn_W': _L1_gnn_in['W'], 'L1_gnn_b': _L1_gnn_in['b'], 'L2_gnn_Wq': _L2_gnn_in['Wq'], 'L2_gnn_Cqk': _L2_gnn_in['Cqk'], 'L2_gnn_Cv': _L2_gnn_in['Cv'], 'L2_gnn_k_w1': _L2_gnn_in['k_w1'], 'L2_gnn_k_b1': _L2_gnn_in['k_b1'], 'L2_gnn_k_w2': _L2_gnn_in['k_w2'], 'L2_gnn_k_b2': _L2_gnn_in['k_b2'], 'L2_gnn_v_w1': _L2_gnn_in['v_w1'], 'L2_gnn_v_b1': _L2_gnn_in['v_b1'], 'L2_gnn_v_w2': _L2_gnn_in['v_w2'], 'L2_gnn_v_b2': _L2_gnn_in['v_b2'], 'L2_gnn_W_out': _L2_gnn_in['W_out'], 'L2_gnn_W_self': _L2_gnn_in['W_self'], 'L2_gnn_gamma': _L2_gnn_in['gamma'], 'L2_gnn_beta': _L2_gnn_in['beta'], 'L3_gnn_W_msg': _L3_gnn_in['W_msg'], 'L3_gnn_b_msg': _L3_gnn_in['b_msg'], 'L3_gnn_W_upd': _L3_gnn_in['W_upd'], 'L3_gnn_b_upd': _L3_gnn_in['b_upd']}

def reference(x, src, dst, edge_attr_64, edge_attr_9, L0_gnn_W_l, L0_gnn_b_l, L0_gnn_W_r, L0_gnn_gamma, L0_gnn_beta, L1_gnn_W, L1_gnn_b, L2_gnn_Wq, L2_gnn_Cqk, L2_gnn_Cv, L2_gnn_k_w1, L2_gnn_k_b1, L2_gnn_k_w2, L2_gnn_k_b2, L2_gnn_v_w1, L2_gnn_v_b1, L2_gnn_v_w2, L2_gnn_v_b2, L2_gnn_W_out, L2_gnn_W_self, L2_gnn_gamma, L2_gnn_beta, L3_gnn_W_msg, L3_gnn_b_msg, L3_gnn_W_upd, L3_gnn_b_upd):
    import jax
    import jax.numpy as jnp

    def _L0_gnn_ref(x, edge_index, W_l, b_l, W_r, gamma, beta):
        import jax, jax.numpy as jnp
        import numpy as np
        N_NODES = 3125
        N_EDGES = 50000
        IN_C = 64
        OUT_C = 64
        BN_EPS = 1e-05
        N = x.shape[0]
        src, dst = (edge_index[0], edge_index[1])
        summed = jax.ops.segment_sum(x[src], dst, num_segments=N)
        cnt = jax.ops.segment_sum(jnp.ones((src.shape[0],), x.dtype), dst, num_segments=N)
        agg = summed / jnp.maximum(cnt, 1.0)[:, None]
        h = agg @ W_l + b_l + x @ W_r
        mean = jnp.mean(h, axis=0)
        var = jnp.mean((h - mean) ** 2, axis=0)
        hn = (h - mean) * jax.lax.rsqrt(var + BN_EPS)
        return jax.nn.relu(hn * gamma + beta)

    def _L1_gnn_ref(x, src, dst, W, b):
        import jax, jax.numpy as jnp
        import numpy as np
        N_NODES = 3125
        N_EDGES = 50000
        D_IN = 64
        D_OUT = 64
        "DGL GraphConv with norm='both':\n            out = D_in^{-1/2} * A^T * (D_out^{-1/2} * x) @ W + b,\n            degrees clamped to a minimum of 1.\n            "
        n = x.shape[0]
        ones_e = jnp.ones(src.shape[0], dtype=x.dtype)
        out_deg = jax.ops.segment_sum(ones_e, src, num_segments=n)
        in_deg = jax.ops.segment_sum(ones_e, dst, num_segments=n)
        src_norm = jax.lax.rsqrt(jnp.maximum(out_deg, 1.0))
        dst_norm = jax.lax.rsqrt(jnp.maximum(in_deg, 1.0))
        h = x * src_norm[:, None]
        agg = jax.ops.segment_sum(h[src], dst, num_segments=n)
        agg = agg * dst_norm[:, None]
        return agg @ W + b

    def _L2_gnn_ref(tfn_features, edge_features, edge_sh, Wq, Cqk, Cv, k_w1, k_b1, k_w2, k_b2, v_w1, v_b1, v_w2, v_b2, W_out, W_self, gamma, beta, edge_index):
        import jax, jax.numpy as jnp
        import numpy as np
        N, E = (10000, 10000)
        D, S, HE = (64, 9, 64)
        H, DQK, DV = (8, 16, 16)
        OK, OV = (H * DQK, H * DV)
        EPS_BN = 1e-05

        def tensor_product(x_e, sh, w, C):
            acc = sh[:, 0:1] * (x_e @ C[:, 0, :])
            for s in range(1, S):
                acc = acc + sh[:, s:s + 1] * (x_e @ C[:, s, :])
            return acc * w

        def mlp2(x, w1, b1, w2, b2):
            return jax.nn.relu(x @ w1 + b1) @ w2 + b2
        edge_dst, edge_src = (edge_index[0], edge_index[1])
        n = tfn_features.shape[0]
        q = (tfn_features @ Wq).reshape(n, H, DQK)
        x_dst = tfn_features[edge_dst]
        wk = mlp2(edge_features, k_w1, k_b1, k_w2, k_b2)
        wv = mlp2(edge_features, v_w1, v_b1, v_w2, v_b2)
        k = tensor_product(x_dst, edge_sh, wk, Cqk).reshape(-1, H, DQK)
        v = tensor_product(x_dst, edge_sh, wv, Cv).reshape(-1, H, DV)
        attn = jnp.einsum('ehd,ehd->eh', q[edge_src], k)
        amax = jax.ops.segment_max(attn, edge_src, num_segments=n)
        ex = jnp.exp(attn - amax[edge_src])
        denom = jax.ops.segment_sum(ex, edge_src, num_segments=n)
        alpha = ex / (denom[edge_src] + 1e-16)
        upd = jax.ops.segment_sum(v * alpha[..., None], edge_src, num_segments=n)
        upd = upd.reshape(n, OV) @ W_out
        out = tfn_features @ W_self + upd
        mu = out.mean(axis=0)
        var = out.var(axis=0)
        return (out - mu) * jax.lax.rsqrt(var + EPS_BN) * gamma + beta

    def _L3_gnn_ref(x, edge_index, W_msg, b_msg, W_upd, b_upd):
        import jax, jax.numpy as jnp
        import numpy as np
        N_NODES = 3125
        N_EDGES = 50000
        IN_DIM = 64
        OUT_DIM = 64
        num_nodes = x.shape[0]
        source, target = (edge_index[0], edge_index[1])
        edge_feats = jnp.concatenate([x[source], x[target]], axis=-1)
        messages = jax.nn.relu(edge_feats @ W_msg + b_msg)
        agg_sum = jax.ops.segment_sum(messages, target, num_segments=num_nodes)
        counts = jax.ops.segment_sum(jnp.ones_like(target, dtype=x.dtype), target, num_segments=num_nodes)
        aggregated = agg_sum / jnp.clip(counts, 1.0, None)[:, None]
        updated = jax.nn.relu(jnp.concatenate([x, aggregated], axis=-1) @ W_upd + b_upd)
        return updated
    edge_index = jnp.stack([src, dst])
    x = _layernorm(x + _L0_gnn_ref(x, edge_index, L0_gnn_W_l, L0_gnn_b_l, L0_gnn_W_r, L0_gnn_gamma, L0_gnn_beta), axis=-1)
    x = _layernorm(x + _L1_gnn_ref(x, src, dst, L1_gnn_W, L1_gnn_b), axis=-1)
    x = _layernorm(x + _L2_gnn_ref(x, edge_attr_64, edge_attr_9, L2_gnn_Wq, L2_gnn_Cqk, L2_gnn_Cv, L2_gnn_k_w1, L2_gnn_k_b1, L2_gnn_k_w2, L2_gnn_k_b2, L2_gnn_v_w1, L2_gnn_v_b1, L2_gnn_v_w2, L2_gnn_v_b2, L2_gnn_W_out, L2_gnn_W_self, L2_gnn_gamma, L2_gnn_beta, edge_index), axis=-1)
    x = _layernorm(x + _L3_gnn_ref(x, edge_index, L3_gnn_W_msg, L3_gnn_b_msg, L3_gnn_W_upd, L3_gnn_b_upd), axis=-1)
    return x

_drawn_inputs = setup_inputs


def setup_inputs(seed=0):
    import zlib

    import numpy as np

    out = dict(_drawn_inputs(seed))
    spreads = {'L0_gnn_b_l': (0.0, 0.8),
     'L0_gnn_gamma': (1.0, 0.2),
     'L0_gnn_beta': (0.0, 0.1),
     'L1_gnn_b': (0.0, 0.1),
     'L2_gnn_k_b1': (0.0, 0.1),
     'L2_gnn_k_b2': (0.0, 0.1),
     'L2_gnn_v_b1': (0.0, 0.1),
     'L2_gnn_v_b2': (0.0, 0.1),
     'L2_gnn_gamma': (1.0, 0.2),
     'L2_gnn_beta': (0.0, 0.1)}
    factors = {'L3_gnn_b_msg': 5.523}
    for name, (base, spread) in spreads.items():
        noise = np.random.default_rng([zlib.crc32(name.encode()), seed]).standard_normal(out[name].shape)
        drawn = base * np.exp(spread * noise) if base else spread * noise
        out[name] = jnp.asarray(drawn.astype(out[name].dtype))
    for name, factor in factors.items():
        out[name] = (out[name] * factor).astype(out[name].dtype)
    return out
```

```python
from contextlib import ExitStack

import concourse.bass as bass
from concourse import mybir

F32 = mybir.dt.float32
BF16 = mybir.dt.bfloat16
I32 = mybir.dt.int32
ALU = mybir.AluOpType
ACT = mybir.ActivationFunctionType
AX_X = mybir.AxisListType.X

P = 128
D = 64
N = 3125
E = 103125
TG = 4
GE = TG * P
G = 2 * (-(-E // (2 * GE)))
T = G * TG
EP = T * P
NB = 26
NP = NB * P
PADN = 3200
NC = 8
CW = NP // NC
S_SH = 9
KC = 5
H = 8
DH = 16
HD = H * DH
EPS = 1e-5
DST_SCALE = 2.0 ** 113
LOWEST = -1e38
assert PADN + P <= NP and PADN >= N and NC * CW == NP and CW <= 512


class Phase:

    sems = []

    def __init__(self, nc, ctx, name):
        self.nc, self.ctx, self.name = nc, ctx, name

    def sem(self, name):
        handle = self.nc.alloc_semaphore(f"{self.name}_{name}")
        self.sems.append(handle)
        return handle

    def sb(self, name, shape, dt=F32):
        return self.ctx.enter_context(self.nc.sbuf_tensor(f"{self.name}_{name}", shape, dt))

    def ps(self, name, shape):
        return self.ctx.enter_context(self.nc.psum_tensor(f"{self.name}_{name}", shape, F32))


def recycle(nc):
    nc.clear_and_free_semaphores(Phase.sems)
    Phase.sems.clear()
    nc.all_engine_barrier()


def setup(nc, dram, sb):
    with ExitStack() as ctx:
        ph = Phase(nc, ctx, "setup")
        loaded = ph.sem("loaded")
        iota_done = ph.sem("iota_done")
        ident_zero = ph.sem("ident_zero")
        ident_done = ph.sem("ident_done")
        dst_float = ph.sem("dst_float")
        base_bcast = ph.sem("base_bcast")
        tables_done = ph.sem("tables_done")
        step = ph.sem("step")
        scaled_done = ph.sem("scaled_done")
        scaled_out = ph.sem("scaled_out")
        consts = ph.sem("consts")
        line_cur = ph.sb("line_cur", [P, T], I32)
        line_scaled = ph.sb("line_scaled", [P, T])
        before = ph.sb("before", [1, 1])
        dst_f = ph.sb("dst_f", [P, T])
        first_row = ph.sb("first_row", [P, P])
        tmp_i = ph.sb("tmp_i", [P, T], I32)
        base_ps = ph.ps("base_ps", [P, 2, 512])
        block = ctx.enter_context(nc.Block())

        loads = [
            (sb["src_i"][:, 0:T], dram["src_tab"]), (sb["dst_i"][:], dram["dst_tab"]),
            (line_cur[:], dram["dst_line"].rearrange("(p t) -> p t", p=P)),
            (sb["x_t"][:], dram["x_t"]),
        ]
        for name in ("L0_W_l", "L0_W_r", "L1_W", "L2_Wq", "L2_W_out", "L2_W_self"):
            loads.append((sb[name][:], dram[name]))
        for name in ("L0_b_l", "L0_gamma", "L0_beta", "L1_b", "L2_gamma", "L2_beta", "L3_b_upd"):
            loads.append((sb[name][:], dram[name].rearrange("(p a) -> p a", a=1)))
        loads.append((sb["L2_w1"][:, 0:D], dram["L2_k_w1"]))
        loads.append((sb["L2_w1"][:, D:2 * D], dram["L2_v_w1"]))
        loads.append((sb["L2_b1"][0:D, :], dram["L2_k_b1"].rearrange("(p a) -> p a", a=1)))
        loads.append((sb["L2_b1"][D:2 * D, :], dram["L2_v_b1"].rearrange("(p a) -> p a", a=1)))
        loads.append((sb["L2_w2"][0:D, :], dram["L2_k_w2"]))
        loads.append((sb["L2_w2"][D:2 * D, :], dram["L2_v_w2"]))
        loads.append((sb["L2_k_b2"][:], dram["L2_k_b2"].rearrange("(p a) -> p a", a=1)))
        loads.append((sb["L2_v_b2"][:], dram["L2_v_b2"].rearrange("(p a) -> p a", a=1)))
        for name in ("L2_Cqk", "L2_Cv"):
            loads.append((sb[name][:, 0:4, :], dram[name][0:4 * P, :].rearrange("(c p) o -> p c o", p=P)))
            loads.append((sb[name][0:D, 4, :], dram[name][4 * P:, :]))
        loads.append((sb["L3_W_msg"][:, 0:D], dram["L3_W_msg"][0:D, :]))
        loads.append((sb["L3_W_msg"][:, D:2 * D], dram["L3_W_msg"][D:2 * D, :]))
        loads.append((sb["L3_b_msg"][:], dram["L3_b_msg"].partition_broadcast(P)))
        loads.append((sb["L3_W_upd_x"][:], dram["L3_W_upd"][0:D, :]))
        loads.append((sb["L3_W_upd_a"][:], dram["L3_W_upd"][D:2 * D, :]))

        @block.sync
        def _(sp):
            for to, frm in loads:
                sp.dma_start(to, frm).then_inc(loaded, 16)
            sp.wait_ge(scaled_done, 2)
            sp.dma_start(dram["dst_scaled"][1:1 + EP].rearrange("(p t) -> p t", p=P), line_scaled[:]).then_inc(scaled_out, 16)
            sp.dma_start(dram["dst_scaled"][0:1].rearrange("(p t) -> p t", p=1), before[:]).then_inc(scaled_out, 16)
            sp.wait_ge(scaled_out, 32)

        @block.gpsimd
        def _(pool):
            pool.iota(sb["iota_row"][:], [[1, P]], base=0, channel_multiplier=0,
                      allow_small_or_imprecise_dtypes=True).then_inc(iota_done, 1)
            pool.iota(sb["iota_col"][:], [[0, 1]], base=0, channel_multiplier=1,
                      allow_small_or_imprecise_dtypes=True).then_inc(iota_done, 1)
            pool.memset(sb["ident"][:], 0.0).then_inc(ident_zero, 1)
            pool.memset(sb["head_sum"][:], 1.0).then_inc(ident_zero, 1)
            pool.memset(sb["mean_mat"][:], 1.0 / D).then_inc(consts, 1)
            pool.memset(sb["cnt_spread"][:], 0.0).then_inc(ident_zero, 1)
            pool.wait_ge(ident_zero, 3)
            pool.affine_select(out=sb["ident"][:], in_=sb["ident"][:], compare_op=ALU.not_equal, fill=1.0,
                               base=0, pattern=[[-1, P]], channel_multiplier=1).then_inc(ident_done, 1)
            pool.affine_select(out=sb["cnt_spread"][:], in_=sb["cnt_spread"][:], compare_op=ALU.not_equal,
                               fill=1.0, base=-D, pattern=[[0, D]], channel_multiplier=1).then_inc(ident_done, 1)
            by_head = sb["head_sum"][:].rearrange("p (h d) -> p h d", h=H)
            pool.affine_select(out=by_head, in_=by_head, compare_op=ALU.is_ge, fill=0.0,
                               base=0, pattern=[[-DH, H], [0, DH]], channel_multiplier=1).then_inc(ident_done, 1)
            pool.wait_ge(ident_done, 3)
            pool.affine_select(out=by_head, in_=by_head, compare_op=ALU.is_ge, fill=0.0,
                               base=DH - 1, pattern=[[DH, H], [0, DH]], channel_multiplier=-1).then_inc(ident_done, 1)

        @block.vector
        def _(dve):
            dve.memset(first_row[:], 0.0).then_inc(step, 1)
            dve.wait_ge(step, 1)
            dve.memset(first_row[0:1, :], 1.0).then_inc(step, 1)
            dve.wait_ge(loaded, 16 * len(loads))
            dve.tensor_copy(dst_f[:], sb["dst_i"][:]).then_inc(dst_float, 1)
            dve.tensor_scalar(line_scaled[:], line_cur[:], DST_SCALE, None, ALU.mult).then_inc(scaled_done, 1)
            dve.memset(before[:], -DST_SCALE).then_inc(scaled_done, 1)
            dve.tensor_scalar(tmp_i[:], sb["src_i"][:, 0:T], 7, None, ALU.logical_shift_right).then_inc(step, 1)
            dve.wait_ge(step, 3)
            dve.tensor_copy(sb["src_hi"][:], tmp_i[:]).then_inc(step, 1)
            dve.wait_ge(step, 4)
            dve.tensor_scalar(tmp_i[:], sb["src_i"][:, 0:T], 127, None, ALU.bitwise_and).then_inc(step, 1)
            dve.wait_ge(step, 5)
            dve.tensor_copy(sb["src_lo"][:], tmp_i[:]).then_inc(step, 1)
            dve.wait_ge(base_bcast, 1)
            dve.wait_ge(dst_float, 1)
            dve.wait_ge(iota_done, 2)
            half = T // 2
            dve.memset(sb["src_i"][:, T:], 0).then_inc(tables_done, 1)
            for k in range(2):
                cols = slice(k * half, (k + 1) * half)
                dve.tensor_tensor(sb["dst_local"][:, cols], dst_f[:, cols], base_ps[:, k, 0:half],
                                  ALU.subtract).then_inc(tables_done, 1)
                dve.tensor_scalar(sb["node_of_part"][:, cols], base_ps[:, k, 0:half], sb["iota_col"][:, 0:1],
                                  DST_SCALE, ALU.add, ALU.mult).then_inc(tables_done, 1)

        @block.tensor
        def _(pe):
            pe.wait_ge(step, 2)
            pe.wait_ge(dst_float, 1)
            half = T // 2
            for k in range(2):
                mm = nc.tensor.matmul(base_ps[:, k, 0:half], first_row[:], dst_f[:, k * half:(k + 1) * half],
                                      start=True, stop=True)
            mm.then_inc(base_bcast, 1)


def window_bases(nc, engine, sb, first_tile):
    return nc.values_load_multi_w_load_instructions(
        sb["dst_i"][0:1, bass.ds(first_tile, TG)], engines=[engine], min_val=0, max_val=PADN,
        skip_runtime_bounds_check_because="dst holds node numbers below N, and PADN")[1]


def sum_loop(nc, name, dram_table, sb, acc, counts):
    M = D + 1 if counts else D
    with ExitStack() as ctx:
        ph = Phase(nc, ctx, name)
        idx_ready = [ph.sem(f"idx_ready{p}") for p in range(2)]
        rows_in = [ph.sem(f"rows_in{p}") for p in range(2)]
        onehot_ready = ph.sem("onehot_ready")
        hist_ready = ph.sem("hist_ready")
        sums_ready = ph.sem("sums_ready")
        added = ph.sem("added")
        ones_set = ph.sem("ones_set")
        acc_clear = ph.sem("acc_clear")
        pool_go = ph.sem("pool_go")
        hist_done = ph.sem("hist_done")
        hist_copied = ph.sem("hist_copied")
        idx = [ph.sb(f"idx{p}", [P, TG], I32) for p in range(2)]
        rows = [ph.sb(f"rows{p}", [P, TG, M]) for p in range(2)]
        onehot = [ph.sb(f"onehot{p}", [P, TG, P]) for p in range(2)]
        sums = [ph.ps(f"sums{p}", [P, TG, P]) for p in range(2)]
        if counts:
            hi = [ph.sb(f"hi{p}", [P, TG, NB], BF16) for p in range(2)]
            lo = [ph.sb(f"lo{p}", [P, TG, P], BF16) for p in range(2)]
            zeros = ph.sb("zeros", [P, P], BF16)
            hist = ph.ps("hist", [P, P])
        block = ctx.enter_context(nc.Block())

        @block.scalar
        def _(act):
            def stage(g, n, p, first):
                if not first:
                    act.wait_ge(rows_in[p], 64 * n)
                nc.scalar.copy(idx[p][:], sb["src_i"][:, bass.ds(TG * g, TG)]).then_inc(idx_ready[p], 1)

            for p in range(2):
                stage(p, 0, p, True)
            with act.Fori(1, G // 2) as n:
                for p in range(2):
                    stage(2 * n + p, n, p, False)

        @block.gpsimd
        def _(pool):
            pool.wait_ge(ones_set, 2)

            def gather(g, n, p, first):
                pool.wait_ge(idx_ready[p], n + 1)
                if not first:
                    pool.wait_ge(sums_ready, g - 1)
                pool.sem_inc(pool_go, 1)
                for t in range(TG):
                    pool.indirect_dma_start(
                        rows[p][:, t, 0:D], None, dram_table,
                        bass.IndirectOffsetOnAxis(ap=idx[p][:, t:t + 1], axis=0)).then_inc(rows_in[p], 16)

            for p in range(2):
                gather(p, 0, p, True)
            with pool.Fori(1, G // 2) as n:
                for p in range(2):
                    gather(2 * n + p, n, p, False)

        @block.vector
        def _(dve):
            dve.memset(acc[:], 0.0).then_inc(acc_clear, 1)
            dve.wait_ge(acc_clear, 1)
            for p in range(2):
                dve.memset(rows[p][:], 1.0).then_inc(ones_set, 1)
            if counts:
                dve.memset(zeros[:], 0.0).then_inc(ones_set, 1)

            def build(g, p, first):
                if not first:
                    dve.wait_ge(sums_ready, g - 1)
                dve.tensor_tensor(onehot[p][:],
                                  sb["iota_row"][:].unsqueeze(1).to_broadcast([P, TG, P]),
                                  sb["dst_local"][:, bass.ds(TG * g, TG)].unsqueeze(2).to_broadcast([P, TG, P]),
                                  ALU.is_equal).then_inc(onehot_ready, 1)
                if counts:
                    dve.tensor_tensor(hi[p][:],
                                      sb["iota_row"][:, 0:NB].unsqueeze(1).to_broadcast([P, TG, NB]),
                                      sb["src_hi"][:, bass.ds(TG * g, TG)].unsqueeze(2).to_broadcast([P, TG, NB]),
                                      ALU.is_equal).then_inc(hist_ready, 1)
                    dve.tensor_tensor(lo[p][:],
                                      sb["iota_row"][:].unsqueeze(1).to_broadcast([P, TG, P]),
                                      sb["src_lo"][:, bass.ds(TG * g, TG)].unsqueeze(2).to_broadcast([P, TG, P]),
                                      ALU.is_equal).then_inc(hist_ready, 1)

            def add(g, p):
                bases = window_bases(nc, mybir.EngineType.DVE, sb, TG * g)
                for t in range(TG):
                    base = bases[t]
                    if t == 0:
                        dve.wait_ge(sums_ready, g + 1)
                    if not (isinstance(g, int) and g == 0 and t == 0):
                        dve.wait_ge(added, TG * g + t)
                    dve.tensor_tensor(acc[0:M, bass.ds(base, P)], acc[0:M, bass.ds(base, P)], sums[p][0:M, t, :],
                                      ALU.add).then_inc(added, 1)

            for p in range(2):
                build(p, p, True)
            for p in range(2):
                add(p, p)
                build(p + 2, p, False)
            with dve.Fori(1, G // 2 - 1) as n:
                for p in range(2):
                    add(2 * n + p, p)
                    build(2 * n + p + 2, p, False)
            for p in range(2):
                add(G - 2 + p, p)
            if counts:
                dve.wait_ge(hist_done, 1)
                dve.tensor_copy(sb["out_deg"][:], hist[0:NB, :]).then_inc(hist_copied, 1)

        @block.tensor
        def _(pe):
            if counts:
                pe.wait_ge(ones_set, 3)
                nc.tensor.matmul(hist[0:NB, :], zeros[:, 0:NB], zeros[:], start=True, stop=False)

            def product(g, n, p, first):
                pe.wait_ge(rows_in[p], 64 * (n + 1))
                pe.wait_ge(onehot_ready, g + 1)
                if not first:
                    pe.wait_ge(added, TG * (g - 1))
                if counts:
                    pe.wait_ge(hist_ready, 2 * (g + 1))
                    for t in range(TG):
                        nc.tensor.matmul(hist[0:NB, :], hi[p][:, t, :], lo[p][:, t, :], start=False, stop=False)
                for t in range(TG):
                    mm = nc.tensor.matmul(sums[p][0:M, t, :], rows[p][:, t, :], onehot[p][:, t, :],
                                          start=True, stop=True)
                mm.then_inc(sums_ready, 1)

            for p in range(2):
                product(p, 0, p, True)
            with pe.Fori(1, G // 2) as n:
                for p in range(2):
                    product(2 * n + p, n, p, False)
            if counts:
                nc.tensor.matmul(hist[0:NB, :], zeros[:, 0:NB], zeros[:], start=False, stop=True
                                 ).then_inc(hist_done, 1)

        if counts:
            @block.sync
            def _(sp):
                sp.wait_ge(hist_copied, 1)
                sp.dma_start(dram_deg_of(sb), sb["out_deg"][:]).then_inc(sb["deg_out_sem"], 16)
                sp.wait_ge(sb["deg_out_sem"], 16)


def dram_deg_of(sb):
    return sb["dram_out_deg"].rearrange("(a b) -> a b", a=NB)


def chunks(ps, rows=D):
    return ps[0:rows, :, 0:CW]


def nodes(t, rows=D):
    return t[0:rows, :].rearrange("p (c w) -> p c w", c=NC)


def node_products(nc, ps, terms, rows=D):
    for c in range(NC):
        for k, (w, x) in enumerate(terms):
            mm = nc.tensor.matmul(ps[0:rows, c, 0:CW], w, x[:, c * CW:(c + 1) * CW],
                                  start=(k == 0), stop=(k == len(terms) - 1))
    return mm


def count_reciprocals(nc, sb):
    with ExitStack() as ctx:
        ph = Phase(nc, ctx, "counts")
        spread, deg_in, step, rec_done, src_rec = (ph.sem(n) for n in ("spread", "deg_in", "step", "rec_done", "src_rec"))
        deg = ph.sb("deg", [D, NP])
        ps = ph.ps("ps", [P, NC, 512])
        block = ctx.enter_context(nc.Block())

        @block.sync
        def _(sp):
            sp.dma_start(deg[:], sb["dram_out_deg"].partition_broadcast(D)).then_inc(deg_in, 16)

        @block.tensor
        def _(pe):
            node_products(nc, ps, [(sb["cnt_spread"][:], sb["acc"][0:D + 1, :])]).then_inc(spread, 1)

        @block.vector
        def _(dve):
            dve.wait_ge(spread, 1)
            dve.tensor_scalar(nodes(sb["rec_in"]), chunks(ps), 1.0, None, ALU.max).then_inc(step, 1)
            dve.wait_ge(deg_in, 16)
            dve.tensor_scalar(deg[:], deg[:], 1.0, None, ALU.max).then_inc(step, 1)
            dve.wait_ge(step, 2)
            dve.reciprocal(sb["rec_in"][:], sb["rec_in"][:]).then_inc(rec_done, 1)
            dve.reciprocal(deg[:], deg[:]).then_inc(src_rec, 1)

        @block.scalar
        def _(act):
            act.wait_ge(rec_done, 1)
            nc.scalar.activation(sb["rsqrt_in"][:], sb["rec_in"][:], ACT.Sqrt).then_inc(step, 1)
            act.wait_ge(src_rec, 1)
            nc.scalar.activation(sb["rsqrt_out"][:], deg[:], ACT.Sqrt).then_inc(step, 1)


def node_linear(nc, name, sb, acc, factor, terms, bias, out, relu=False):
    with ExitStack() as ctx:
        ph = Phase(nc, ctx, name)
        scaled, summed, done = ph.sem("scaled"), ph.sem("summed"), ph.sem("done")
        agg = ph.sb("agg", [D, NP])
        ps = ph.ps("ps", [P, NC, 512])
        block = ctx.enter_context(nc.Block())

        @block.vector
        def _(dve):
            dve.tensor_tensor(agg[:], acc[0:D, :], factor[:], ALU.mult).then_inc(scaled, 1)

        @block.tensor
        def _(pe):
            pe.wait_ge(scaled, 1)
            node_products(nc, ps, [(w, agg[:] if x is None else x) for w, x in terms]).then_inc(summed, 1)

        @block.scalar
        def _(act):
            act.wait_ge(summed, 1)
            nc.scalar.activation(nodes(out), chunks(ps), ACT.Relu if relu else ACT.Identity,
                                 bias=bias[:, 0:1]).then_inc(done, 1)


def batch_norm(nc, name, sb, h, gamma, beta, relu):
    with ExitStack() as ctx:
        ph = Phase(nc, ctx, name)
        step, var_done, std_done, affine = (ph.sem(n) for n in ("step", "var_done", "std_done", "affine"))
        col = ph.sb("col", [D, 8])
        sq = ph.sb("sq", [D, N])
        block = ctx.enter_context(nc.Block())
        total, mean, sqsum, var, std, rstd, scale = (col[:, i:i + 1] for i in range(7))

        @block.vector
        def _(dve):
            dve.tensor_reduce(total, h[:, 0:N], AX_X, ALU.add).then_inc(step, 1)
            dve.wait_ge(step, 1)
            dve.tensor_scalar(mean, total, 1.0 / N, None, ALU.mult).then_inc(step, 1)
            dve.wait_ge(step, 2)
            dve.tensor_scalar(h[:], h[:], mean, None, ALU.subtract).then_inc(step, 1)
            dve.wait_ge(step, 3)
            dve.tensor_tensor(sq[:], h[:, 0:N], h[:, 0:N], ALU.mult).then_inc(step, 1)
            dve.wait_ge(step, 4)
            dve.tensor_reduce(sqsum, sq[:], AX_X, ALU.add).then_inc(step, 1)
            dve.wait_ge(step, 5)
            dve.tensor_scalar(var, sqsum, 1.0 / N, EPS, ALU.mult, ALU.add).then_inc(var_done, 1)
            dve.wait_ge(std_done, 1)
            dve.reciprocal(rstd, std).then_inc(step, 1)
            dve.wait_ge(step, 6)
            dve.tensor_tensor(scale, rstd, gamma[:], ALU.mult).then_inc(affine, 1)

        @block.scalar
        def _(act):
            act.wait_ge(var_done, 1)
            nc.scalar.activation(std, var, ACT.Sqrt).then_inc(std_done, 1)
            act.wait_ge(affine, 1)
            nc.scalar.activation(h[:], h[:], ACT.Relu if relu else ACT.Identity, bias=beta[:, 0:1],
                                 scale=scale).then_inc(std_done, 1)


def add_layer_norm(nc, name, sb, x, h):
    with ExitStack() as ctx:
        ph = Phase(nc, ctx, name)
        step, sum_done, mean_done, sq_done, var_done, std_done, done = (
            ph.sem(n) for n in ("step", "sum_done", "mean_done", "sq_done", "var_done", "std_done", "done"))
        sq = ph.sb("sq", [D, NP])
        ps = ph.ps("ps", [P, NC, 512])
        block = ctx.enter_context(nc.Block())

        @block.vector
        def _(dve):
            dve.tensor_tensor(x[:], x[:], h[:], ALU.add).then_inc(sum_done, 1)
            dve.wait_ge(mean_done, 1)
            dve.tensor_tensor(nodes(x), nodes(x), chunks(ps), ALU.subtract).then_inc(step, 1)
            dve.wait_ge(step, 1)
            dve.tensor_tensor(sq[:], x[:], x[:], ALU.mult).then_inc(sq_done, 1)
            dve.wait_ge(var_done, 1)
            dve.tensor_scalar(nodes(sq), chunks(ps), EPS, None, ALU.add).then_inc(step, 1)
            dve.wait_ge(std_done, 1)
            dve.reciprocal(sq[:], sq[:]).then_inc(step, 1)
            dve.wait_ge(step, 3)
            dve.tensor_tensor(x[:], x[:], sq[:], ALU.mult).then_inc(done, 1)

        @block.tensor
        def _(pe):
            pe.wait_ge(sum_done, 1)
            node_products(nc, ps, [(sb["mean_mat"][:], x)]).then_inc(mean_done, 1)
            pe.wait_ge(sq_done, 1)
            node_products(nc, ps, [(sb["mean_mat"][:], sq)]).then_inc(var_done, 1)

        @block.scalar
        def _(act):
            act.wait_ge(step, 2)
            nc.scalar.activation(sq[:], sq[:], ACT.Sqrt).then_inc(std_done, 1)


def write_rows(nc, name, sb, x, terms, width, outs, factor=None, bias=None):
    with ExitStack() as ctx:
        ph = Phase(nc, ctx, name)
        scaled, made, copied, out_sem = (ph.sem(n) for n in ("scaled", "made", "copied", "out"))
        rows = ph.sb("rows", [P, NB, width])
        xs = ph.sb("xs", [D, NP])
        ps = ph.ps("ps", [P, 2, 512])
        block = ctx.enter_context(nc.Block())
        per = 512 // width
        rounds = [range(r, min(r + per, NB)) for r in range(0, NB, per)]

        @block.vector
        def _(dve):
            if factor is None:
                dve.tensor_copy(xs[:], x[:]).then_inc(scaled, 1)
            else:
                dve.tensor_tensor(xs[:], x[:], factor[:], ALU.mult).then_inc(scaled, 1)
            for r, blocks in enumerate(rounds):
                dve.wait_ge(made, r + 1)
                k = len(blocks)
                src = ps[:, r % 2, 0:k * width].rearrange("p (b w) -> p b w", b=k)
                dst = rows[:, blocks[0]:blocks[0] + k, :]
                if bias is None:
                    dve.tensor_copy(dst, src).then_inc(copied, 1)
                else:
                    nc.vector.tensor_copy(dst[:, :, 0:D], src[:, :, 0:D])
                    dve.tensor_tensor(dst[:, :, D:2 * D], src[:, :, D:2 * D],
                                      bias[:].unsqueeze(1).to_broadcast([P, k, D]), ALU.add).then_inc(copied, 1)

        @block.tensor
        def _(pe):
            pe.wait_ge(scaled, 1)
            for r, blocks in enumerate(rounds):
                if r >= 2:
                    pe.wait_ge(copied, r - 1)
                for b in blocks:
                    at = (b - blocks[0]) * width
                    for col, w in terms:
                        o = ps[:, r % 2, at + col:at + col + (D if w is None else w.shape[1])]
                        if w is None:
                            mm = nc.tensor.transpose(o, xs[:, b * P:(b + 1) * P], sb["ident"][0:D, 0:D])
                        else:
                            mm = nc.tensor.matmul(o, xs[:, b * P:(b + 1) * P], w, start=True, stop=True)
                mm.then_inc(made, 1)

        @block.sync
        def _(sp):
            sp.wait_ge(copied, len(rounds))
            n = 0
            for to, col, w in outs:
                full = to.shape[0] // P
                sp.dma_start(to[0:full * P, :].rearrange("(b p) f -> p b f", p=P),
                             rows[:, 0:full, col:col + w]).then_inc(out_sem, 16)
                n += 16
                if to.shape[0] % P:
                    sp.dma_start(to[full * P:, :], rows[0:to.shape[0] % P, full, col:col + w]).then_inc(out_sem, 16)
                    n += 16
            sp.wait_ge(out_sem, n)


def attention_loop(nc, dram, sb):
    with ExitStack() as ctx:
        ph = Phase(nc, ctx, "attn")
        two = range(2)
        idx_ready = [ph.sem(f"idx_ready{p}") for p in two]
        rows_in = [ph.sem(f"rows_in{p}") for p in two]
        feat_in = [ph.sem(f"feat_in{p}") for p in two]
        sh_in = [ph.sem(f"sh_in{p}") for p in two]
        dst_in = [ph.sem(f"dst_in{p}") for p in two]
        qwin_in = [ph.sem(f"qwin_in{p}") for p in two]
        xt_ps, hid_ps, q_ps, w_ps, k_ps, v_ps, vt_ps, attn_ps, sum_ps = (
            ph.sem(n) for n in ("xt_ps", "hid_ps", "q_ps", "w_ps", "k_ps", "v_ps", "vt_ps", "attn_ps", "sum_ps"))
        pick_ready, z_ready, masked, ran, topped, shifted, onehot_ready, kw_ready, u_ready, vx_ready, vw_ready, dve_set = (
            ph.sem(n) for n in ("pick_ready", "z_ready", "masked", "ran", "topped", "shifted", "onehot_ready",
                                "kw_ready", "u_ready", "vx_ready", "vw_ready", "dve_set"))
        xt_sb, hid_sb, w_sb, ex_sb, vt_sb, sum_sb = (
            ph.sem(n) for n in ("xt_sb", "hid_sb", "w_sb", "ex_sb", "vt_sb", "sum_sb"))
        added, acc_clear = ph.sem("added"), ph.sem("acc_clear")
        STEPS = 2 + 2 * TG
        pool_go, pe_go = ph.sem("pool_go"), ph.sem("pe_go")

        idx = [ph.sb(f"idx{p}", [P, TG], I32) for p in two]
        rows = [ph.sb(f"rows{p}", [P, TG, 2 * D]) for p in two]
        feat = [ph.sb(f"feat{p}", [D, GE]) for p in two]
        sh = [ph.sb(f"sh{p}", [P, KC, GE]) for p in two]
        dst = [ph.sb(f"dst{p}", [P, GE + 1]) for p in two]
        qwin = [ph.sb(f"qwin{p}", [P, TG, HD]) for p in two]
        xt = [ph.sb(f"xt{p}", [P, GE]) for p in two]
        z = [ph.sb(f"z{p}", [P, KC, GE]) for p in two]
        hid = [ph.sb(f"hid{p}", [P, GE]) for p in two]
        wk = ph.sb("wk", [P, GE])
        wv = ph.sb("wv", [P, GE])
        pick = ph.sb("pick", [P, TG, P])
        onehot = ph.sb("onehot", [P, TG, P])
        u = ph.sb("u", [P, GE])
        vw = [ph.sb(f"vw{p}", [P, GE]) for p in two]
        vx = ph.sb("vx", [P, GE])
        mask = [ph.sb(f"mask{p}", [P, GE + 1]) for p in two]
        run = [ph.sb(f"run{p}", [P, GE]) for p in two]
        top = ph.sb("top", [P, GE])
        ex = [ph.sb(f"ex{p}", [P, GE + 1]) for p in two]
        zero = ph.sb("zero", [P, 1])
        vt = ph.sb("vt", [P, TG, HD])
        et = ph.sb("et", [P, TG, HD])
        sums = [ph.sb(f"sums{p}", [P, TG, P]) for p in two]
        dens = [ph.sb(f"dens{p}", [P, TG, P]) for p in two]

        b_xt, b_hid_vt, b_q, b_wk_sum, b_wv_den, b_k, b_v, b_attn = (
            ph.ps(n, [P, 512]) for n in ("b_xt", "b_hid_vt", "b_q", "b_wk_sum", "b_wv_den", "b_k", "b_v", "b_attn"))
        block = ctx.enter_context(nc.Block())
        rows_of = [P] * 4 + [D]

        def run_groups(eng, body, last_front=G):
            body(0, 0, 0, True, False)
            body(1, 0, 1, True, True)
            with eng.Fori(1, G // 2) as n:
                for p in two:
                    body(2 * n + p, n, p, True, True)
            body(G, G // 2, 0, False, True)

        def is_first(g, k):
            return isinstance(g, int) and g == k

        @block.scalar
        def _(act):
            def stage_idx(g, p):
                nc.scalar.copy(idx[p][:], sb["src_i"][:, bass.ds(TG * g, TG)]).then_inc(idx_ready[p], 1)

            def body(g, n, p, front, back):
                if front:
                    act.wait_ge(xt_ps, g + 1)
                    nc.scalar.copy(xt[p][:], b_xt[:]).then_inc(xt_sb, 1)
                    stage_idx(g + 2, p)
                    act.wait_ge(hid_ps, g + 1)
                    nc.scalar.activation(hid[p][:], b_hid_vt[:], ACT.Relu, bias=sb["L2_b1"][:, 0:1]).then_inc(hid_sb, 1)
                    act.wait_ge(w_ps, g + 1)
                    if not is_first(g, 0):
                        act.wait_ge(vw_ready, g)
                    nc.scalar.activation(wk[:], b_wk_sum[:], ACT.Identity, bias=sb["L2_k_b2"][:, 0:1]).then_inc(w_sb, 1)
                    nc.scalar.activation(wv[:], b_wv_den[:], ACT.Identity, bias=sb["L2_v_b2"][:, 0:1]).then_inc(w_sb, 1)
                if back:
                    q = 1 - p
                    act.wait_ge(shifted, 2 * g)
                    nc.scalar.activation(ex[q][:], ex[q][:], ACT.Exp).then_inc(ex_sb, 1)
                    act.wait_ge(vt_ps, g)
                    nc.scalar.copy(vt[:], b_hid_vt[:].rearrange("p (t c) -> p t c", t=TG)).then_inc(vt_sb, 1)
                    nc.scalar.copy(et[:], b_wv_den[:].rearrange("p (t c) -> p t c", t=TG)).then_inc(vt_sb, 1)
                    act.wait_ge(sum_ps, g)
                    if not (is_first(g, 1) or is_first(g, 2)):
                        act.wait_ge(added, STEPS * (g - 2))
                    nc.scalar.copy(sums[q][:], b_wk_sum[:].rearrange("p (t c) -> p t c", t=TG)).then_inc(sum_sb, 1)
                    nc.scalar.copy(dens[q][:], b_wv_den[:].rearrange("p (t c) -> p t c", t=TG)).then_inc(sum_sb, 1)

            stage_idx(0, 0)
            stage_idx(1, 1)
            body(0, 0, 0, True, False)
            body(1, 0, 1, True, True)
            body(2, 1, 0, True, True)
            body(3, 1, 1, True, True)
            with act.Fori(2, G // 2) as n:
                for p in two:
                    body(2 * n + p, n, p, True, True)
            body(G, G // 2, 0, False, True)

        @block.gpsimd
        def _(pool):
            def gather(g, n, p, first):
                pool.wait_ge(idx_ready[p], n + 1)
                if not first:
                    pool.wait_ge(xt_ps, g - 1)
                pool.sem_inc(pool_go, 1)
                for t in range(TG):
                    pool.indirect_dma_start(
                        rows[p][:, t, :], None, dram["x_twice"],
                        bass.IndirectOffsetOnAxis(ap=idx[p][:, t:t + 1], axis=0)).then_inc(rows_in[p], 16)

            def add(g, p):
                bases = window_bases(nc, mybir.EngineType.Pool, sb, TG * g)
                factor = ex[p][:, GE:GE + 1]
                steps = [(sb["acc"], bases[0], 1, factor, ALU.mult), (sb["den"], bases[0], 1, factor, ALU.mult)]
                for t in range(TG):
                    steps.append((sb["acc"], bases[t], P, sums[p][:, t, :], ALU.add))
                    steps.append((sb["den"], bases[t], P, dens[p][:, t, :], ALU.add))
                pool.wait_ge(sum_sb, 2 * (g + 1))
                for k, (acc, base, width, term, op) in enumerate(steps):
                    if k >= 2:
                        pool.wait_ge(added, STEPS * g + k - 1)
                    elif not is_first(g, 0):
                        pool.wait_ge(added, STEPS * g)
                    pool.sem_inc(pool_go, 1)
                    cols = bass.ds(base, width)
                    pool.tensor_tensor(acc[:, cols], acc[:, cols], term, op).then_inc(added, 1)

            pool.memset(sb["acc"][:], 0.0).then_inc(acc_clear, 1)
            pool.memset(sb["den"][:], 0.0).then_inc(acc_clear, 1)
            for p in two:
                gather(p, 0, p, True)
            pool.wait_ge(acc_clear, 2)
            gather(2, 1, 0, False)
            add(0, 0)
            gather(3, 1, 1, False)
            add(1, 1)
            with pool.Fori(2, G // 2) as n:
                for p in two:
                    gather(2 * n + p, n, p, False)
                    add(2 * n + p - 2, p)
            for p in two:
                add(G - 2 + p, p)

        @block.sync
        def _(sp):
            def load(g, n, p, first):
                edges = bass.ds(g * GE, GE)
                if not first:
                    sp.wait_ge(hid_ps, g - 1)
                sp.dma_start(feat[p][:], dram["edge_feat"][:, edges]).then_inc(feat_in[p], 16)
                bases = window_bases(nc, mybir.EngineType.SP, sb, TG * g)
                if not first:
                    sp.wait_ge(q_ps, g - 1)
                for t in range(TG):
                    sp.dma_start(qwin[p][:, t, :], dram["q_rows"][bass.ds(bases[t], P), :]).then_inc(qwin_in[p], 16)
                if not first:
                    sp.wait_ge(z_ready, KC * (g - 1))
                sp.dma_start(sh[p][0:D, :, :], dram["edge_sh"][0:S_SH:2, edges].partition_broadcast(D)
                             ).then_inc(sh_in[p], 16)
                sp.dma_start(sh[p][D:P, 0:4, :], dram["edge_sh"][1:S_SH:2, edges].partition_broadcast(D)
                             ).then_inc(sh_in[p], 16)
                if not first:
                    sp.wait_ge(masked, g - 1)
                sp.dma_start(dst[p][:], dram["dst_scaled"][bass.ds(g * GE, GE + 1)].partition_broadcast(P)
                             ).then_inc(dst_in[p], 16)

            for p in two:
                load(p, 0, p, True)
            with sp.Fori(1, G // 2) as n:
                for p in two:
                    load(2 * n + p, n, p, False)

        @block.tensor
        def _(pe):
            def body(g, n, p, front, back):
                q = 1 - p
                if front:
                    pe.wait_ge(rows_in[p], 64 * (n + 1))
                    for t in range(TG):
                        mm = nc.tensor.transpose(b_xt[:, t * P:(t + 1) * P], rows[p][:, t, :], sb["ident"][:])
                    mm.then_inc(xt_ps, 1)
                    pe.wait_ge(feat_in[p], 16 * (n + 1))
                    nc.tensor.matmul(b_hid_vt[:], sb["L2_w1"][:], feat[p][:], start=True, stop=True).then_inc(hid_ps, 1)
                    pe.wait_ge(qwin_in[p], 64 * (n + 1))
                    pe.wait_ge(pick_ready, g + 1)
                    for t in range(TG):
                        mm = nc.tensor.matmul(b_q[:, t * P:(t + 1) * P], qwin[p][:, t, :], pick[:, t, :],
                                              start=True, stop=True)
                    mm.then_inc(q_ps, 1)
                    pe.wait_ge(hid_sb, g + 1)
                    if back and not is_first(g, 1):
                        pe.wait_ge(sum_sb, 2 * (g - 1))
                        pe.sem_inc(pe_go, 1)
                    nc.tensor.matmul(b_wk_sum[:], sb["L2_w2"][0:D, :], hid[p][0:D, :], start=True, stop=True)
                    nc.tensor.matmul(b_wv_den[:], sb["L2_w2"][D:P, :], hid[p][D:P, :], start=True,
                                     stop=True).then_inc(w_ps, 1)
                    for c in range(KC):
                        r = rows_of[c]
                        pe.wait_ge(z_ready, KC * g + c + 1)
                        mm = nc.tensor.matmul(b_k[:], sb["L2_Cqk"][0:r, c, :], z[p][0:r, c, :],
                                              start=(c == 0), stop=(c == KC - 1))
                    mm.then_inc(k_ps, 1)
                    if back:
                        pe.wait_ge(vw_ready, g)
                    for c in range(KC):
                        r = rows_of[c]
                        mm = nc.tensor.matmul(b_v[:], sb["L2_Cv"][0:r, c, :], z[p][0:r, c, :],
                                              start=(c == 0), stop=(c == KC - 1))
                    mm.then_inc(v_ps, 1)
                if back:
                    pe.wait_ge(vx_ready, g)
                    if front:
                        pe.wait_ge(w_sb, 2 * (g + 1))
                    for t in range(TG):
                        nc.tensor.transpose(b_hid_vt[:, t * P:(t + 1) * P], vx[:, t * P:(t + 1) * P], sb["ident"][:])
                    for t in range(TG):
                        mm = nc.tensor.transpose(b_wv_den[:, t * P:(t + 1) * P], ex[q][:, t * P:(t + 1) * P],
                                                 sb["ident"][:])
                    mm.then_inc(vt_ps, 1)
                if front:
                    pe.wait_ge(u_ready, g + 1)
                    nc.tensor.matmul(b_attn[:], sb["head_sum"][:], u[:], start=True, stop=True).then_inc(attn_ps, 1)
                if back:
                    pe.wait_ge(vt_sb, 2 * g)
                    pe.wait_ge(onehot_ready, g)
                    for t in range(TG):
                        nc.tensor.matmul(b_wk_sum[:, t * P:(t + 1) * P], vt[:, t, :], onehot[:, t, :],
                                         start=True, stop=True)
                    for t in range(TG):
                        mm = nc.tensor.matmul(b_wv_den[:, t * P:(t + 1) * P], et[:, t, :], onehot[:, t, :],
                                              start=True, stop=True)
                    mm.then_inc(sum_ps, 1)

            run_groups(pe, body)

        @block.vector
        def _(dve):
            dve.memset(run[1][:], LOWEST).then_inc(dve_set, 1)
            dve.memset(mask[0][:, GE:GE + 1], 0.0).then_inc(dve_set, 1)
            dve.memset(mask[1][:, GE:GE + 1], 0.0).then_inc(dve_set, 1)
            dve.memset(zero[:], 0.0).then_inc(dve_set, 1)

            def backward(t, n):
                a = t[:]
                return bass.AP(a.tensor, a.offset + n - 1, [list(a.ap[0]), [-1, GE]])

            def body(g, n, p, front, back):
                q = 1 - p
                if front:
                    dve.wait_ge(dst_in[p], 16 * (n + 1))
                    dve.tensor_tensor(pick[:], dst[p][:, 1:GE + 1].rearrange("p (t e) -> p t e", t=TG),
                                      sb["node_of_part"][:, bass.ds(TG * g, TG)].unsqueeze(2).to_broadcast([P, TG, P]),
                                      ALU.is_equal).then_inc(pick_ready, 1)
                    dve.wait_ge(sh_in[p], 32 * (n + 1))
                    dve.wait_ge(xt_sb, g + 1)
                    for c in range(KC):
                        r = rows_of[c]
                        dve.tensor_tensor(z[p][0:r, c, :], xt[p][0:r, :], sh[p][0:r, c, :], ALU.mult).then_inc(z_ready, 1)
                    dve.tensor_tensor(mask[p][:, 0:GE], dst[p][:, 0:GE], dst[p][:, 1:GE + 1], ALU.subtract).then_inc(masked, 1)
                if back:
                    dve.wait_ge(attn_ps, g)
                    dve.wait_ge(masked, g)
                    dve.tensor_tensor_scan(run[q][:], mask[q][:, 0:GE], b_attn[:], run[p][:, GE - 1:GE],
                                           ALU.add, ALU.max).then_inc(ran, 1)
                    dve.wait_ge(ran, g)
                    dve.tensor_tensor_scan(backward(top, GE), backward(mask[q], GE + 1), backward(run[q], GE), LOWEST,
                                           ALU.add, ALU.max).then_inc(topped, 1)
                    if not front:
                        dve.wait_ge(sum_ps, g - 1)
                    dve.tensor_tensor(onehot[:], sb["iota_row"][:].unsqueeze(1).to_broadcast([P, TG, P]),
                                      sb["dst_local"][:, bass.ds(TG * g - TG, TG)].unsqueeze(2).to_broadcast([P, TG, P]),
                                      ALU.is_equal).then_inc(onehot_ready, 1)
                    dve.wait_ge(topped, g)
                    if not (is_first(g, 1) or is_first(g, 2)):
                        dve.wait_ge(added, STEPS * (g - 2))
                    dve.tensor_tensor(ex[q][:, 0:GE], b_attn[:], top[:], ALU.subtract).then_inc(shifted, 1)
                    dve.scalar_tensor_tensor(out=ex[q][:, GE:GE + 1], in0=run[p][:, GE - 1:GE], scalar=top[:, 0:1],
                                             in1=zero[:], op0=ALU.subtract, op1=ALU.min).then_inc(shifted, 1)
                if front:
                    dve.wait_ge(k_ps, g + 1)
                    dve.wait_ge(w_sb, 2 * (g + 1))
                    dve.tensor_tensor(u[:], b_k[:], wk[:], ALU.mult).then_inc(kw_ready, 1)
                    dve.wait_ge(q_ps, g + 1)
                    dve.wait_ge(kw_ready, g + 1)
                    dve.tensor_tensor(u[:], b_q[:], u[:], ALU.mult).then_inc(u_ready, 1)
                if back:
                    dve.wait_ge(ex_sb, g)
                    dve.wait_ge(vw_ready, g)
                    dve.tensor_tensor(vx[:], ex[q][:, 0:GE], vw[q][:], ALU.mult).then_inc(vx_ready, 1)
                if front:
                    dve.wait_ge(v_ps, g + 1)
                    dve.tensor_tensor(vw[p][:], b_v[:], wv[:], ALU.mult).then_inc(vw_ready, 1)

            dve.wait_ge(dve_set, 4)
            dve_body = body
            dve_body(0, 0, 0, True, False)
            dve_body(1, 0, 1, True, True)
            dve_body(2, 1, 0, True, True)
            dve_body(3, 1, 1, True, True)
            with dve.Fori(2, G // 2) as n:
                for p in two:
                    dve_body(2 * n + p, n, p, True, True)
            dve_body(G, G // 2, 0, False, True)


def attention_out(nc, sb, h):
    with ExitStack() as ctx:
        ph = Phase(nc, ctx, "attn_out")
        step, scaled, summed = (ph.sem(n) for n in ("step", "scaled", "summed"))
        ps = ph.ps("ps", [P, NC, 512])
        block = ctx.enter_context(nc.Block())

        @block.vector
        def _(dve):
            dve.tensor_scalar(sb["den"][:], sb["den"][:], 1e-16, None, ALU.add).then_inc(step, 1)
            dve.wait_ge(step, 1)
            dve.reciprocal(sb["den"][:], sb["den"][:]).then_inc(step, 1)
            dve.wait_ge(step, 2)
            dve.tensor_tensor(sb["acc"][:], sb["acc"][:], sb["den"][:], ALU.mult).then_inc(scaled, 1)
            dve.wait_ge(summed, 1)
            dve.tensor_copy(nodes(h), chunks(ps))

        @block.tensor
        def _(pe):
            pe.wait_ge(scaled, 1)
            node_products(nc, ps, [(sb["L2_W_self"][:], sb["x_t"]), (sb["L2_W_out"][:], sb["acc"])]).then_inc(summed, 1)


def message_loop(nc, dram, sb):
    with ExitStack() as ctx:
        ph = Phase(nc, ctx, "msg")
        two = range(2)
        idx_ready = [ph.sem(f"idx_ready{p}") for p in two]
        rows_in = [ph.sem(f"rows_in{p}") for p in two]
        dst_in = [ph.sem(f"dst_in{p}") for p in two]
        bwin_in = [ph.sem(f"bwin_in{p}") for p in two]
        pick_ready, onehot_ready, picked, pre_ready, msg_ready, sums_ready, added, pool_go, acc_clear = (
            ph.sem(n) for n in ("pick_ready", "onehot_ready", "picked", "pre_ready", "msg_ready", "sums_ready", "added",
                                "pool_go", "acc_clear"))
        idx = [ph.sb(f"idx{p}", [P, TG], I32) for p in two]
        rows = [ph.sb(f"rows{p}", [P, TG, D]) for p in two]
        dst = [ph.sb(f"dst{p}", [P, TG, P]) for p in two]
        bwin = [ph.sb(f"bwin{p}", [P, TG, D]) for p in two]
        pick = [ph.sb(f"pick{p}", [P, TG, P]) for p in two]
        onehot = [ph.sb(f"onehot{p}", [P, TG, P]) for p in two]
        pre = [ph.sb(f"pre{p}", [P, TG, D]) for p in two]
        msg = [ph.sb(f"msg{p}", [P, TG, D]) for p in two]
        at_dst = [ph.ps(f"at_dst{p}", [P, 512]) for p in two]
        sums = [ph.ps(f"sums{p}", [P, TG, P]) for p in two]
        block = ctx.enter_context(nc.Block())

        @block.scalar
        def _(act):
            def stage(g, p):
                nc.scalar.copy(idx[p][:], sb["src_i"][:, bass.ds(TG * g, TG)]).then_inc(idx_ready[p], 1)

            def relu(g, p, first):
                act.wait_ge(pre_ready, g + 1)
                if not first:
                    act.wait_ge(sums_ready, g - 1)
                nc.scalar.activation(msg[p][:], pre[p][:], ACT.Relu).then_inc(msg_ready, 1)

            for p in two:
                stage(p, p)
            for p in two:
                relu(p, p, True)
                stage(p + 2, p)
            with act.Fori(1, G // 2 - 1) as n:
                for p in two:
                    relu(2 * n + p, p, False)
                    stage(2 * n + p + 2, p)
            for p in two:
                relu(G - 2 + p, p, False)

        @block.gpsimd
        def _(pool):
            def gather(g, n, p, first):
                pool.wait_ge(idx_ready[p], n + 1)
                if not first:
                    pool.wait_ge(pre_ready, g - 1)
                pool.sem_inc(pool_go, 1)
                for t in range(TG):
                    pool.indirect_dma_start(
                        rows[p][:, t, :], None, dram["a_rows"],
                        bass.IndirectOffsetOnAxis(ap=idx[p][:, t:t + 1], axis=0)).then_inc(rows_in[p], 16)

            for p in two:
                gather(p, 0, p, True)
            with pool.Fori(1, G // 2) as n:
                for p in two:
                    gather(2 * n + p, n, p, False)

        @block.sync
        def _(sp):
            def load(g, p, first):
                if not first:
                    sp.wait_ge(pick_ready, g - 1)
                sp.dma_start(dst[p][:].rearrange("p t e -> p (t e)"),
                             dram["dst_scaled"][bass.ds(g * GE + 1, GE)].partition_broadcast(P)).then_inc(dst_in[p], 16)
                if not first:
                    sp.wait_ge(picked, g - 1)
                bases = window_bases(nc, mybir.EngineType.SP, sb, TG * g)
                for t in range(TG):
                    sp.dma_start(bwin[p][:, t, :], dram["b_rows"][bass.ds(bases[t], P), :]).then_inc(bwin_in[p], 16)

            for p in two:
                load(p, p, True)
            with sp.Fori(1, G // 2) as n:
                for p in two:
                    load(2 * n + p, p, False)

        @block.tensor
        def _(pe):
            def choose(g, n, p, first):
                pe.wait_ge(bwin_in[p], 64 * (n + 1))
                pe.wait_ge(pick_ready, g + 1)
                if not first:
                    pe.wait_ge(pre_ready, g - 1)
                for t in range(TG):
                    mm = nc.tensor.matmul(at_dst[p][:, t * D:(t + 1) * D], pick[p][:, t, :], bwin[p][:, t, :],
                                          start=True, stop=True)
                mm.then_inc(picked, 1)

            def total(g, p, first):
                pe.wait_ge(msg_ready, g + 1)
                pe.wait_ge(onehot_ready, g + 1)
                if not first:
                    pe.wait_ge(added, TG * (g - 1))
                for t in range(TG):
                    mm = nc.tensor.matmul(sums[p][0:D, t, :], msg[p][:, t, :], onehot[p][:, t, :], start=True, stop=True)
                mm.then_inc(sums_ready, 1)

            for p in two:
                choose(p, 0, p, True)
            for p in two:
                total(p, p, True)
                choose(2 + p, 1, p, False)
            with pe.Fori(1, G // 2 - 1) as n:
                for p in two:
                    total(2 * n + p, p, False)
                    choose(2 * n + 2 + p, n + 1, p, False)
            for p in two:
                total(G - 2 + p, p, False)

        @block.vector
        def _(dve):
            def build(g, n, p, first):
                dve.wait_ge(dst_in[p], 16 * (n + 1))
                if not first:
                    dve.wait_ge(sums_ready, g - 1)
                dve.tensor_tensor(pick[p][:], dst[p][:],
                                  sb["node_of_part"][:, bass.ds(TG * g, TG)].unsqueeze(2).to_broadcast([P, TG, P]),
                                  ALU.is_equal).then_inc(pick_ready, 1)
                dve.tensor_tensor(onehot[p][:], sb["iota_row"][:].unsqueeze(1).to_broadcast([P, TG, P]),
                                  sb["dst_local"][:, bass.ds(TG * g, TG)].unsqueeze(2).to_broadcast([P, TG, P]),
                                  ALU.is_equal).then_inc(onehot_ready, 1)

            def join(g, n, p, first):
                dve.wait_ge(rows_in[p], 64 * (n + 1))
                dve.wait_ge(picked, g + 1)
                if not first:
                    dve.wait_ge(msg_ready, g - 1)
                dve.tensor_tensor(pre[p][:], rows[p][:], at_dst[p][:, 0:TG * D].rearrange("p (t d) -> p t d", t=TG),
                                  ALU.add).then_inc(pre_ready, 1)

            def add(g, p):
                bases = window_bases(nc, mybir.EngineType.DVE, sb, TG * g)
                for t in range(TG):
                    base = bases[t]
                    if t == 0:
                        dve.wait_ge(sums_ready, g + 1)
                    if not (isinstance(g, int) and g == 0 and t == 0):
                        dve.wait_ge(added, TG * g + t)
                    cols = bass.ds(base, P)
                    dve.tensor_tensor(sb["acc"][0:D, cols], sb["acc"][0:D, cols], sums[p][0:D, t, :],
                                      ALU.add).then_inc(added, 1)

            dve.memset(sb["acc"][:], 0.0).then_inc(acc_clear, 1)
            dve.wait_ge(acc_clear, 1)
            for p in two:
                build(p, 0, p, True)
            for p in two:
                join(p, 0, p, True)
            for p in two:
                add(p, p)
                build(2 + p, 1, p, False)
                join(2 + p, 1, p, False)
            with dve.Fori(1, G // 2 - 1) as n:
                for p in two:
                    add(2 * n + p, p)
                    build(2 * n + 2 + p, n + 1, p, False)
                    join(2 * n + 2 + p, n + 1, p, False)
            for p in two:
                add(G - 2 + p, p)


def program(nc, dram, out):
    Phase.sems.clear()
    with ExitStack() as ctx:
        sb = {}

        def table(name, shape, dt=F32):
            sb[name] = ctx.enter_context(nc.sbuf_tensor(name, shape, dt))

        table("src_i", [P, T + 2 * TG], I32)
        table("dst_i", [P, T], I32)
        for name in ("src_hi", "src_lo", "dst_local", "node_of_part"):
            table(name, [P, T])
        table("iota_row", [P, P])
        table("iota_col", [P, 1])
        table("ident", [P, P])
        table("mean_mat", [D, D])
        table("cnt_spread", [D + 1, D])
        table("head_sum", [HD, HD])
        for name in ("L0_W_l", "L0_W_r", "L1_W", "L2_W_self", "L3_W_upd_x", "L3_W_upd_a"):
            table(name, [D, D])
        table("L2_W_out", [HD, D])
        table("L2_Wq", [D, HD])
        for name in ("L0_b_l", "L0_gamma", "L0_beta", "L1_b", "L2_gamma", "L2_beta", "L3_b_upd"):
            table(name, [D, 1])
        table("L2_w1", [D, 2 * D])
        table("L2_b1", [2 * D, 1])
        table("L2_w2", [2 * D, HD])
        table("L2_k_b2", [HD, 1])
        table("L2_v_b2", [HD, 1])
        table("L2_Cqk", [P, KC, HD])
        table("L2_Cv", [P, KC, HD])
        table("L3_W_msg", [D, 2 * D])
        table("L3_b_msg", [P, D])
        table("x_t", [D, NP])
        table("acc", [P, NP])
        table("den", [HD, NP])
        table("rec_in", [D, NP])
        table("out_deg", [NB, P])
        sb["deg_out_sem"] = ctx.enter_context(nc.semaphore("deg_out"))

        def scratch(name, shape):
            dram[name] = nc.dram_tensor(name, shape, F32, kind="Internal").ap()

        scratch("dst_scaled", (EP + 1,))
        scratch("out_deg_line", (NP,))
        scratch("x1_rows", (NP, D))
        scratch("x_twice", (NP, 2 * D))
        scratch("q_rows", (NP, HD))
        scratch("a_rows", (NP, D))
        scratch("b_rows", (NP, D))
        sb["dram_out_deg"] = dram["out_deg_line"]

        setup(nc, dram, sb)
        with ExitStack() as early:
            for name in ("h", "rsqrt_in", "rsqrt_out"):
                sb[name] = early.enter_context(nc.sbuf_tensor(name, [D, NP], F32))
            sum_loop(nc, "sum0", dram["x"], sb, sb["acc"], True)
            count_reciprocals(nc, sb)
            node_linear(nc, "lin0", sb, sb["acc"], sb["rec_in"],
                        [(sb["L0_W_l"][:], None), (sb["L0_W_r"][:], sb["x_t"])], sb["L0_b_l"], sb["h"])
            batch_norm(nc, "bn0", sb, sb["h"], sb["L0_gamma"], sb["L0_beta"], True)
            add_layer_norm(nc, "ln0", sb, sb["x_t"], sb["h"])
            write_rows(nc, "rows1", sb, sb["x_t"], [(0, None)], D, [(dram["x1_rows"], 0, D)], factor=sb["rsqrt_out"])
            sum_loop(nc, "sum1", dram["x1_rows"], sb, sb["acc"], False)
            node_linear(nc, "lin1", sb, sb["acc"], sb["rsqrt_in"], [(sb["L1_W"][:], None)], sb["L1_b"], sb["h"])
            add_layer_norm(nc, "ln1", sb, sb["x_t"], sb["h"])
        write_rows(nc, "rows2", sb, sb["x_t"], [(0, None), (D, None), (2 * D, sb["L2_Wq"][:])], 4 * D,
                   [(dram["x_twice"], 0, 2 * D), (dram["q_rows"], 2 * D, HD)])
        recycle(nc)
        attention_loop(nc, dram, sb)
        sb["h"] = ctx.enter_context(nc.sbuf_tensor("h_late", [D, NP], F32))
        attention_out(nc, sb, sb["h"])
        batch_norm(nc, "bn2", sb, sb["h"], sb["L2_gamma"], sb["L2_beta"], False)
        add_layer_norm(nc, "ln2", sb, sb["x_t"], sb["h"])
        write_rows(nc, "rows3", sb, sb["x_t"], [(0, sb["L3_W_msg"][:])], 2 * D,
                   [(dram["a_rows"], 0, D), (dram["b_rows"], D, D)], bias=sb["L3_b_msg"])
        message_loop(nc, dram, sb)
        node_linear(nc, "lin3", sb, sb["acc"], sb["rec_in"],
                    [(sb["L3_W_upd_x"][:], sb["x_t"]), (sb["L3_W_upd_a"][:], None)], sb["L3_b_upd"], sb["h"], relu=True)
        add_layer_norm(nc, "ln3", sb, sb["x_t"], sb["h"])
        write_rows(nc, "rows4", sb, sb["x_t"], [(0, None)], D, [(out, 0, D)])


def kernel(**inputs):
    import numpy as np
    import concourse.bacc as bacc
    from concourse.bass_utils import run_bass_kernel_spmd

    nc = bacc.Bacc("TRN2", target_bir_lowering=False, num_devices=1)
    a = {k: np.asarray(v) for k, v in inputs.items()}
    pad = EP - E
    src = np.concatenate([a["src"], np.full(pad, PADN, a["src"].dtype)])
    dst = np.concatenate([a["dst"], np.full(pad, PADN, a["dst"].dtype)])
    arrays = {
        "x": np.concatenate([a["x"], np.zeros((NP - N, D), a["x"].dtype)]),
        "x_t": np.concatenate([a["x"].T, np.zeros((D, NP - N), a["x"].dtype)], axis=1),
        "src_tab": src.reshape(T, P).T,
        "dst_tab": dst.reshape(T, P).T,
        "dst_line": dst,
        "edge_feat": np.concatenate([a["edge_attr_64"].T, np.zeros((D, pad), a["edge_attr_64"].dtype)], axis=1),
        "edge_sh": np.concatenate([a["edge_attr_9"].T, np.zeros((S_SH, pad), a["edge_attr_9"].dtype)], axis=1),
        "L2_Cqk": a["L2_gnn_Cqk"].transpose(1, 0, 2).reshape(S_SH * D, HD),
        "L2_Cv": a["L2_gnn_Cv"].transpose(1, 0, 2).reshape(S_SH * D, HD),
    }
    for name, value in a.items():
        short = name.replace("_gnn_", "_")
        if name[0] == "L" and short not in arrays:
            arrays[short] = value
    arrays = {k: np.ascontiguousarray(v) for k, v in arrays.items()}
    dram = {k: nc.dram_tensor("in_" + k, v.shape, mybir.dt.from_np(v.dtype), kind="ExternalInput").ap()
            for k, v in arrays.items()}
    out = nc.dram_tensor("out", (N, D), F32, kind="ExternalOutput").ap()
    program(nc, dram, out)
    r = run_bass_kernel_spmd(nc, [{"in_" + k: v for k, v in arrays.items()}], core_ids=[0])
    return r.results[0]["out"]
```

```python
from contextlib import ExitStack

import concourse.bass as bass
from concourse import mybir

F32 = mybir.dt.float32
F32R = mybir.dt.float32r
BF16 = mybir.dt.bfloat16
I32 = mybir.dt.int32
ALU = mybir.AluOpType
ACT = mybir.ActivationFunctionType
AX_X = mybir.AxisListType.X

P = 128
D = 64
N = 3125
E = 103125
TG = 4
GE = TG * P
G = 2 * (-(-E // (2 * GE)))
T = G * TG
EP = T * P
NB = 26
NP = NB * P
PADN = 3200
NC = 8
CW = NP // NC
S_SH = 9
KC = 5
H = 8
DH = 16
HD = H * DH
EPS = 1e-5
DST_SCALE = 2.0 ** 113
LOWEST = -1e38
assert PADN + P <= NP and PADN >= N and NC * CW == NP and CW <= 512


class Phase:

    sems = []

    def __init__(self, nc, ctx, name):
        self.nc, self.ctx, self.name = nc, ctx, name

    def sem(self, name):
        handle = self.nc.alloc_semaphore(f"{self.name}_{name}")
        self.sems.append(handle)
        return handle

    def sb(self, name, shape, dt=F32):
        return self.ctx.enter_context(self.nc.sbuf_tensor(f"{self.name}_{name}", shape, dt))

    def ps(self, name, shape):
        return self.ctx.enter_context(self.nc.psum_tensor(f"{self.name}_{name}", shape, F32))


def recycle(nc):
    nc.clear_and_free_semaphores(Phase.sems)
    Phase.sems.clear()
    nc.all_engine_barrier()


def setup(nc, dram, sb):
    with ExitStack() as ctx:
        ph = Phase(nc, ctx, "setup")
        loaded = ph.sem("loaded")
        iota_done = ph.sem("iota_done")
        ident_zero = ph.sem("ident_zero")
        ident_done = ph.sem("ident_done")
        dst_float = ph.sem("dst_float")
        base_bcast = ph.sem("base_bcast")
        tables_done = ph.sem("tables_done")
        step = ph.sem("step")
        scaled_done = ph.sem("scaled_done")
        scaled_out = ph.sem("scaled_out")
        consts = ph.sem("consts")
        split = ph.sem("split")
        line_cur = ph.sb("line_cur", [P, T], I32)
        line_scaled = ph.sb("line_scaled", [P, T])
        before = ph.sb("before", [1, 1])
        dst_f = ph.sb("dst_f", [P, T])
        first_row = ph.sb("first_row", [P, P])
        tmp_i = ph.sb("tmp_i", [P, T], I32)
        base_ps = ph.ps("base_ps", [P, 2, 512])
        paths = {name: ph.sb(name, [P, KC, HD]) for name in ("L2_Cqk", "L2_Cv")}
        block = ctx.enter_context(nc.Block())

        loads = [
            (sb["src_i"][:, 0:T], dram["src_tab"]), (sb["dst_i"][:], dram["dst_tab"]),
            (line_cur[:], dram["dst_line"].rearrange("(p t) -> p t", p=P)),
            (sb["x_t"][:], dram["x_t"]),
        ]
        for name in ("L0_W_l", "L0_W_r", "L1_W", "L2_Wq", "L2_W_out", "L2_W_self"):
            loads.append((sb[name][:], dram[name]))
        for name in ("L0_b_l", "L0_gamma", "L0_beta", "L1_b", "L2_gamma", "L2_beta", "L3_b_upd"):
            loads.append((sb[name][:], dram[name].rearrange("(p a) -> p a", a=1)))
        loads.append((sb["L2_w1"][:, 0:D], dram["L2_k_w1"]))
        loads.append((sb["L2_w1"][:, D:2 * D], dram["L2_v_w1"]))
        loads.append((sb["L2_b1"][0:D, :], dram["L2_k_b1"].rearrange("(p a) -> p a", a=1)))
        loads.append((sb["L2_b1"][D:2 * D, :], dram["L2_v_b1"].rearrange("(p a) -> p a", a=1)))
        loads.append((sb["L2_w2"][0:D, :], dram["L2_k_w2"]))
        loads.append((sb["L2_w2"][D:2 * D, :], dram["L2_v_w2"]))
        loads.append((sb["L2_k_b2"][:], dram["L2_k_b2"].rearrange("(p a) -> p a", a=1)))
        loads.append((sb["L2_v_b2"][:], dram["L2_v_b2"].rearrange("(p a) -> p a", a=1)))
        for name in ("L2_Cqk", "L2_Cv"):
            loads.append((paths[name][:, 0:4, :], dram[name][0:4 * P, :].rearrange("(c p) o -> p c o", p=P)))
            loads.append((paths[name][0:D, 4, :], dram[name][4 * P:, :]))
            loads.append((paths[name][D:P, 4, :], dram[name][4 * P:, :]))
        loads.append((sb["L3_W_msg"][:, 0:D], dram["L3_W_msg"][0:D, :]))
        loads.append((sb["L3_W_msg"][:, D:2 * D], dram["L3_W_msg"][D:2 * D, :]))
        loads.append((sb["L3_b_msg"][:], dram["L3_b_msg"].partition_broadcast(P)))
        loads.append((sb["L3_W_upd_x"][:], dram["L3_W_upd"][0:D, :]))
        loads.append((sb["L3_W_upd_a"][:], dram["L3_W_upd"][D:2 * D, :]))

        @block.sync
        def _(sp):
            for to, frm in loads:
                sp.dma_start(to, frm).then_inc(loaded, 16)
            sp.wait_ge(scaled_done, 2)
            sp.dma_start(dram["dst_scaled"][1:1 + EP].rearrange("(p t) -> p t", p=P), line_scaled[:]).then_inc(scaled_out, 16)
            sp.dma_start(dram["dst_scaled"][0:1].rearrange("(p t) -> p t", p=1), before[:]).then_inc(scaled_out, 16)
            sp.wait_ge(scaled_out, 32)

        @block.gpsimd
        def _(pool):
            pool.iota(sb["iota_row"][:], [[1, P]], base=0, channel_multiplier=0,
                      allow_small_or_imprecise_dtypes=True).then_inc(iota_done, 1)
            pool.iota(sb["iota_col"][:], [[0, 1]], base=0, channel_multiplier=1,
                      allow_small_or_imprecise_dtypes=True).then_inc(iota_done, 1)
            pool.memset(sb["ident"][:], 0.0).then_inc(ident_zero, 1)
            pool.memset(sb["head_sum"][:], 1.0).then_inc(ident_zero, 1)
            pool.memset(sb["mean_mat"][:], 1.0 / D).then_inc(consts, 1)
            pool.memset(sb["cnt_spread"][:], 0.0).then_inc(ident_zero, 1)
            pool.wait_ge(ident_zero, 3)
            pool.affine_select(out=sb["ident"][:], in_=sb["ident"][:], compare_op=ALU.not_equal, fill=1.0,
                               base=0, pattern=[[-1, P]], channel_multiplier=1).then_inc(ident_done, 1)
            pool.affine_select(out=sb["cnt_spread"][:], in_=sb["cnt_spread"][:], compare_op=ALU.not_equal,
                               fill=1.0, base=-D, pattern=[[0, D]], channel_multiplier=1).then_inc(ident_done, 1)
            by_head = sb["head_sum"][:].rearrange("p (h d) -> p h d", h=H)
            pool.affine_select(out=by_head, in_=by_head, compare_op=ALU.is_ge, fill=0.0,
                               base=0, pattern=[[-DH, H], [0, DH]], channel_multiplier=1).then_inc(ident_done, 1)
            pool.wait_ge(ident_done, 3)
            pool.affine_select(out=by_head, in_=by_head, compare_op=ALU.is_ge, fill=0.0,
                               base=DH - 1, pattern=[[DH, H], [0, DH]], channel_multiplier=-1).then_inc(ident_done, 1)

        @block.vector
        def _(dve):
            dve.memset(first_row[:], 0.0).then_inc(step, 1)
            dve.wait_ge(step, 1)
            dve.memset(first_row[0:1, :], 1.0).then_inc(step, 1)
            dve.wait_ge(loaded, 16 * len(loads))
            dve.tensor_copy(dst_f[:], sb["dst_i"][:]).then_inc(dst_float, 1)
            for k, name in enumerate(("L2_Cqk", "L2_Cv")):
                dve.tensor_copy(sb[name + "_hi"][:], paths[name][:]).then_inc(split, 1)
                dve.wait_ge(split, k + 1)
                dve.tensor_tensor(sb[name + "_lo"][:], paths[name][:], sb[name + "_hi"][:].bitcast(F32), ALU.subtract)
            dve.tensor_scalar(line_scaled[:], line_cur[:], DST_SCALE, None, ALU.mult).then_inc(scaled_done, 1)
            dve.memset(before[:], -DST_SCALE).then_inc(scaled_done, 1)
            dve.tensor_scalar(tmp_i[:], sb["src_i"][:, 0:T], 7, None, ALU.logical_shift_right).then_inc(step, 1)
            dve.wait_ge(step, 3)
            dve.tensor_copy(sb["src_hi"][:], tmp_i[:]).then_inc(step, 1)
            dve.wait_ge(step, 4)
            dve.tensor_scalar(tmp_i[:], sb["src_i"][:, 0:T], 127, None, ALU.bitwise_and).then_inc(step, 1)
            dve.wait_ge(step, 5)
            dve.tensor_copy(sb["src_lo"][:], tmp_i[:]).then_inc(step, 1)
            dve.wait_ge(base_bcast, 1)
            dve.wait_ge(dst_float, 1)
            dve.wait_ge(iota_done, 2)
            half = T // 2
            dve.memset(sb["src_i"][:, T:], 0).then_inc(tables_done, 1)
            for k in range(2):
                cols = slice(k * half, (k + 1) * half)
                dve.tensor_tensor(sb["dst_local"][:, cols], dst_f[:, cols], base_ps[:, k, 0:half],
                                  ALU.subtract).then_inc(tables_done, 1)
                dve.tensor_scalar(sb["node_of_part"][:, cols], base_ps[:, k, 0:half], sb["iota_col"][:, 0:1],
                                  DST_SCALE, ALU.add, ALU.mult).then_inc(tables_done, 1)

        @block.tensor
        def _(pe):
            pe.wait_ge(step, 2)
            pe.wait_ge(dst_float, 1)
            half = T // 2
            for k in range(2):
                mm = nc.tensor.matmul(base_ps[:, k, 0:half], first_row[:], dst_f[:, k * half:(k + 1) * half],
                                      start=True, stop=True)
            mm.then_inc(base_bcast, 1)


def window_bases(nc, engine, sb, first_tile):
    return nc.values_load_multi_w_load_instructions(
        sb["dst_i"][0:1, bass.ds(first_tile, TG)], engines=[engine], min_val=0, max_val=PADN,
        skip_runtime_bounds_check_because="dst holds node numbers below N, and PADN")[1]


def sum_loop(nc, name, dram_table, sb, acc, counts):
    M = D + 1 if counts else D
    with ExitStack() as ctx:
        ph = Phase(nc, ctx, name)
        idx_ready = [ph.sem(f"idx_ready{p}") for p in range(2)]
        rows_in = [ph.sem(f"rows_in{p}") for p in range(2)]
        onehot_ready = ph.sem("onehot_ready")
        hist_ready = ph.sem("hist_ready")
        sums_ready = ph.sem("sums_ready")
        added = ph.sem("added")
        ones_set = ph.sem("ones_set")
        acc_clear = ph.sem("acc_clear")
        pool_go = ph.sem("pool_go")
        hist_done = ph.sem("hist_done")
        hist_copied = ph.sem("hist_copied")
        idx = [ph.sb(f"idx{p}", [P, TG], I32) for p in range(2)]
        rows = [ph.sb(f"rows{p}", [P, TG, M]) for p in range(2)]
        onehot = [ph.sb(f"onehot{p}", [P, TG, P]) for p in range(2)]
        sums = [ph.ps(f"sums{p}", [P, TG, P]) for p in range(2)]
        if counts:
            hi = [ph.sb(f"hi{p}", [P, TG, NB], BF16) for p in range(2)]
            lo = [ph.sb(f"lo{p}", [P, TG, P], BF16) for p in range(2)]
            zeros = ph.sb("zeros", [P, P], BF16)
            hist = ph.ps("hist", [P, P])
        block = ctx.enter_context(nc.Block())

        @block.scalar
        def _(act):
            def stage(g, n, p, first):
                if not first:
                    act.wait_ge(rows_in[p], 64 * n)
                nc.scalar.copy(idx[p][:], sb["src_i"][:, bass.ds(TG * g, TG)]).then_inc(idx_ready[p], 1)

            for p in range(2):
                stage(p, 0, p, True)
            with act.Fori(1, G // 2) as n:
                for p in range(2):
                    stage(2 * n + p, n, p, False)

        @block.gpsimd
        def _(pool):
            pool.wait_ge(ones_set, 2)

            def gather(g, n, p, first):
                pool.wait_ge(idx_ready[p], n + 1)
                if not first:
                    pool.wait_ge(sums_ready, g - 1)
                pool.sem_inc(pool_go, 1)
                for t in range(TG):
                    pool.indirect_dma_start(
                        rows[p][:, t, 0:D], None, dram_table,
                        bass.IndirectOffsetOnAxis(ap=idx[p][:, t:t + 1], axis=0)).then_inc(rows_in[p], 16)

            for p in range(2):
                gather(p, 0, p, True)
            with pool.Fori(1, G // 2) as n:
                for p in range(2):
                    gather(2 * n + p, n, p, False)

        @block.vector
        def _(dve):
            dve.memset(acc[:], 0.0).then_inc(acc_clear, 1)
            dve.wait_ge(acc_clear, 1)
            for p in range(2):
                dve.memset(rows[p][:], 1.0).then_inc(ones_set, 1)
            if counts:
                dve.memset(zeros[:], 0.0).then_inc(ones_set, 1)

            def build(g, p, first):
                if not first:
                    dve.wait_ge(sums_ready, g - 1)
                dve.tensor_tensor(onehot[p][:],
                                  sb["iota_row"][:].unsqueeze(1).to_broadcast([P, TG, P]),
                                  sb["dst_local"][:, bass.ds(TG * g, TG)].unsqueeze(2).to_broadcast([P, TG, P]),
                                  ALU.is_equal).then_inc(onehot_ready, 1)
                if counts:
                    dve.tensor_tensor(hi[p][:],
                                      sb["iota_row"][:, 0:NB].unsqueeze(1).to_broadcast([P, TG, NB]),
                                      sb["src_hi"][:, bass.ds(TG * g, TG)].unsqueeze(2).to_broadcast([P, TG, NB]),
                                      ALU.is_equal).then_inc(hist_ready, 1)
                    dve.tensor_tensor(lo[p][:],
                                      sb["iota_row"][:].unsqueeze(1).to_broadcast([P, TG, P]),
                                      sb["src_lo"][:, bass.ds(TG * g, TG)].unsqueeze(2).to_broadcast([P, TG, P]),
                                      ALU.is_equal).then_inc(hist_ready, 1)

            def add(g, p):
                bases = window_bases(nc, mybir.EngineType.DVE, sb, TG * g)
                for t in range(TG):
                    base = bases[t]
                    if t == 0:
                        dve.wait_ge(sums_ready, g + 1)
                    if not (isinstance(g, int) and g == 0 and t == 0):
                        dve.wait_ge(added, TG * g + t)
                    dve.tensor_tensor(acc[0:M, bass.ds(base, P)], acc[0:M, bass.ds(base, P)], sums[p][0:M, t, :],
                                      ALU.add).then_inc(added, 1)

            for p in range(2):
                build(p, p, True)
            for p in range(2):
                add(p, p)
                build(p + 2, p, False)
            with dve.Fori(1, G // 2 - 1) as n:
                for p in range(2):
                    add(2 * n + p, p)
                    build(2 * n + p + 2, p, False)
            for p in range(2):
                add(G - 2 + p, p)
            if counts:
                dve.wait_ge(hist_done, 1)
                dve.tensor_copy(sb["out_deg"][:], hist[0:NB, :]).then_inc(hist_copied, 1)

        @block.tensor
        def _(pe):
            if counts:
                pe.wait_ge(ones_set, 3)
                nc.tensor.matmul(hist[0:NB, :], zeros[:, 0:NB], zeros[:], start=True, stop=False)

            def product(g, n, p, first):
                pe.wait_ge(rows_in[p], 64 * (n + 1))
                pe.wait_ge(onehot_ready, g + 1)
                if not first:
                    pe.wait_ge(added, TG * (g - 1))
                if counts:
                    pe.wait_ge(hist_ready, 2 * (g + 1))
                    for t in range(TG):
                        nc.tensor.matmul(hist[0:NB, :], hi[p][:, t, :], lo[p][:, t, :], start=False, stop=False)
                for t in range(TG):
                    mm = nc.tensor.matmul(sums[p][0:M, t, :], rows[p][:, t, :], onehot[p][:, t, :],
                                          start=True, stop=True)
                mm.then_inc(sums_ready, 1)

            for p in range(2):
                product(p, 0, p, True)
            with pe.Fori(1, G // 2) as n:
                for p in range(2):
                    product(2 * n + p, n, p, False)
            if counts:
                nc.tensor.matmul(hist[0:NB, :], zeros[:, 0:NB], zeros[:], start=False, stop=True
                                 ).then_inc(hist_done, 1)

        if counts:
            @block.sync
            def _(sp):
                sp.wait_ge(hist_copied, 1)
                sp.dma_start(dram_deg_of(sb), sb["out_deg"][:]).then_inc(sb["deg_out_sem"], 16)
                sp.wait_ge(sb["deg_out_sem"], 16)


def dram_deg_of(sb):
    return sb["dram_out_deg"].rearrange("(a b) -> a b", a=NB)


def chunks(ps, rows=D):
    return ps[0:rows, :, 0:CW]


def nodes(t, rows=D):
    return t[0:rows, :].rearrange("p (c w) -> p c w", c=NC)


def node_products(nc, ps, terms, rows=D):
    for c in range(NC):
        for k, (w, x) in enumerate(terms):
            mm = nc.tensor.matmul(ps[0:rows, c, 0:CW], w, x[:, c * CW:(c + 1) * CW],
                                  start=(k == 0), stop=(k == len(terms) - 1))
    return mm


def count_reciprocals(nc, sb):
    with ExitStack() as ctx:
        ph = Phase(nc, ctx, "counts")
        spread, deg_in, step, rec_done, src_rec = (ph.sem(n) for n in ("spread", "deg_in", "step", "rec_done", "src_rec"))
        deg = ph.sb("deg", [D, NP])
        ps = ph.ps("ps", [P, NC, 512])
        block = ctx.enter_context(nc.Block())

        @block.sync
        def _(sp):
            sp.dma_start(deg[:], sb["dram_out_deg"].partition_broadcast(D)).then_inc(deg_in, 16)

        @block.tensor
        def _(pe):
            node_products(nc, ps, [(sb["cnt_spread"][:], sb["acc"][0:D + 1, :])]).then_inc(spread, 1)

        @block.vector
        def _(dve):
            dve.wait_ge(spread, 1)
            dve.tensor_scalar(nodes(sb["rec_in"]), chunks(ps), 1.0, None, ALU.max).then_inc(step, 1)
            dve.wait_ge(deg_in, 16)
            dve.tensor_scalar(deg[:], deg[:], 1.0, None, ALU.max).then_inc(step, 1)
            dve.wait_ge(step, 2)
            dve.reciprocal(sb["rec_in"][:], sb["rec_in"][:]).then_inc(rec_done, 1)
            dve.reciprocal(deg[:], deg[:]).then_inc(src_rec, 1)

        @block.scalar
        def _(act):
            act.wait_ge(rec_done, 1)
            nc.scalar.activation(sb["rsqrt_in"][:], sb["rec_in"][:], ACT.Sqrt).then_inc(step, 1)
            act.wait_ge(src_rec, 1)
            nc.scalar.activation(sb["rsqrt_out"][:], deg[:], ACT.Sqrt).then_inc(step, 1)


def node_linear(nc, name, sb, acc, factor, terms, bias, out, relu=False):
    with ExitStack() as ctx:
        ph = Phase(nc, ctx, name)
        scaled, summed, done = ph.sem("scaled"), ph.sem("summed"), ph.sem("done")
        agg = ph.sb("agg", [D, NP])
        ps = ph.ps("ps", [P, NC, 512])
        block = ctx.enter_context(nc.Block())

        @block.vector
        def _(dve):
            dve.tensor_tensor(agg[:], acc[0:D, :], factor[:], ALU.mult).then_inc(scaled, 1)

        @block.tensor
        def _(pe):
            pe.wait_ge(scaled, 1)
            node_products(nc, ps, [(w, agg[:] if x is None else x) for w, x in terms]).then_inc(summed, 1)

        @block.scalar
        def _(act):
            act.wait_ge(summed, 1)
            nc.scalar.activation(nodes(out), chunks(ps), ACT.Relu if relu else ACT.Identity,
                                 bias=bias[:, 0:1]).then_inc(done, 1)


def batch_norm(nc, name, sb, h, gamma, beta, relu):
    with ExitStack() as ctx:
        ph = Phase(nc, ctx, name)
        step, var_done, std_done, affine = (ph.sem(n) for n in ("step", "var_done", "std_done", "affine"))
        col = ph.sb("col", [D, 8])
        sq = ph.sb("sq", [D, N])
        block = ctx.enter_context(nc.Block())
        total, mean, sqsum, var, std, rstd, scale = (col[:, i:i + 1] for i in range(7))

        @block.vector
        def _(dve):
            dve.tensor_reduce(total, h[:, 0:N], AX_X, ALU.add).then_inc(step, 1)
            dve.wait_ge(step, 1)
            dve.tensor_scalar(mean, total, 1.0 / N, None, ALU.mult).then_inc(step, 1)
            dve.wait_ge(step, 2)
            dve.tensor_scalar(h[:], h[:], mean, None, ALU.subtract).then_inc(step, 1)
            dve.wait_ge(step, 3)
            dve.tensor_tensor(sq[:], h[:, 0:N], h[:, 0:N], ALU.mult).then_inc(step, 1)
            dve.wait_ge(step, 4)
            dve.tensor_reduce(sqsum, sq[:], AX_X, ALU.add).then_inc(step, 1)
            dve.wait_ge(step, 5)
            dve.tensor_scalar(var, sqsum, 1.0 / N, EPS, ALU.mult, ALU.add).then_inc(var_done, 1)
            dve.wait_ge(std_done, 1)
            dve.reciprocal(rstd, std).then_inc(step, 1)
            dve.wait_ge(step, 6)
            dve.tensor_tensor(scale, rstd, gamma[:], ALU.mult).then_inc(affine, 1)

        @block.scalar
        def _(act):
            act.wait_ge(var_done, 1)
            nc.scalar.activation(std, var, ACT.Sqrt).then_inc(std_done, 1)
            act.wait_ge(affine, 1)
            nc.scalar.activation(h[:], h[:], ACT.Relu if relu else ACT.Identity, bias=beta[:, 0:1],
                                 scale=scale).then_inc(std_done, 1)


def add_layer_norm(nc, name, sb, x, h):
    with ExitStack() as ctx:
        ph = Phase(nc, ctx, name)
        step, sum_done, mean_done, sq_done, var_done, std_done, done = (
            ph.sem(n) for n in ("step", "sum_done", "mean_done", "sq_done", "var_done", "std_done", "done"))
        sq = ph.sb("sq", [D, NP])
        ps = ph.ps("ps", [P, NC, 512])
        block = ctx.enter_context(nc.Block())

        @block.vector
        def _(dve):
            dve.tensor_tensor(x[:], x[:], h[:], ALU.add).then_inc(sum_done, 1)
            dve.wait_ge(mean_done, 1)
            dve.tensor_tensor(nodes(x), nodes(x), chunks(ps), ALU.subtract).then_inc(step, 1)
            dve.wait_ge(step, 1)
            dve.tensor_tensor(sq[:], x[:], x[:], ALU.mult).then_inc(sq_done, 1)
            dve.wait_ge(var_done, 1)
            dve.tensor_scalar(nodes(sq), chunks(ps), EPS, None, ALU.add).then_inc(step, 1)
            dve.wait_ge(std_done, 1)
            dve.reciprocal(sq[:], sq[:]).then_inc(step, 1)
            dve.wait_ge(step, 3)
            dve.tensor_tensor(x[:], x[:], sq[:], ALU.mult).then_inc(done, 1)

        @block.tensor
        def _(pe):
            pe.wait_ge(sum_done, 1)
            node_products(nc, ps, [(sb["mean_mat"][:], x)]).then_inc(mean_done, 1)
            pe.wait_ge(sq_done, 1)
            node_products(nc, ps, [(sb["mean_mat"][:], sq)]).then_inc(var_done, 1)

        @block.scalar
        def _(act):
            act.wait_ge(step, 2)
            nc.scalar.activation(sq[:], sq[:], ACT.Sqrt).then_inc(std_done, 1)


def write_rows(nc, name, sb, x, terms, width, outs, factor=None, bias=None):
    with ExitStack() as ctx:
        ph = Phase(nc, ctx, name)
        scaled, made, copied, out_sem = (ph.sem(n) for n in ("scaled", "made", "copied", "out"))
        rows = ph.sb("rows", [P, NB, width])
        xs = ph.sb("xs", [D, NP])
        ps = ph.ps("ps", [P, 2, 512])
        block = ctx.enter_context(nc.Block())
        per = 512 // width
        rounds = [range(r, min(r + per, NB)) for r in range(0, NB, per)]

        @block.vector
        def _(dve):
            if factor is None:
                dve.tensor_copy(xs[:], x[:]).then_inc(scaled, 1)
            else:
                dve.tensor_tensor(xs[:], x[:], factor[:], ALU.mult).then_inc(scaled, 1)
            for r, blocks in enumerate(rounds):
                dve.wait_ge(made, r + 1)
                k = len(blocks)
                src = ps[:, r % 2, 0:k * width].rearrange("p (b w) -> p b w", b=k)
                dst = rows[:, blocks[0]:blocks[0] + k, :]
                if bias is None:
                    dve.tensor_copy(dst, src).then_inc(copied, 1)
                else:
                    nc.vector.tensor_copy(dst[:, :, 0:D], src[:, :, 0:D])
                    dve.tensor_tensor(dst[:, :, D:2 * D], src[:, :, D:2 * D],
                                      bias[:].unsqueeze(1).to_broadcast([P, k, D]), ALU.add).then_inc(copied, 1)

        @block.tensor
        def _(pe):
            pe.wait_ge(scaled, 1)
            for r, blocks in enumerate(rounds):
                if r >= 2:
                    pe.wait_ge(copied, r - 1)
                for b in blocks:
                    at = (b - blocks[0]) * width
                    for col, w in terms:
                        o = ps[:, r % 2, at + col:at + col + (D if w is None else w.shape[1])]
                        if w is None:
                            mm = nc.tensor.transpose(o, xs[:, b * P:(b + 1) * P], sb["ident"][0:D, 0:D])
                        else:
                            mm = nc.tensor.matmul(o, xs[:, b * P:(b + 1) * P], w, start=True, stop=True)
                mm.then_inc(made, 1)

        @block.sync
        def _(sp):
            sp.wait_ge(copied, len(rounds))
            n = 0
            for to, col, w in outs:
                full = to.shape[0] // P
                sp.dma_start(to[0:full * P, :].rearrange("(b p) f -> p b f", p=P),
                             rows[:, 0:full, col:col + w]).then_inc(out_sem, 16)
                n += 16
                if to.shape[0] % P:
                    sp.dma_start(to[full * P:, :], rows[0:to.shape[0] % P, full, col:col + w]).then_inc(out_sem, 16)
                    n += 16
            sp.wait_ge(out_sem, n)


def attention_loop(nc, dram, sb):
    with ExitStack() as ctx:
        ph = Phase(nc, ctx, "attn")
        two = range(2)
        idx_ready = [ph.sem(f"idx_ready{p}") for p in two]
        rows_in = [ph.sem(f"rows_in{p}") for p in two]
        feat_in = [ph.sem(f"feat_in{p}") for p in two]
        sh_in = [ph.sem(f"sh_in{p}") for p in two]
        dst_in = [ph.sem(f"dst_in{p}") for p in two]
        qwin_in = [ph.sem(f"qwin_in{p}") for p in two]
        xt_ps, hid_ps, q_ps, w_ps, k_ps, v_ps, vt_ps, attn_ps, sum_ps = (
            ph.sem(n) for n in ("xt_ps", "hid_ps", "q_ps", "w_ps", "k_ps", "v_ps", "vt_ps", "attn_ps", "sum_ps"))
        (pick_ready, z_ready, low_ready, ran, topped, shifted, onehot_ready, kw_ready, u_ready, vw_ready,
         dve_set) = (
            ph.sem(n) for n in ("pick_ready", "z_ready", "low_ready", "ran", "topped", "shifted", "onehot_ready",
                                "kw_ready", "u_ready", "vw_ready", "dve_set"))
        xt_sb, hid_sb, w_sb, ex_sb, vt_sb, sum_sb, high_sb = (
            ph.sem(n) for n in ("xt_sb", "hid_sb", "w_sb", "ex_sb", "vt_sb", "sum_sb", "high_sb"))
        masked, vx_ready = ph.sem("masked"), ph.sem("vx_ready")
        added, acc_clear = ph.sem("added"), ph.sem("acc_clear")
        STEPS = 2 + 2 * TG
        pool_go, pe_go = ph.sem("pool_go"), ph.sem("pe_go")

        idx = [ph.sb(f"idx{p}", [P, TG], I32) for p in two]
        rows = [ph.sb(f"rows{p}", [P, TG, 2 * D]) for p in two]
        feat = [ph.sb(f"feat{p}", [D, GE]) for p in two]
        sh = [ph.sb(f"sh{p}", [P, KC, GE]) for p in two]
        dst = [ph.sb(f"dst{p}", [P, GE + 1]) for p in two]
        qwin = [ph.sb(f"qwin{p}", [P, TG, HD]) for p in two]
        xt = [ph.sb(f"xt{p}", [P, GE]) for p in two]
        z = ph.sb("z", [P, 2, GE])
        z_hi = [ph.sb(f"z_hi{p}", [P, KC, GE], F32R) for p in two]
        z_lo = [ph.sb(f"z_lo{p}", [P, KC - 1, GE], F32R) for p in two]
        hid = [ph.sb(f"hid{p}", [P, GE]) for p in two]
        wk = ph.sb("wk", [P, GE])
        wv = ph.sb("wv", [P, GE])
        pick = ph.sb("pick", [P, TG, P])
        onehot = ph.sb("onehot", [P, TG, P])
        u = ph.sb("u", [P, GE])
        vw = [ph.sb(f"vw{p}", [P, GE]) for p in two]
        vx = ph.sb("vx", [P, GE])
        mask = [ph.sb(f"mask{p}", [P, GE + 1]) for p in two]
        run = [ph.sb(f"run{p}", [P, GE]) for p in two]
        top = ph.sb("top", [P, GE])
        ex = [ph.sb(f"ex{p}", [P, GE + 1]) for p in two]
        zero = ph.sb("zero", [P, 1])
        vt = ph.sb("vt", [P, TG, HD])
        et = ph.sb("et", [P, TG, HD])
        sums = [ph.sb(f"sums{p}", [P, TG, P]) for p in two]
        dens = [ph.sb(f"dens{p}", [P, TG, P]) for p in two]

        b_xt, b_hid_vt, b_q, b_wk_sum, b_wv_den, b_k, b_v, b_attn = (
            ph.ps(n, [P, 512]) for n in ("b_xt", "b_hid_vt", "b_q", "b_wk_sum", "b_wv_den", "b_k", "b_v", "b_attn"))
        block = ctx.enter_context(nc.Block())

        def run_rounds(eng, prepare, body):
            prepare(0, 0, 0)
            body(0, 0, 0, True, True, False)
            body(1, 0, 1, True, True, True)
            body(2, 1, 0, True, True, True)
            body(3, 1, 1, True, True, True)
            with eng.Fori(2, G // 2 - 1) as n:
                for p in two:
                    body(2 * n + p, n, p, True, True, True)
            body(G - 2, G // 2 - 1, 0, True, True, True)
            body(G - 1, G // 2 - 1, 1, False, True, True)
            body(G, G // 2, 0, False, False, True)

        def after(g, n, p):
            return g + 1, n + p, 1 - p

        def is_first(g, k):
            return isinstance(g, int) and g == k

        @block.scalar
        def _(act):
            def stage_idx(g, p):
                nc.scalar.copy(idx[p][:], sb["src_i"][:, bass.ds(TG * g, TG)]).then_inc(idx_ready[p], 1)

            def prepare(g, n, p):
                act.wait_ge(xt_ps, g + 1)
                nc.scalar.copy(xt[p][:], b_xt[:]).then_inc(xt_sb, 1)
                stage_idx(g + 2, p)
                act.wait_ge(hid_ps, g + 1)
                nc.scalar.activation(hid[p][:], b_hid_vt[:], ACT.Relu, bias=sb["L2_b1"][:, 0:1]).then_inc(hid_sb, 1)
                for c in range(3):
                    high(g, p, c)

            def high(g, p, c):
                act.wait_ge(z_ready, KC * g + c + 1)
                nc.scalar.copy(z_hi[p][:, c, :], z[:, c % 2, :]).then_inc(high_sb, 1)

            def body(g, n, p, next, front, back):
                q = 1 - p
                if next:
                    prepare(*after(g, n, p))
                if front:
                    act.wait_ge(w_ps, g + 1)
                    if not is_first(g, 0):
                        act.wait_ge(vw_ready, g)
                    nc.scalar.activation(wk[:], b_wk_sum[:], ACT.Identity, bias=sb["L2_k_b2"][:, 0:1]).then_inc(w_sb, 1)
                if next:
                    high(g + 1, q, 3)
                if front:
                    nc.scalar.activation(wv[:], b_wv_den[:], ACT.Identity, bias=sb["L2_v_b2"][:, 0:1]).then_inc(w_sb, 1)
                if next:
                    high(g + 1, q, 4)
                if back:
                    act.wait_ge(vt_ps, g)
                    nc.scalar.copy(vt[:], b_hid_vt[:].rearrange("p (t c) -> p t c", t=TG)).then_inc(vt_sb, 1)
                    nc.scalar.copy(et[:], b_wv_den[:].rearrange("p (t c) -> p t c", t=TG)).then_inc(vt_sb, 1)
                if front:
                    act.wait_ge(shifted, 2 * g + 2)
                    nc.scalar.activation(ex[p][:], ex[p][:], ACT.Exp).then_inc(ex_sb, 1)
                if back:
                    act.wait_ge(sum_ps, g)
                    if not (is_first(g, 1) or is_first(g, 2)):
                        act.wait_ge(added, STEPS * (g - 2))
                    nc.scalar.copy(sums[q][:], b_wk_sum[:].rearrange("p (t c) -> p t c", t=TG)).then_inc(sum_sb, 1)
                    nc.scalar.copy(dens[q][:], b_wv_den[:].rearrange("p (t c) -> p t c", t=TG)).then_inc(sum_sb, 1)

            def first(g, n, p):
                prepare(g, n, p)
                high(g, p, 3)
                high(g, p, 4)

            stage_idx(0, 0)
            stage_idx(1, 1)
            run_rounds(act, first, body)

        @block.gpsimd
        def _(pool):
            def gather(g, n, p, first):
                pool.wait_ge(idx_ready[p], n + 1)
                if not first:
                    pool.wait_ge(xt_ps, g - 1)
                pool.sem_inc(pool_go, 1)
                for t in range(TG):
                    pool.indirect_dma_start(
                        rows[p][:, t, :], None, dram["x_twice"],
                        bass.IndirectOffsetOnAxis(ap=idx[p][:, t:t + 1], axis=0)).then_inc(rows_in[p], 16)

            def add(g, p):
                bases = window_bases(nc, mybir.EngineType.Pool, sb, TG * g)
                factor = ex[p][:, GE:GE + 1]
                steps = [(sb["acc"], bases[0], 1, factor, ALU.mult), (sb["den"], bases[0], 1, factor, ALU.mult)]
                for t in range(TG):
                    steps.append((sb["acc"], bases[t], P, sums[p][:, t, :], ALU.add))
                    steps.append((sb["den"], bases[t], P, dens[p][:, t, :], ALU.add))
                pool.wait_ge(sum_sb, 2 * (g + 1))
                for k, (acc, base, width, term, op) in enumerate(steps):
                    if k >= 2:
                        pool.wait_ge(added, STEPS * g + k - 1)
                    elif not is_first(g, 0):
                        pool.wait_ge(added, STEPS * g)
                    pool.sem_inc(pool_go, 1)
                    cols = bass.ds(base, width)
                    pool.tensor_tensor(acc[:, cols], acc[:, cols], term, op).then_inc(added, 1)

            pool.memset(sb["acc"][:], 0.0).then_inc(acc_clear, 1)
            pool.memset(sb["den"][:], 0.0).then_inc(acc_clear, 1)
            def make_mask(g, n, p, first):
                pool.wait_ge(dst_in[p], 16 * (n + 1))
                if not first:
                    pool.wait_ge(topped, g - 1)
                pool.tensor_tensor(mask[p][:, 0:GE], dst[p][:, 0:GE], dst[p][:, 1:GE + 1], ALU.subtract).then_inc(masked, 1)

            def weigh(g, p):
                pool.wait_ge(ex_sb, g + 1)
                pool.wait_ge(vw_ready, g + 1)
                if not is_first(g, 0):
                    pool.wait_ge(vt_ps, g)
                pool.tensor_tensor(vx[:], ex[p][:, 0:GE], vw[p][:], ALU.mult).then_inc(vx_ready, 1)

            for p in two:
                gather(p, 0, p, True)
            make_mask(0, 0, 0, True)
            pool.wait_ge(acc_clear, 2)
            gather(2, 1, 0, False)
            make_mask(1, 0, 1, True)
            weigh(0, 0)
            gather(3, 1, 1, False)
            make_mask(2, 1, 0, False)
            weigh(1, 1)
            add(0, 0)
            with pool.Fori(2, G // 2) as n:
                gather(2 * n, n, 0, False)
                make_mask(2 * n - 1, n - 1, 1, False)
                weigh(2 * n - 2, 0)
                add(2 * n - 3, 1)
                gather(2 * n + 1, n, 1, False)
                make_mask(2 * n, n, 0, False)
                weigh(2 * n - 1, 1)
                add(2 * n - 2, 0)
            make_mask(G - 1, G // 2 - 1, 1, False)
            weigh(G - 2, 0)
            add(G - 3, 1)
            weigh(G - 1, 1)
            add(G - 2, 0)
            add(G - 1, 1)

        @block.sync
        def _(sp):
            def load(g, n, p, first):
                edges = bass.ds(g * GE, GE)
                if not first:
                    sp.wait_ge(hid_ps, g - 1)
                sp.dma_start(feat[p][:], dram["edge_feat"][:, edges]).then_inc(feat_in[p], 16)
                bases = window_bases(nc, mybir.EngineType.SP, sb, TG * g)
                if not first:
                    sp.wait_ge(z_ready, KC * (g - 1))
                for k in two:
                    sp.dma_start(sh[p][k * D:(k + 1) * D, :, :], dram["edge_sh"][k::2, edges].partition_broadcast(D)
                                 ).then_inc(sh_in[p], 16)
                if not first:
                    sp.wait_ge(masked, g - 1)
                    sp.wait_ge(pick_ready, g - 1)
                sp.dma_start(dst[p][:], dram["dst_scaled"][bass.ds(g * GE, GE + 1)].partition_broadcast(P)
                             ).then_inc(dst_in[p], 16)
                if not first:
                    sp.wait_ge(q_ps, g - 1)
                for t in range(TG):
                    sp.dma_start(qwin[p][:, t, :], dram["q_rows"][bass.ds(bases[t], P), :]).then_inc(qwin_in[p], 16)

            for p in two:
                load(p, 0, p, True)
            with sp.Fori(1, G // 2) as n:
                for p in two:
                    load(2 * n + p, n, p, False)

        @block.tensor
        def _(pe):
            def prepare(g, n, p):
                pe.wait_ge(rows_in[p], 64 * (n + 1))
                if not is_first(g, 0):
                    pe.wait_ge(xt_sb, g)
                for t in range(TG):
                    mm = nc.tensor.transpose(b_xt[:, t * P:(t + 1) * P], rows[p][:, t, :], sb["ident"][:])
                mm.then_inc(xt_ps, 1)
                pe.wait_ge(feat_in[p], 16 * (n + 1))
                if is_first(g, 1) or is_first(g, 2):
                    pe.wait_ge(hid_sb, g)
                nc.tensor.matmul(b_hid_vt[:], sb["L2_w1"][:], feat[p][:], start=True, stop=True).then_inc(hid_ps, 1)

            def pick_q(g, n, p):
                pe.wait_ge(qwin_in[p], 64 * (n + 1))
                pe.wait_ge(pick_ready, g + 1)
                for t in range(TG):
                    mm = nc.tensor.matmul(b_q[:, t * P:(t + 1) * P], qwin[p][:, t, :], pick[:, t, :],
                                          start=True, stop=True)
                mm.then_inc(q_ps, 1)

            def split_product(bank, name, g, p, waits):
                hi, lo = sb[name + "_hi"], sb[name + "_lo"]
                for c in range(KC - 1):
                    if waits:
                        pe.wait_ge(low_ready, KC * g + c + 1)
                    nc.tensor.matmul(bank[:], hi[:, c, :], z_hi[p][:, c, :], start=(c == 0), stop=False)
                    nc.tensor.matmul(bank[:], lo[:, c, :], z_hi[p][:, c, :], start=False, stop=False)
                    nc.tensor.matmul(bank[:], hi[:, c, :], z_lo[p][:, c, :], start=False, stop=False)
                if waits:
                    pe.wait_ge(low_ready, KC * (g + 1))
                nc.tensor.matmul(bank[:], hi[:, KC - 1, :], z_hi[p][:, KC - 1, :], start=False, stop=False)
                return nc.tensor.matmul(bank[:], lo[0:D, KC - 1, :], z_hi[p][0:D, KC - 1, :], start=False, stop=True)

            def body(g, n, p, next, front, back):
                q = 1 - p
                if next:
                    prepare(*after(g, n, p))
                if front:
                    split_product(b_k, "L2_Cqk", g, p, True).then_inc(k_ps, 1)
                    pe.wait_ge(hid_sb, g + 1)
                    if is_first(g, 1):
                        pe.wait_ge(w_sb, 2)
                    elif back:
                        pe.wait_ge(sum_sb, 2 * (g - 1))
                        pe.sem_inc(pe_go, 1)
                    nc.tensor.matmul(b_wk_sum[:], sb["L2_w2"][0:D, :], hid[p][0:D, :], start=True, stop=True)
                    nc.tensor.matmul(b_wv_den[:], sb["L2_w2"][D:P, :], hid[p][D:P, :], start=True,
                                     stop=True).then_inc(w_ps, 1)
                    if back:
                        pe.wait_ge(vw_ready, g)
                    split_product(b_v, "L2_Cv", g, p, False).then_inc(v_ps, 1)
                if back:
                    pe.wait_ge(vx_ready, g)
                    if front:
                        pe.wait_ge(w_sb, 2 * (g + 1))
                    else:
                        pe.wait_ge(sum_sb, 2 * (g - 1))
                    if next:
                        pe.wait_ge(hid_sb, g + 2)
                    for t in range(TG):
                        nc.tensor.transpose(b_hid_vt[:, t * P:(t + 1) * P], vx[:, t * P:(t + 1) * P], sb["ident"][:])
                    for t in range(TG):
                        mm = nc.tensor.transpose(b_wv_den[:, t * P:(t + 1) * P], ex[q][:, t * P:(t + 1) * P],
                                                 sb["ident"][:])
                    mm.then_inc(vt_ps, 1)
                if front:
                    pe.wait_ge(u_ready, g + 1)
                    nc.tensor.matmul(b_attn[:], sb["head_sum"][:], u[:], start=True, stop=True).then_inc(attn_ps, 1)
                if next:
                    pick_q(*after(g, n, p))
                if back:
                    pe.wait_ge(vt_sb, 2 * g)
                    pe.wait_ge(onehot_ready, g)
                    for t in range(TG):
                        nc.tensor.matmul(b_wk_sum[:, t * P:(t + 1) * P], vt[:, t, :], onehot[:, t, :],
                                         start=True, stop=True)
                    for t in range(TG):
                        mm = nc.tensor.matmul(b_wv_den[:, t * P:(t + 1) * P], et[:, t, :], onehot[:, t, :],
                                              start=True, stop=True)
                    mm.then_inc(sum_ps, 1)

            def first(g, n, p):
                prepare(g, n, p)
                pick_q(g, n, p)

            run_rounds(pe, first, body)

        @block.vector
        def _(dve):
            dve.memset(run[1][:], LOWEST).then_inc(dve_set, 1)
            dve.memset(mask[0][:, GE:GE + 1], 0.0).then_inc(dve_set, 1)
            dve.memset(mask[1][:, GE:GE + 1], 0.0).then_inc(dve_set, 1)
            dve.memset(zero[:], 0.0).then_inc(dve_set, 1)

            def backward(t, n):
                a = t[:]
                return bass.AP(a.tensor, a.offset + n - 1, [list(a.ap[0]), [-1, GE]])

            def make_pick(g, n, p):
                dve.wait_ge(dst_in[p], 16 * (n + 1))
                if not is_first(g, 0):
                    dve.wait_ge(q_ps, g)
                dve.tensor_tensor(pick[:], dst[p][:, 1:GE + 1].rearrange("p (t e) -> p t e", t=TG),
                                  sb["node_of_part"][:, bass.ds(TG * g, TG)].unsqueeze(2).to_broadcast([P, TG, P]),
                                  ALU.is_equal).then_inc(pick_ready, 1)

            def make(g, n, p, c):
                if c == 0:
                    dve.wait_ge(sh_in[p], 32 * (n + 1))
                    dve.wait_ge(xt_sb, g + 1)
                if c >= 2:
                    dve.wait_ge(low_ready, KC * g + c - 1)
                elif not is_first(g, 0):
                    dve.wait_ge(low_ready, KC * g)
                dve.tensor_tensor(z[:, c % 2, :], xt[p][:], sh[p][:, c, :], ALU.mult).then_inc(z_ready, 1)

            def low(g, n, p, c):
                dve.wait_ge(high_sb, KC * g + c + 1)
                if c < KC - 1:
                    dve.tensor_tensor(z_lo[p][:, c, :], z[:, c % 2, :], z_hi[p][:, c, :].bitcast(F32),
                                      ALU.subtract).then_inc(low_ready, 1)
                else:
                    dve.tensor_tensor(z_hi[p][D:P, c, :], z[D:P, c % 2, :], z_hi[p][D:P, c, :].bitcast(F32),
                                      ALU.subtract).then_inc(low_ready, 1)

            def split_begin(*group):
                make(*group, 0)
                make(*group, 1)
                low(*group, 0)
                make(*group, 2)
                low(*group, 1)
                make(*group, 3)
                low(*group, 2)

            def split_end(*group):
                make(*group, 4)
                low(*group, 3)
                low(*group, 4)

            def maxima(g, n, p):
                q = 1 - p
                dve.wait_ge(attn_ps, g + 1)
                dve.wait_ge(masked, g + 1)
                dve.tensor_tensor_scan(run[p][:], mask[p][:, 0:GE], b_attn[:], run[q][:, GE - 1:GE],
                                       ALU.add, ALU.max).then_inc(ran, 1)
                dve.wait_ge(ran, g + 1)
                dve.tensor_tensor_scan(backward(top, GE), backward(mask[p], GE + 1), backward(run[p], GE), LOWEST,
                                       ALU.add, ALU.max).then_inc(topped, 1)
                dve.wait_ge(topped, g + 1)
                if not (is_first(g, 0) or is_first(g, 1)):
                    dve.wait_ge(added, STEPS * (g - 1))
                dve.tensor_tensor(ex[p][:, 0:GE], b_attn[:], top[:], ALU.subtract).then_inc(shifted, 1)
                dve.scalar_tensor_tensor(out=ex[p][:, GE:GE + 1], in0=run[q][:, GE - 1:GE], scalar=top[:, 0:1],
                                         in1=zero[:], op0=ALU.subtract, op1=ALU.min).then_inc(shifted, 1)

            def body(g, n, p, next, front, back):
                if next:
                    make_pick(*after(g, n, p))
                if back:
                    if not is_first(g, 1):
                        dve.wait_ge(sum_ps, g - 1)
                    dve.tensor_tensor(onehot[:], sb["iota_row"][:].unsqueeze(1).to_broadcast([P, TG, P]),
                                      sb["dst_local"][:, bass.ds(TG * g - TG, TG)].unsqueeze(2).to_broadcast([P, TG, P]),
                                      ALU.is_equal).then_inc(onehot_ready, 1)
                if next:
                    split_begin(*after(g, n, p))
                if front:
                    dve.wait_ge(k_ps, g + 1)
                    dve.wait_ge(w_sb, 2 * g + 1)
                    dve.tensor_tensor(u[:], b_k[:], wk[:], ALU.mult).then_inc(kw_ready, 1)
                    dve.wait_ge(q_ps, g + 1)
                    dve.wait_ge(kw_ready, g + 1)
                    dve.tensor_tensor(u[:], b_q[:], u[:], ALU.mult).then_inc(u_ready, 1)
                if next:
                    split_end(*after(g, n, p))
                if front:
                    dve.wait_ge(v_ps, g + 1)
                    dve.wait_ge(w_sb, 2 * g + 2)
                    dve.tensor_tensor(vw[p][:], b_v[:], wv[:], ALU.mult).then_inc(vw_ready, 1)
                if front:
                    maxima(g, n, p)

            def first(g, n, p):
                make_pick(g, n, p)
                split_begin(g, n, p)
                split_end(g, n, p)

            dve.wait_ge(dve_set, 4)
            run_rounds(dve, first, body)


def attention_out(nc, sb, h):
    with ExitStack() as ctx:
        ph = Phase(nc, ctx, "attn_out")
        step, scaled, summed = (ph.sem(n) for n in ("step", "scaled", "summed"))
        ps = ph.ps("ps", [P, NC, 512])
        block = ctx.enter_context(nc.Block())

        @block.vector
        def _(dve):
            dve.tensor_scalar(sb["den"][:], sb["den"][:], 1e-16, None, ALU.add).then_inc(step, 1)
            dve.wait_ge(step, 1)
            dve.reciprocal(sb["den"][:], sb["den"][:]).then_inc(step, 1)
            dve.wait_ge(step, 2)
            dve.tensor_tensor(sb["acc"][:], sb["acc"][:], sb["den"][:], ALU.mult).then_inc(scaled, 1)
            dve.wait_ge(summed, 1)
            dve.tensor_copy(nodes(h), chunks(ps))

        @block.tensor
        def _(pe):
            pe.wait_ge(scaled, 1)
            node_products(nc, ps, [(sb["L2_W_self"][:], sb["x_t"]), (sb["L2_W_out"][:], sb["acc"])]).then_inc(summed, 1)


def message_loop(nc, dram, sb):
    with ExitStack() as ctx:
        ph = Phase(nc, ctx, "msg")
        two = range(2)
        idx_ready = [ph.sem(f"idx_ready{p}") for p in two]
        rows_in = [ph.sem(f"rows_in{p}") for p in two]
        dst_in = [ph.sem(f"dst_in{p}") for p in two]
        bwin_in = [ph.sem(f"bwin_in{p}") for p in two]
        pick_ready, onehot_ready, picked, pre_ready, msg_ready, sums_ready, added, pool_go, acc_clear = (
            ph.sem(n) for n in ("pick_ready", "onehot_ready", "picked", "pre_ready", "msg_ready", "sums_ready", "added",
                                "pool_go", "acc_clear"))
        idx = [ph.sb(f"idx{p}", [P, TG], I32) for p in two]
        rows = [ph.sb(f"rows{p}", [P, TG, D]) for p in two]
        dst = [ph.sb(f"dst{p}", [P, TG, P]) for p in two]
        bwin = [ph.sb(f"bwin{p}", [P, TG, D]) for p in two]
        pick = [ph.sb(f"pick{p}", [P, TG, P]) for p in two]
        onehot = [ph.sb(f"onehot{p}", [P, TG, P]) for p in two]
        pre = [ph.sb(f"pre{p}", [P, TG, D]) for p in two]
        msg = [ph.sb(f"msg{p}", [P, TG, D]) for p in two]
        at_dst = [ph.ps(f"at_dst{p}", [P, 512]) for p in two]
        sums = [ph.ps(f"sums{p}", [P, TG, P]) for p in two]
        block = ctx.enter_context(nc.Block())

        def is_first(g, k):
            return isinstance(g, int) and g == k

        def run_steps(eng, step):
            for g in range(4):
                step(g, g // 2, g % 2)
            with eng.Fori(2, G // 2 - 1) as n:
                for p in two:
                    step(2 * n + p, n, p)
            step(G - 2, G // 2 - 1, 0)
            step(G - 1, G // 2 - 1, 1, last=True)

        @block.scalar
        def _(act):
            def stage(g, p):
                nc.scalar.copy(idx[p][:], sb["src_i"][:, bass.ds(TG * g, TG)]).then_inc(idx_ready[p], 1)

            def relu(g, p, first):
                act.wait_ge(pre_ready, g + 1)
                if not first:
                    act.wait_ge(sums_ready, g - 1)
                nc.scalar.activation(msg[p][:], pre[p][:], ACT.Relu).then_inc(msg_ready, 1)

            for p in two:
                stage(p, p)
            for p in two:
                relu(p, p, True)
                stage(p + 2, p)
            with act.Fori(1, G // 2 - 1) as n:
                for p in two:
                    relu(2 * n + p, p, False)
                    stage(2 * n + p + 2, p)
            for p in two:
                relu(G - 2 + p, p, False)

        @block.gpsimd
        def _(pool):
            def gather(g, n, p, first):
                pool.wait_ge(idx_ready[p], n + 1)
                if not first:
                    pool.wait_ge(pre_ready, g - 1)
                pool.sem_inc(pool_go, 1)
                for t in range(TG):
                    pool.indirect_dma_start(
                        rows[p][:, t, :], None, dram["a_rows"],
                        bass.IndirectOffsetOnAxis(ap=idx[p][:, t:t + 1], axis=0)).then_inc(rows_in[p], 16)

            for p in two:
                gather(p, 0, p, True)
            with pool.Fori(1, G // 2) as n:
                for p in two:
                    gather(2 * n + p, n, p, False)

        @block.sync
        def _(sp):
            def load(g, p, first):
                if not first:
                    sp.wait_ge(pick_ready, g - 1)
                sp.dma_start(dst[p][:].rearrange("p t e -> p (t e)"),
                             dram["dst_scaled"][bass.ds(g * GE + 1, GE)].partition_broadcast(P)).then_inc(dst_in[p], 16)
                if not first:
                    sp.wait_ge(picked, g - 1)
                bases = window_bases(nc, mybir.EngineType.SP, sb, TG * g)
                for t in range(TG):
                    sp.dma_start(bwin[p][:, t, :], dram["b_rows"][bass.ds(bases[t], P), :]).then_inc(bwin_in[p], 16)

            for p in two:
                load(p, p, True)
            with sp.Fori(1, G // 2) as n:
                for p in two:
                    load(2 * n + p, p, False)

        @block.tensor
        def _(pe):
            def choose(g, n, p):
                pe.wait_ge(bwin_in[p], 64 * (n + 1))
                pe.wait_ge(pick_ready, g + 1)
                if not (is_first(g, 0) or is_first(g, 1)):
                    pe.wait_ge(pre_ready, g - 1)
                for t in range(TG):
                    mm = nc.tensor.matmul(at_dst[p][:, t * D:(t + 1) * D], pick[p][:, t, :], bwin[p][:, t, :],
                                          start=True, stop=True)
                mm.then_inc(picked, 1)

            def total(g, p):
                pe.wait_ge(msg_ready, g + 1)
                pe.wait_ge(onehot_ready, g + 1)
                if not (is_first(g, 0) or is_first(g, 1)):
                    pe.wait_ge(added, TG * (g - 1))
                for t in range(TG):
                    mm = nc.tensor.matmul(sums[p][0:D, t, :], msg[p][:, t, :], onehot[p][:, t, :], start=True, stop=True)
                mm.then_inc(sums_ready, 1)

            def step(g, n, p, last=False):
                if not last:
                    choose(g + 1, n + p, 1 - p)
                total(g, p)

            choose(0, 0, 0)
            run_steps(pe, step)

        @block.vector
        def _(dve):
            def make_pick(g, n, p):
                dve.wait_ge(dst_in[p], 16 * (n + 1))
                dve.tensor_tensor(pick[p][:], dst[p][:],
                                  sb["node_of_part"][:, bass.ds(TG * g, TG)].unsqueeze(2).to_broadcast([P, TG, P]),
                                  ALU.is_equal).then_inc(pick_ready, 1)

            def make_onehot(g, p):
                dve.tensor_tensor(onehot[p][:], sb["iota_row"][:].unsqueeze(1).to_broadcast([P, TG, P]),
                                  sb["dst_local"][:, bass.ds(TG * g, TG)].unsqueeze(2).to_broadcast([P, TG, P]),
                                  ALU.is_equal).then_inc(onehot_ready, 1)

            def join(g, n, p):
                dve.wait_ge(rows_in[p], 64 * (n + 1))
                dve.wait_ge(picked, g + 1)
                if not (is_first(g, 0) or is_first(g, 1)):
                    dve.wait_ge(msg_ready, g - 1)
                dve.tensor_tensor(pre[p][:], rows[p][:], at_dst[p][:, 0:TG * D].rearrange("p (t d) -> p t d", t=TG),
                                  ALU.add).then_inc(pre_ready, 1)

            def add(g, p):
                bases = window_bases(nc, mybir.EngineType.DVE, sb, TG * g)
                for t in range(TG):
                    base = bases[t]
                    if t == 0:
                        dve.wait_ge(sums_ready, g + 1)
                    if not (is_first(g, 0) and t == 0):
                        dve.wait_ge(added, TG * g + t)
                    cols = bass.ds(base, P)
                    dve.tensor_tensor(sb["acc"][0:D, cols], sb["acc"][0:D, cols], sums[p][0:D, t, :],
                                      ALU.add).then_inc(added, 1)

            def step(g, n, p, last=False):
                join(g, n, p)
                if not last:
                    make_pick(g + 1, n + p, 1 - p)
                if not is_first(g, 0):
                    add(g - 1, 1 - p)
                if not last:
                    make_onehot(g + 1, 1 - p)

            dve.memset(sb["acc"][:], 0.0).then_inc(acc_clear, 1)
            dve.wait_ge(acc_clear, 1)
            make_pick(0, 0, 0)
            make_onehot(0, 0)
            run_steps(dve, step)
            add(G - 1, 1)


def program(nc, dram, out):
    Phase.sems.clear()
    with ExitStack() as ctx:
        sb = {}

        def table(name, shape, dt=F32):
            sb[name] = ctx.enter_context(nc.sbuf_tensor(name, shape, dt))

        table("src_i", [P, T + 2 * TG], I32)
        table("dst_i", [P, T], I32)
        for name in ("dst_local", "node_of_part"):
            table(name, [P, T])
        table("iota_row", [P, P])
        table("iota_col", [P, 1])
        table("ident", [P, P])
        table("mean_mat", [D, D])
        table("cnt_spread", [D + 1, D])
        table("head_sum", [HD, HD])
        for name in ("L0_W_l", "L0_W_r", "L1_W", "L2_W_self", "L3_W_upd_x", "L3_W_upd_a"):
            table(name, [D, D])
        table("L2_W_out", [HD, D])
        table("L2_Wq", [D, HD])
        for name in ("L0_b_l", "L0_gamma", "L0_beta", "L1_b", "L2_gamma", "L2_beta", "L3_b_upd"):
            table(name, [D, 1])
        table("L2_w1", [D, 2 * D])
        table("L2_b1", [2 * D, 1])
        table("L2_w2", [2 * D, HD])
        table("L2_k_b2", [HD, 1])
        table("L2_v_b2", [HD, 1])
        for name in ("L2_Cqk_hi", "L2_Cqk_lo", "L2_Cv_hi", "L2_Cv_lo"):
            table(name, [P, KC, HD], F32R)
        table("L3_W_msg", [D, 2 * D])
        table("L3_b_msg", [P, D])
        table("x_t", [D, NP])
        table("acc", [P, NP])
        table("den", [HD, NP])
        table("rec_in", [D, NP])
        table("out_deg", [NB, P])
        sb["deg_out_sem"] = ctx.enter_context(nc.semaphore("deg_out"))

        def scratch(name, shape):
            dram[name] = nc.dram_tensor(name, shape, F32, kind="Internal").ap()

        scratch("dst_scaled", (EP + 1,))
        scratch("out_deg_line", (NP,))
        scratch("x1_rows", (NP, D))
        scratch("x_twice", (NP, 2 * D))
        scratch("q_rows", (NP, HD))
        scratch("a_rows", (NP, D))
        scratch("b_rows", (NP, D))
        sb["dram_out_deg"] = dram["out_deg_line"]

        with ExitStack() as early:
            for name in ("src_hi", "src_lo"):
                sb[name] = early.enter_context(nc.sbuf_tensor(name, [P, T], F32))
            setup(nc, dram, sb)
            for name in ("h", "rsqrt_in", "rsqrt_out"):
                sb[name] = early.enter_context(nc.sbuf_tensor(name, [D, NP], F32))
            sum_loop(nc, "sum0", dram["x"], sb, sb["acc"], True)
            count_reciprocals(nc, sb)
            node_linear(nc, "lin0", sb, sb["acc"], sb["rec_in"],
                        [(sb["L0_W_l"][:], None), (sb["L0_W_r"][:], sb["x_t"])], sb["L0_b_l"], sb["h"])
            batch_norm(nc, "bn0", sb, sb["h"], sb["L0_gamma"], sb["L0_beta"], True)
            add_layer_norm(nc, "ln0", sb, sb["x_t"], sb["h"])
            write_rows(nc, "rows1", sb, sb["x_t"], [(0, None)], D, [(dram["x1_rows"], 0, D)], factor=sb["rsqrt_out"])
            sum_loop(nc, "sum1", dram["x1_rows"], sb, sb["acc"], False)
            node_linear(nc, "lin1", sb, sb["acc"], sb["rsqrt_in"], [(sb["L1_W"][:], None)], sb["L1_b"], sb["h"])
            add_layer_norm(nc, "ln1", sb, sb["x_t"], sb["h"])
        write_rows(nc, "rows2", sb, sb["x_t"], [(0, None), (D, None), (2 * D, sb["L2_Wq"][:])], 4 * D,
                   [(dram["x_twice"], 0, 2 * D), (dram["q_rows"], 2 * D, HD)])
        recycle(nc)
        attention_loop(nc, dram, sb)
        sb["h"] = ctx.enter_context(nc.sbuf_tensor("h_late", [D, NP], F32))
        attention_out(nc, sb, sb["h"])
        batch_norm(nc, "bn2", sb, sb["h"], sb["L2_gamma"], sb["L2_beta"], False)
        add_layer_norm(nc, "ln2", sb, sb["x_t"], sb["h"])
        write_rows(nc, "rows3", sb, sb["x_t"], [(0, sb["L3_W_msg"][:])], 2 * D,
                   [(dram["a_rows"], 0, D), (dram["b_rows"], D, D)], bias=sb["L3_b_msg"])
        message_loop(nc, dram, sb)
        node_linear(nc, "lin3", sb, sb["acc"], sb["rec_in"],
                    [(sb["L3_W_upd_x"][:], sb["x_t"]), (sb["L3_W_upd_a"][:], None)], sb["L3_b_upd"], sb["h"], relu=True)
        add_layer_norm(nc, "ln3", sb, sb["x_t"], sb["h"])
        write_rows(nc, "rows4", sb, sb["x_t"], [(0, None)], D, [(out, 0, D)])


def kernel(**inputs):
    import numpy as np
    import concourse.bacc as bacc
    from concourse.bass_utils import run_bass_kernel_spmd

    nc = bacc.Bacc("TRN2", target_bir_lowering=False, num_devices=1)
    a = {k: np.asarray(v) for k, v in inputs.items()}
    pad = EP - E
    src = np.concatenate([a["src"], np.full(pad, PADN, a["src"].dtype)])
    dst = np.concatenate([a["dst"], np.full(pad, PADN, a["dst"].dtype)])
    arrays = {
        "x": np.concatenate([a["x"], np.zeros((NP - N, D), a["x"].dtype)]),
        "x_t": np.concatenate([a["x"].T, np.zeros((D, NP - N), a["x"].dtype)], axis=1),
        "src_tab": src.reshape(T, P).T,
        "dst_tab": dst.reshape(T, P).T,
        "dst_line": dst,
        "edge_feat": np.concatenate([a["edge_attr_64"].T, np.zeros((D, pad), a["edge_attr_64"].dtype)], axis=1),
        "edge_sh": np.concatenate([a["edge_attr_9"].T[[*range(S_SH), S_SH - 1]],
                                   np.zeros((S_SH + 1, pad), a["edge_attr_9"].dtype)], axis=1),
        "L2_Cqk": a["L2_gnn_Cqk"].transpose(1, 0, 2).reshape(S_SH * D, HD),
        "L2_Cv": a["L2_gnn_Cv"].transpose(1, 0, 2).reshape(S_SH * D, HD),
    }
    for name, value in a.items():
        short = name.replace("_gnn_", "_")
        if name[0] == "L" and short not in arrays:
            arrays[short] = value
    arrays = {k: np.ascontiguousarray(v) for k, v in arrays.items()}
    dram = {k: nc.dram_tensor("in_" + k, v.shape, mybir.dt.from_np(v.dtype), kind="ExternalInput").ap()
            for k, v in arrays.items()}
    out = nc.dram_tensor("out", (N, D), F32, kind="ExternalOutput").ap()
    program(nc, dram, out)
    r = run_bass_kernel_spmd(nc, [{"in_" + k: v for k, v in arrays.items()}], core_ids=[0])
    return r.results[0]["out"]
```

```python
from contextlib import ExitStack

import concourse.bass as bass
from concourse import mybir

F32 = mybir.dt.float32
F32R = mybir.dt.float32r
BF16 = mybir.dt.bfloat16
I32 = mybir.dt.int32
ALU = mybir.AluOpType
ACT = mybir.ActivationFunctionType
AX_X = mybir.AxisListType.X

P = 128
D = 64
N = 3125
E = 103125
TG = 4
GE = TG * P
G = 2 * (-(-E // (2 * GE)))
T = G * TG
EP = T * P
NB = 26
NP = NB * P
PADN = 3200
NC = 8
CW = NP // NC
S_SH = 9
KC = 5
H = 8
DH = 16
HD = H * DH
EPS = 1e-5
DST_SCALE = 2.0 ** 113
LOWEST = -1e38
assert PADN + P <= NP and PADN >= N and NC * CW == NP and CW <= 512


class Phase:

    sems = []

    def __init__(self, nc, ctx, name):
        self.nc, self.ctx, self.name = nc, ctx, name

    def sem(self, name):
        handle = self.nc.alloc_semaphore(f"{self.name}_{name}")
        self.sems.append(handle)
        return handle

    def sb(self, name, shape, dt=F32):
        return self.ctx.enter_context(self.nc.sbuf_tensor(f"{self.name}_{name}", shape, dt))

    def ps(self, name, shape):
        return self.ctx.enter_context(self.nc.psum_tensor(f"{self.name}_{name}", shape, F32))


def recycle(nc):
    nc.clear_and_free_semaphores(Phase.sems)
    Phase.sems.clear()
    nc.all_engine_barrier()


def setup(nc, dram, sb):
    with ExitStack() as ctx:
        ph = Phase(nc, ctx, "setup")
        loaded = ph.sem("loaded")
        iota_done = ph.sem("iota_done")
        ident_zero = ph.sem("ident_zero")
        ident_done = ph.sem("ident_done")
        dst_float = ph.sem("dst_float")
        base_bcast = ph.sem("base_bcast")
        tables_done = ph.sem("tables_done")
        step = ph.sem("step")
        scaled_done = ph.sem("scaled_done")
        scaled_out = ph.sem("scaled_out")
        consts = ph.sem("consts")
        split = ph.sem("split")
        line_cur = ph.sb("line_cur", [P, T], I32)
        line_scaled = ph.sb("line_scaled", [P, T])
        before = ph.sb("before", [1, 1])
        dst_f = ph.sb("dst_f", [P, T])
        first_row = ph.sb("first_row", [P, P])
        tmp_i = ph.sb("tmp_i", [P, T], I32)
        base_ps = ph.ps("base_ps", [P, 2, 512])
        w1 = ph.sb("w1", [P, 2 * D])
        paths = {name: ph.sb(name, [P, KC, HD]) for name in ("L2_Cqk", "L2_Cv")}
        block = ctx.enter_context(nc.Block())

        loads = [
            (sb["src_i"][:, 0:T], dram["src_tab"]), (sb["dst_i"][:], dram["dst_tab"]),
            (line_cur[:], dram["dst_line"].rearrange("(p t) -> p t", p=P)),
            (sb["x_t"][:], dram["x_t"]),
        ]
        for name in ("L0_W_l", "L0_W_r", "L1_W", "L2_Wq", "L2_W_out", "L2_W_self"):
            loads.append((sb[name][:], dram[name]))
        for name in ("L0_b_l", "L0_gamma", "L0_beta", "L1_b", "L2_gamma", "L2_beta", "L3_b_upd"):
            loads.append((sb[name][:], dram[name].rearrange("(p a) -> p a", a=1)))
        for k in range(2):
            half = slice(k * D, (k + 1) * D)
            loads.append((w1[half, 0:D], dram["L2_k_w1"]))
            loads.append((w1[half, D:2 * D], dram["L2_v_w1"]))
        loads.append((sb["L2_b1"][0:D, :], dram["L2_k_b1"].rearrange("(p a) -> p a", a=1)))
        loads.append((sb["L2_b1"][D:2 * D, :], dram["L2_v_b1"].rearrange("(p a) -> p a", a=1)))
        loads.append((sb["L2_w2"][0:D, :], dram["L2_k_w2"]))
        loads.append((sb["L2_w2"][D:2 * D, :], dram["L2_v_w2"]))
        loads.append((sb["L2_k_b2"][:], dram["L2_k_b2"].rearrange("(p a) -> p a", a=1)))
        loads.append((sb["L2_v_b2"][:], dram["L2_v_b2"].rearrange("(p a) -> p a", a=1)))
        for name in ("L2_Cqk", "L2_Cv"):
            loads.append((paths[name][:, 0:4, :], dram[name][0:4 * P, :].rearrange("(c p) o -> p c o", p=P)))
            loads.append((paths[name][0:D, 4, :], dram[name][4 * P:, :]))
            loads.append((paths[name][D:P, 4, :], dram[name][4 * P:, :]))
        loads.append((sb["L3_W_msg"][:, 0:D], dram["L3_W_msg"][0:D, :]))
        loads.append((sb["L3_W_msg"][:, D:2 * D], dram["L3_W_msg"][D:2 * D, :]))
        loads.append((sb["L3_b_msg"][:], dram["L3_b_msg"].partition_broadcast(P)))
        loads.append((sb["L3_W_upd_x"][:], dram["L3_W_upd"][0:D, :]))
        loads.append((sb["L3_W_upd_a"][:], dram["L3_W_upd"][D:2 * D, :]))

        @block.sync
        def _(sp):
            for to, frm in loads[0::2]:
                sp.dma_start(to, frm).then_inc(loaded, 16)
            sp.wait_ge(scaled_done, 2)
            sp.dma_start(dram["dst_scaled"][1:1 + EP].rearrange("(p t) -> p t", p=P), line_scaled[:]).then_inc(scaled_out, 16)
            sp.dma_start(dram["dst_scaled"][0:1].rearrange("(p t) -> p t", p=1), before[:]).then_inc(scaled_out, 16)
            sp.wait_ge(scaled_out, 32)

        @block.scalar
        def _(act):
            for to, frm in loads[1::2]:
                act.dma_start(to, frm).then_inc(loaded, 16)

        @block.gpsimd
        def _(pool):
            pool.iota(sb["iota_row"][:], [[1, P]], base=0, channel_multiplier=0,
                      allow_small_or_imprecise_dtypes=True).then_inc(iota_done, 1)
            pool.iota(sb["iota_col"][:], [[0, 1]], base=0, channel_multiplier=1,
                      allow_small_or_imprecise_dtypes=True).then_inc(iota_done, 1)
            pool.memset(sb["ident"][:], 0.0).then_inc(ident_zero, 1)
            pool.memset(sb["head_sum"][:], 1.0).then_inc(ident_zero, 1)
            for k, value in enumerate((0.0, 1.0 / D, 0.0)):
                pool.memset(sb["mean_mat"][:, k * D:(k + 1) * D], value).then_inc(consts, 1)
            pool.memset(sb["eps_col"][:], EPS).then_inc(consts, 1)
            pool.memset(sb["cnt_spread"][:], 0.0).then_inc(ident_zero, 1)
            pool.wait_ge(ident_zero, 3)
            pool.affine_select(out=sb["ident"][:], in_=sb["ident"][:], compare_op=ALU.not_equal, fill=1.0,
                               base=0, pattern=[[-1, P]], channel_multiplier=1).then_inc(ident_done, 1)
            pool.affine_select(out=sb["cnt_spread"][:], in_=sb["cnt_spread"][:], compare_op=ALU.not_equal,
                               fill=1.0, base=-D, pattern=[[0, D]], channel_multiplier=1).then_inc(ident_done, 1)
            by_head = sb["head_sum"][:].rearrange("p (h d) -> p h d", h=H)
            pool.affine_select(out=by_head, in_=by_head, compare_op=ALU.is_ge, fill=0.0,
                               base=0, pattern=[[-DH, H], [0, DH]], channel_multiplier=1).then_inc(ident_done, 1)
            pool.wait_ge(ident_done, 3)
            pool.affine_select(out=by_head, in_=by_head, compare_op=ALU.is_ge, fill=0.0,
                               base=DH - 1, pattern=[[DH, H], [0, DH]], channel_multiplier=-1).then_inc(ident_done, 1)

        @block.vector
        def _(dve):
            dve.memset(first_row[:], 0.0).then_inc(step, 1)
            dve.wait_ge(step, 1)
            dve.memset(first_row[0:1, :], 1.0).then_inc(step, 1)
            dve.wait_ge(loaded, 16 * len(loads))
            dve.tensor_copy(dst_f[:], sb["dst_i"][:]).then_inc(dst_float, 1)
            for k, name in enumerate(("L2_Cqk", "L2_Cv")):
                dve.tensor_copy(sb[name + "_hi"][:], paths[name][:]).then_inc(split, 1)
                dve.wait_ge(split, k + 1)
                dve.tensor_tensor(sb[name + "_lo"][:], paths[name][:], sb[name + "_hi"][:].bitcast(F32), ALU.subtract)
            dve.tensor_copy(sb["L2_w1_hi"][:], w1[:]).then_inc(split, 1)
            dve.wait_ge(split, 3)
            dve.tensor_tensor(sb["L2_w1_lo"][:], w1[0:D, :], sb["L2_w1_hi"][0:D, :].bitcast(F32), ALU.subtract)
            dve.tensor_scalar(line_scaled[:], line_cur[:], DST_SCALE, None, ALU.mult).then_inc(scaled_done, 1)
            dve.memset(before[:], -DST_SCALE).then_inc(scaled_done, 1)
            dve.tensor_scalar(tmp_i[:], sb["src_i"][:, 0:T], 7, None, ALU.logical_shift_right).then_inc(step, 1)
            dve.wait_ge(step, 3)
            dve.tensor_copy(sb["src_hi"][:], tmp_i[:]).then_inc(step, 1)
            dve.wait_ge(step, 4)
            dve.tensor_scalar(tmp_i[:], sb["src_i"][:, 0:T], 127, None, ALU.bitwise_and).then_inc(step, 1)
            dve.wait_ge(step, 5)
            dve.tensor_copy(sb["src_lo"][:], tmp_i[:]).then_inc(step, 1)
            dve.wait_ge(base_bcast, 1)
            dve.wait_ge(dst_float, 1)
            dve.wait_ge(iota_done, 2)
            half = T // 2
            dve.memset(sb["src_i"][:, T:], 0).then_inc(tables_done, 1)
            for k in range(2):
                cols = slice(k * half, (k + 1) * half)
                dve.tensor_tensor(sb["dst_local"][:, cols], dst_f[:, cols], base_ps[:, k, 0:half],
                                  ALU.subtract).then_inc(tables_done, 1)
                dve.tensor_scalar(sb["node_of_part"][:, cols], base_ps[:, k, 0:half], sb["iota_col"][:, 0:1],
                                  DST_SCALE, ALU.add, ALU.mult).then_inc(tables_done, 1)

        @block.tensor
        def _(pe):
            pe.wait_ge(step, 2)
            pe.wait_ge(dst_float, 1)
            half = T // 2
            for k in range(2):
                mm = nc.tensor.matmul(base_ps[:, k, 0:half], first_row[:], dst_f[:, k * half:(k + 1) * half],
                                      start=True, stop=True)
            mm.then_inc(base_bcast, 1)


def window_bases(nc, engine, sb, first_tile):
    return nc.values_load_multi_w_load_instructions(
        sb["dst_i"][0:1, bass.ds(first_tile, TG)], engines=[engine], min_val=0, max_val=PADN,
        skip_runtime_bounds_check_because="dst holds node numbers below N, and PADN")[1]


def sum_loop(nc, name, dram_table, sb, acc, counts):
    M = D + 1 if counts else D
    with ExitStack() as ctx:
        ph = Phase(nc, ctx, name)
        idx_ready = [ph.sem(f"idx_ready{p}") for p in range(2)]
        rows_in = [ph.sem(f"rows_in{p}") for p in range(2)]
        onehot_ready = ph.sem("onehot_ready")
        hist_ready = ph.sem("hist_ready")
        sums_ready = ph.sem("sums_ready")
        added = ph.sem("added")
        ones_set = ph.sem("ones_set")
        acc_clear = ph.sem("acc_clear")
        pool_go = ph.sem("pool_go")
        hist_done = ph.sem("hist_done")
        hist_copied = ph.sem("hist_copied")
        idx = [ph.sb(f"idx{p}", [P, TG], I32) for p in range(2)]
        rows = [ph.sb(f"rows{p}", [P, TG, M]) for p in range(2)]
        onehot = [ph.sb(f"onehot{p}", [P, TG, P]) for p in range(2)]
        sums = [ph.ps(f"sums{p}", [P, TG, P]) for p in range(2)]
        if counts:
            hi = [ph.sb(f"hi{p}", [P, TG, NB], BF16) for p in range(2)]
            lo = [ph.sb(f"lo{p}", [P, TG, P], BF16) for p in range(2)]
            zeros = ph.sb("zeros", [P, P], BF16)
            hist = ph.ps("hist", [P, P])
        block = ctx.enter_context(nc.Block())

        @block.scalar
        def _(act):
            def stage(g, n, p, first):
                if not first:
                    act.wait_ge(rows_in[p], 64 * n)
                nc.scalar.copy(idx[p][:], sb["src_i"][:, bass.ds(TG * g, TG)]).then_inc(idx_ready[p], 1)

            for p in range(2):
                stage(p, 0, p, True)
            with act.Fori(1, G // 2) as n:
                for p in range(2):
                    stage(2 * n + p, n, p, False)

        @block.gpsimd
        def _(pool):
            pool.wait_ge(ones_set, 2)

            def gather(g, n, p, first):
                pool.wait_ge(idx_ready[p], n + 1)
                if not first:
                    pool.wait_ge(sums_ready, g - 1)
                pool.sem_inc(pool_go, 1)
                for t in range(TG):
                    pool.indirect_dma_start(
                        rows[p][:, t, 0:D], None, dram_table,
                        bass.IndirectOffsetOnAxis(ap=idx[p][:, t:t + 1], axis=0)).then_inc(rows_in[p], 16)

            for p in range(2):
                gather(p, 0, p, True)
            with pool.Fori(1, G // 2) as n:
                for p in range(2):
                    gather(2 * n + p, n, p, False)

        @block.vector
        def _(dve):
            dve.memset(acc[:], 0.0).then_inc(acc_clear, 1)
            dve.wait_ge(acc_clear, 1)
            for p in range(2):
                dve.memset(rows[p][:], 1.0).then_inc(ones_set, 1)
            if counts:
                dve.memset(zeros[:], 0.0).then_inc(ones_set, 1)

            def build(g, p, first):
                if not first:
                    dve.wait_ge(sums_ready, g - 1)
                dve.tensor_tensor(onehot[p][:],
                                  sb["iota_row"][:].unsqueeze(1).to_broadcast([P, TG, P]),
                                  sb["dst_local"][:, bass.ds(TG * g, TG)].unsqueeze(2).to_broadcast([P, TG, P]),
                                  ALU.is_equal).then_inc(onehot_ready, 1)
                if counts:
                    dve.tensor_tensor(hi[p][:],
                                      sb["iota_row"][:, 0:NB].unsqueeze(1).to_broadcast([P, TG, NB]),
                                      sb["src_hi"][:, bass.ds(TG * g, TG)].unsqueeze(2).to_broadcast([P, TG, NB]),
                                      ALU.is_equal).then_inc(hist_ready, 1)
                    dve.tensor_tensor(lo[p][:],
                                      sb["iota_row"][:].unsqueeze(1).to_broadcast([P, TG, P]),
                                      sb["src_lo"][:, bass.ds(TG * g, TG)].unsqueeze(2).to_broadcast([P, TG, P]),
                                      ALU.is_equal).then_inc(hist_ready, 1)

            def add(g, p):
                bases = window_bases(nc, mybir.EngineType.DVE, sb, TG * g)
                for t in range(TG):
                    base = bases[t]
                    if t == 0:
                        dve.wait_ge(sums_ready, g + 1)
                    if not (isinstance(g, int) and g == 0 and t == 0):
                        dve.wait_ge(added, TG * g + t)
                    dve.tensor_tensor(acc[0:M, bass.ds(base, P)], acc[0:M, bass.ds(base, P)], sums[p][0:M, t, :],
                                      ALU.add).then_inc(added, 1)

            for p in range(2):
                build(p, p, True)
            for p in range(2):
                add(p, p)
                build(p + 2, p, False)
            with dve.Fori(1, G // 2 - 1) as n:
                for p in range(2):
                    add(2 * n + p, p)
                    build(2 * n + p + 2, p, False)
            for p in range(2):
                add(G - 2 + p, p)
            if counts:
                dve.wait_ge(hist_done, 1)
                dve.tensor_copy(sb["out_deg"][:], hist[0:NB, :]).then_inc(hist_copied, 1)

        @block.tensor
        def _(pe):
            if counts:
                pe.wait_ge(ones_set, 3)
                nc.tensor.matmul(hist[0:NB, :], zeros[:, 0:NB], zeros[:], start=True, stop=False)

            def product(g, n, p, first):
                pe.wait_ge(rows_in[p], 64 * (n + 1))
                pe.wait_ge(onehot_ready, g + 1)
                if not first:
                    pe.wait_ge(added, TG * (g - 1))
                if counts:
                    pe.wait_ge(hist_ready, 2 * (g + 1))
                    for t in range(TG):
                        nc.tensor.matmul(hist[0:NB, :], hi[p][:, t, :], lo[p][:, t, :], start=False, stop=False)
                for t in range(TG):
                    mm = nc.tensor.matmul(sums[p][0:M, t, :], rows[p][:, t, :], onehot[p][:, t, :],
                                          start=True, stop=True)
                mm.then_inc(sums_ready, 1)

            for p in range(2):
                product(p, 0, p, True)
            with pe.Fori(1, G // 2) as n:
                for p in range(2):
                    product(2 * n + p, n, p, False)
            if counts:
                nc.tensor.matmul(hist[0:NB, :], zeros[:, 0:NB], zeros[:], start=False, stop=True
                                 ).then_inc(hist_done, 1)

        if counts:
            @block.sync
            def _(sp):
                sp.wait_ge(hist_copied, 1)
                sp.dma_start(dram_deg_of(sb), sb["out_deg"][:]).then_inc(sb["deg_out_sem"], 16)
                sp.wait_ge(sb["deg_out_sem"], 16)


def dram_deg_of(sb):
    return sb["dram_out_deg"].rearrange("(a b) -> a b", a=NB)


def chunks(ps, rows=D):
    return ps[0:rows, :, 0:CW]


def nodes(t, rows=D):
    return t[0:rows, :].rearrange("p (c w) -> p c w", c=NC)


def move(nc, name, to, frm):
    with ExitStack() as ctx:
        moved = Phase(nc, ctx, name).sem("moved")
        block = ctx.enter_context(nc.Block())

        @block.sync
        def _(sp):
            sp.dma_start(to, frm).then_inc(moved, 16)
            sp.wait_ge(moved, 16)


def part(t, c):
    return t[0:D, c * CW:(c + 1) * CW]


def node_products(nc, ps, terms, rows=D):
    for c in range(NC):
        for k, (w, x) in enumerate(terms):
            mm = nc.tensor.matmul(ps[0:rows, c, 0:CW], w, x[:, c * CW:(c + 1) * CW],
                                  start=(k == 0), stop=(k == len(terms) - 1))
    return mm


def count_reciprocals(nc, sb):
    with ExitStack() as ctx:
        ph = Phase(nc, ctx, "counts")
        spread, deg_in, clamped, rec_done, done = (ph.sem(n) for n in ("spread", "deg_in", "clamped", "rec_done", "done"))
        deg = ph.sb("deg", [P, NP])
        rec = ph.sb("rec", [P, NP])
        ps = ph.ps("ps", [P, NC, 512])
        block = ctx.enter_context(nc.Block())

        @block.sync
        def _(sp):
            sp.dma_start(deg[D:P, :], sb["dram_out_deg"].partition_broadcast(D)).then_inc(deg_in, 16)

        @block.tensor
        def _(pe):
            node_products(nc, ps, [(sb["cnt_spread"][:], sb["acc"][0:D + 1, :])]).then_inc(spread, 1)

        @block.vector
        def _(dve):
            dve.wait_ge(deg_in, 16)
            dve.tensor_scalar(deg[D:P, :], deg[D:P, :], 1.0, None, ALU.max).then_inc(clamped, 1)
            dve.wait_ge(spread, 1)
            dve.tensor_scalar(nodes(deg), chunks(ps), 1.0, None, ALU.max).then_inc(clamped, 1)
            dve.wait_ge(clamped, 2)
            for c in range(NC):
                cols = slice(c * CW, (c + 1) * CW)
                dve.reciprocal(rec[:, cols], deg[:, cols]).then_inc(rec_done, 1)
            dve.wait_ge(rec_done, NC)
            dve.tensor_copy(sb["rec_in"][:], rec[0:D, :]).then_inc(done, 1)

        @block.scalar
        def _(act):
            for c in range(NC):
                cols = slice(c * CW, (c + 1) * CW)
                act.wait_ge(rec_done, c + 1)
                nc.scalar.activation(sb["rsqrt_in"][:, cols], rec[0:D, cols], ACT.Sqrt).then_inc(done, 1)
                nc.scalar.activation(sb["rsqrt_out"][:, cols], rec[D:P, cols], ACT.Sqrt).then_inc(done, 1)


def node_linear(nc, name, sb, acc, factor, terms, bias, out, relu=False):
    with ExitStack() as ctx:
        ph = Phase(nc, ctx, name)
        scaled, summed, done = ph.sem("scaled"), ph.sem("summed"), ph.sem("done")
        agg = ph.sb("agg", [D, NP])
        ps = ph.ps("ps", [P, NC, 512])
        block = ctx.enter_context(nc.Block())

        @block.vector
        def _(dve):
            for c in range(NC):
                dve.tensor_tensor(part(agg, c), part(acc, c), part(factor, c), ALU.mult).then_inc(scaled, 1)

        @block.tensor
        def _(pe):
            for c in range(NC):
                pe.wait_ge(scaled, c + 1)
                for k, (w, x) in enumerate(terms):
                    mm = nc.tensor.matmul(ps[0:D, c, 0:CW], w, part(agg if x is None else x, c),
                                          start=(k == 0), stop=(k == len(terms) - 1))
                mm.then_inc(summed, 1)

        @block.scalar
        def _(act):
            for c in range(NC):
                act.wait_ge(summed, c + 1)
                nc.scalar.activation(part(out, c), ps[0:D, c, 0:CW], ACT.Relu if relu else ACT.Identity,
                                     bias=bias[:, 0:1]).then_inc(done, 1)


def batch_norm(nc, name, sb, h, gamma, beta, relu):
    with ExitStack() as ctx:
        ph = Phase(nc, ctx, name)
        step, var_done, std_done, affine = (ph.sem(n) for n in ("step", "var_done", "std_done", "affine"))
        col = ph.sb("col", [D, 8])
        sq = ph.sb("sq", [D, N])
        block = ctx.enter_context(nc.Block())
        total, mean, sqsum, var, std, rstd, scale = (col[:, i:i + 1] for i in range(7))

        @block.vector
        def _(dve):
            dve.tensor_reduce(total, h[:, 0:N], AX_X, ALU.add).then_inc(step, 1)
            dve.wait_ge(step, 1)
            dve.tensor_scalar(mean, total, 1.0 / N, None, ALU.mult).then_inc(step, 1)
            dve.wait_ge(step, 2)
            dve.tensor_scalar(h[:], h[:], mean, None, ALU.subtract).then_inc(step, 1)
            dve.wait_ge(step, 3)
            dve.tensor_tensor(sq[:], h[:, 0:N], h[:, 0:N], ALU.mult).then_inc(step, 1)
            dve.wait_ge(step, 4)
            dve.tensor_reduce(sqsum, sq[:], AX_X, ALU.add).then_inc(step, 1)
            dve.wait_ge(step, 5)
            dve.tensor_scalar(var, sqsum, 1.0 / N, EPS, ALU.mult, ALU.add).then_inc(var_done, 1)
            dve.wait_ge(std_done, 1)
            dve.reciprocal(rstd, std).then_inc(step, 1)
            dve.wait_ge(step, 6)
            dve.tensor_tensor(scale, rstd, gamma[:], ALU.mult).then_inc(affine, 1)

        @block.scalar
        def _(act):
            act.wait_ge(var_done, 1)
            nc.scalar.activation(std, var, ACT.Sqrt).then_inc(std_done, 1)
            act.wait_ge(affine, 1)
            nc.scalar.activation(h[:], h[:], ACT.Relu if relu else ACT.Identity, bias=beta[:, 0:1],
                                 scale=scale).then_inc(std_done, 1)


def add_layer_norm(nc, name, sb, x, h):
    HALF = NC // 2
    with ExitStack() as ctx:
        ph = Phase(nc, ctx, name)
        sum_done, mean_done, centred, sq_done, var_done, std_done, rec_done, moved, done = (
            ph.sem(n) for n in ("sum_done", "mean_done", "centred", "sq_done", "var_done", "std_done", "rec_done",
                                "moved", "done"))
        sq = ph.sb("sq", [D, NP])
        std = ph.sb("std", [P, HALF, CW])
        rec = ph.sb("rec", [P, HALF, CW])
        rec_up = ph.sb("rec_up", [D, HALF, CW])
        ps = ph.ps("ps", [P, NC, 512])
        block = ctx.enter_context(nc.Block())
        order = [c for k in range(HALF) for c in (k, k + HALF)]

        @block.vector
        def _(dve):
            for c in order:
                dve.tensor_tensor(part(x, c), part(x, c), part(h, c), ALU.add).then_inc(sum_done, 1)
            for i, c in enumerate(order):
                dve.wait_ge(mean_done, i + 1)
                dve.tensor_tensor(part(x, c), part(x, c), ps[0:D, c, 0:CW], ALU.subtract).then_inc(centred, 1)
            for k in range(HALF):
                dve.wait_ge(std_done, k + 1)
                dve.reciprocal(rec[:, k, :], std[:, k, :]).then_inc(rec_done, 1)
                if k == HALF - 1:
                    dve.wait_ge(rec_done, HALF)
                    dve.tensor_tensor(part(x, k), part(x, k), rec[0:D, k, :], ALU.mult).then_inc(done, 1)
                    dve.wait_ge(moved, HALF)
                    dve.tensor_tensor(part(x, k + HALF), part(x, k + HALF), rec_up[:, k, :], ALU.mult).then_inc(done, 1)

        @block.gpsimd
        def _(pool):
            for k in range(HALF - 1):
                pool.wait_ge(rec_done, k + 1)
                pool.tensor_tensor(part(x, k), part(x, k), rec[0:D, k, :], ALU.mult).then_inc(done, 1)
                pool.wait_ge(moved, k + 1)
                pool.tensor_tensor(part(x, k + HALF), part(x, k + HALF), rec_up[:, k, :], ALU.mult).then_inc(done, 1)

        @block.tensor
        def _(pe):
            for i, c in enumerate(order):
                pe.wait_ge(sum_done, i + 1)
                nc.tensor.matmul(ps[0:D, c, 0:CW], sb["mean_mat"][:, D:2 * D], part(x, c), start=True, stop=True
                                 ).then_inc(mean_done, 1)
            for k in range(HALF):
                pe.wait_ge(sq_done, 2 * k + 2)
                nc.tensor.matmul(ps[:, k, 0:CW], sb["mean_mat"][:, D:3 * D], part(sq, k), start=True, stop=False)
                nc.tensor.matmul(ps[:, k, 0:CW], sb["mean_mat"][:, 0:2 * D], part(sq, k + HALF), start=False, stop=True
                                 ).then_inc(var_done, 1)

        @block.scalar
        def _(act):
            for i, c in enumerate(order):
                act.wait_ge(centred, i + 1)
                nc.scalar.activation(part(sq, c), part(x, c), ACT.Square).then_inc(sq_done, 1)
            for k in range(HALF + 1):
                if k < HALF:
                    act.wait_ge(var_done, k + 1)
                    nc.scalar.activation(std[:, k, :], ps[:, k, 0:CW], ACT.Sqrt, bias=sb["eps_col"][:, 0:1]
                                         ).then_inc(std_done, 1)
                if k >= 1:
                    act.wait_ge(rec_done, k)
                    nc.scalar.copy(rec_up[:, k - 1, :], rec[D:P, k - 1, :]).then_inc(moved, 1)


def write_rows(nc, name, sb, x, terms, width, outs, factor=None, bias=None):
    with ExitStack() as ctx:
        ph = Phase(nc, ctx, name)
        scaled, made, copied, out_sem = (ph.sem(n) for n in ("scaled", "made", "copied", "out"))
        rows = ph.sb("rows", [P, NB, width])
        xs = x if factor is None else ph.sb("xs", [D, NP])
        ps = ph.ps("ps", [P, 2, 512])
        block = ctx.enter_context(nc.Block())
        per = 512 // width
        rounds = [range(r, min(r + per, NB)) for r in range(0, NB, per)]

        @block.vector
        def _(dve):
            if factor is not None:
                dve.tensor_tensor(xs[:], x[:], factor[:], ALU.mult).then_inc(scaled, 1)
            for r, blocks in enumerate(rounds):
                dve.wait_ge(made, r + 1)
                k = len(blocks)
                src = ps[:, r % 2, 0:k * width].rearrange("p (b w) -> p b w", b=k)
                dst = rows[:, blocks[0]:blocks[0] + k, :]
                if bias is None:
                    dve.tensor_copy(dst, src).then_inc(copied, 1)
                else:
                    nc.vector.tensor_copy(dst[:, :, 0:D], src[:, :, 0:D])
                    dve.tensor_tensor(dst[:, :, D:2 * D], src[:, :, D:2 * D],
                                      bias[:].unsqueeze(1).to_broadcast([P, k, D]), ALU.add).then_inc(copied, 1)

        @block.tensor
        def _(pe):
            if factor is not None:
                pe.wait_ge(scaled, 1)
            for r, blocks in enumerate(rounds):
                if r >= 2:
                    pe.wait_ge(copied, r - 1)
                for b in blocks:
                    at = (b - blocks[0]) * width
                    for col, w in terms:
                        o = ps[:, r % 2, at + col:at + col + (D if w is None else w.shape[1])]
                        if w is None:
                            mm = nc.tensor.transpose(o, xs[:, b * P:(b + 1) * P], sb["ident"][0:D, 0:D])
                        else:
                            mm = nc.tensor.matmul(o, xs[:, b * P:(b + 1) * P], w, start=True, stop=True)
                mm.then_inc(made, 1)

        @block.sync
        def _(sp):
            sp.wait_ge(copied, len(rounds))
            n = 0
            for to, col, w in outs:
                full = to.shape[0] // P
                sp.dma_start(to[0:full * P, :].rearrange("(b p) f -> p b f", p=P),
                             rows[:, 0:full, col:col + w]).then_inc(out_sem, 16)
                n += 16
                if to.shape[0] % P:
                    sp.dma_start(to[full * P:, :], rows[0:to.shape[0] % P, full, col:col + w]).then_inc(out_sem, 16)
                    n += 16
            sp.wait_ge(out_sem, n)


def attention_loop(nc, dram, sb):
    with ExitStack() as ctx:
        ph = Phase(nc, ctx, "attn")
        two = range(2)
        idx_ready = [ph.sem(f"idx_ready{p}") for p in two]
        rows_in = [ph.sem(f"rows_in{p}") for p in two]
        feat_in = [ph.sem(f"feat_in{p}") for p in two]
        sh_in = [ph.sem(f"sh_in{p}") for p in two]
        dst_in = [ph.sem(f"dst_in{p}") for p in two]
        qwin_in = [ph.sem(f"qwin_in{p}") for p in two]
        xt_ps, hid_ps, q_ps, w_ps, k_ps, v_ps, vt_ps, attn_ps, sum_ps = (
            ph.sem(n) for n in ("xt_ps", "hid_ps", "q_ps", "w_ps", "k_ps", "v_ps", "vt_ps", "attn_ps", "sum_ps"))
        (pick_ready, z_ready, low_ready, ran, topped, shifted, onehot_ready, kw_ready, u_ready, vw_ready,
         dve_set) = (
            ph.sem(n) for n in ("pick_ready", "z_ready", "low_ready", "ran", "topped", "shifted", "onehot_ready",
                                "kw_ready", "u_ready", "vw_ready", "dve_set"))
        xt_sb, hid_sb, w_sb, ex_sb, vt_sb, sum_sb, high_sb, feat_high_sb = (
            ph.sem(n) for n in ("xt_sb", "hid_sb", "w_sb", "ex_sb", "vt_sb", "sum_sb", "high_sb",
                                "feat_high_sb"))
        masked, vx_ready = ph.sem("masked"), ph.sem("vx_ready")
        feat_low_ready = ph.sem("feat_low_ready")
        added, acc_clear = ph.sem("added"), ph.sem("acc_clear")
        STEPS = 2 + 2 * TG
        pool_go, pe_go = ph.sem("pool_go"), ph.sem("pe_go")

        idx = [ph.sb(f"idx{p}", [P, TG], I32) for p in two]
        rows = [ph.sb(f"rows{p}", [P, TG, 2 * D]) for p in two]
        feat = [ph.sb(f"feat{p}", [P, GE]) for p in two]
        feat_split = [ph.sb(f"feat_split{p}", [P, GE], F32R) for p in two]
        sh = [ph.sb(f"sh{p}", [P, KC, GE]) for p in two]
        dst = [ph.sb(f"dst{p}", [P, GE + 1]) for p in two]
        qwin = [ph.sb(f"qwin{p}", [P, TG, HD]) for p in two]
        xt = [ph.sb(f"xt{p}", [P, GE]) for p in two]
        z = ph.sb("z", [P, 2, GE])
        z_hi = [ph.sb(f"z_hi{p}", [P, KC, GE], F32R) for p in two]
        z_lo = [ph.sb(f"z_lo{p}", [P, KC - 1, GE], F32R) for p in two]
        hid = [ph.sb(f"hid{p}", [P, GE]) for p in two]
        wk = ph.sb("wk", [P, GE])
        wv = ph.sb("wv", [P, GE])
        pick = ph.sb("pick", [P, TG, P])
        onehot = ph.sb("onehot", [P, TG, P])
        u = ph.sb("u", [P, GE])
        vw = [ph.sb(f"vw{p}", [P, GE]) for p in two]
        vx = ph.sb("vx", [P, GE])
        mask = [ph.sb(f"mask{p}", [P, GE + 1]) for p in two]
        run = [ph.sb(f"run{p}", [P, GE]) for p in two]
        top = ph.sb("top", [P, GE])
        ex = [ph.sb(f"ex{p}", [P, GE + 1]) for p in two]
        zero = ph.sb("zero", [P, 1])
        vt = ph.sb("vt", [P, TG, HD])
        et = ph.sb("et", [P, TG, HD])
        sums = [ph.sb(f"sums{p}", [P, TG, P]) for p in two]
        dens = [ph.sb(f"dens{p}", [P, TG, P]) for p in two]

        b_xt, b_hid_vt, b_q, b_wk_sum, b_wv_den, b_k, b_v, b_attn = (
            ph.ps(n, [P, 512]) for n in ("b_xt", "b_hid_vt", "b_q", "b_wk_sum", "b_wv_den", "b_k", "b_v", "b_attn"))
        block = ctx.enter_context(nc.Block())

        def run_rounds(eng, prepare, body):
            prepare(0, 0, 0)
            body(0, 0, 0, True, True, False)
            body(1, 0, 1, True, True, True)
            body(2, 1, 0, True, True, True)
            body(3, 1, 1, True, True, True)
            with eng.Fori(2, G // 2 - 2) as n:
                for p in two:
                    body(2 * n + p, n, p, True, True, True)
            body(G - 4, G // 2 - 2, 0, True, True, True)
            body(G - 3, G // 2 - 2, 1, True, True, True)
            body(G - 2, G // 2 - 1, 0, True, True, True)
            body(G - 1, G // 2 - 1, 1, False, True, True)
            body(G, G // 2, 0, False, False, True)

        def after(g, n, p):
            return g + 1, n + p, 1 - p

        def is_first(g, k):
            return isinstance(g, int) and g == k

        @block.scalar
        def _(act):
            def stage_idx(g, p):
                nc.scalar.copy(idx[p][:], sb["src_i"][:, bass.ds(TG * g, TG)]).then_inc(idx_ready[p], 1)

            def empty(g, p):
                act.wait_ge(sum_ps, g + 1)
                if not (is_first(g, 0) or is_first(g, 1)):
                    act.wait_ge(added, STEPS * (g - 1))
                nc.scalar.copy(sums[p][:], b_wk_sum[:].rearrange("p (t c) -> p t c", t=TG)).then_inc(sum_sb, 1)
                nc.scalar.copy(dens[p][:], b_wv_den[:].rearrange("p (t c) -> p t c", t=TG)).then_inc(sum_sb, 1)

            def prepare(g, n, p):
                act.wait_ge(xt_ps, g + 1)
                nc.scalar.copy(xt[p][:], b_xt[:]).then_inc(xt_sb, 1)
                stage_idx(g + 2, p)
                if not (is_first(g, 0) or is_first(g, 1) or is_first(g, 2)):
                    empty(g - 3, 1 - p)
                high(g, p, 0)
                high(g, p, 1)
                act.wait_ge(hid_ps, g + 1)
                nc.scalar.activation(hid[p][:], b_hid_vt[:], ACT.Relu, bias=sb["L2_b1"][:, 0:1]).then_inc(hid_sb, 1)
                high(g, p, 2)

            def feat_high(g, n, p):
                act.wait_ge(feat_in[p], 32 * (n + 1))
                nc.scalar.copy(feat_split[p][:], feat[p][:]).then_inc(feat_high_sb, 1)

            def high(g, p, c):
                act.wait_ge(z_ready, KC * g + c + 1)
                nc.scalar.copy(z_hi[p][:, c, :], z[:, c % 2, :]).then_inc(high_sb, 1)

            def body(g, n, p, next, front, back):
                q = 1 - p
                if next:
                    prepare(*after(g, n, p))
                else:
                    empty(g - 2, p)
                if front:
                    act.wait_ge(w_ps, g + 1)
                    if not is_first(g, 0):
                        act.wait_ge(vw_ready, g)
                    nc.scalar.activation(wk[:], b_wk_sum[:], ACT.Identity, bias=sb["L2_k_b2"][:, 0:1]).then_inc(w_sb, 1)
                if next:
                    high(g + 1, q, 3)
                if front:
                    nc.scalar.activation(wv[:], b_wv_den[:], ACT.Identity, bias=sb["L2_v_b2"][:, 0:1]).then_inc(w_sb, 1)
                if next:
                    high(g + 1, q, 4)
                if back:
                    act.wait_ge(vt_ps, g)
                    nc.scalar.copy(vt[:], b_hid_vt[:].rearrange("p (t c) -> p t c", t=TG)).then_inc(vt_sb, 1)
                    nc.scalar.copy(et[:], b_wv_den[:].rearrange("p (t c) -> p t c", t=TG)).then_inc(vt_sb, 1)
                if not (isinstance(g, int) and g > G - 4):
                    feat_high(g + 3, n + 1 + p, q)
                if front:
                    act.wait_ge(shifted, 2 * g + 2)
                    nc.scalar.activation(ex[p][:], ex[p][:], ACT.Exp).then_inc(ex_sb, 1)
                if is_first(g, G):
                    empty(g - 1, q)

            def first(g, n, p):
                feat_high(0, 0, 0)
                feat_high(1, 0, 1)
                prepare(g, n, p)
                feat_high(2, 1, 0)
                high(g, p, 3)
                high(g, p, 4)

            stage_idx(0, 0)
            stage_idx(1, 1)
            run_rounds(act, first, body)

        @block.gpsimd
        def _(pool):
            def gather(g, n, p, first):
                pool.wait_ge(idx_ready[p], n + 1)
                if not first:
                    pool.wait_ge(xt_ps, g - 1)
                pool.sem_inc(pool_go, 1)
                for t in range(TG):
                    pool.indirect_dma_start(
                        rows[p][:, t, :], None, dram["x_twice"],
                        bass.IndirectOffsetOnAxis(ap=idx[p][:, t:t + 1], axis=0)).then_inc(rows_in[p], 16)

            def add(g, p):
                bases = window_bases(nc, mybir.EngineType.Pool, sb, TG * g)
                factor = ex[p][:, GE:GE + 1]
                steps = [(sb["acc"], bases[0], 1, factor, ALU.mult), (sb["den"], bases[0], 1, factor, ALU.mult)]
                for t in range(TG):
                    steps.append((sb["acc"], bases[t], P, sums[p][:, t, :], ALU.add))
                    steps.append((sb["den"], bases[t], P, dens[p][:, t, :], ALU.add))
                pool.wait_ge(sum_sb, 2 * (g + 1))
                for k, (acc, base, width, term, op) in enumerate(steps):
                    if k >= 2:
                        pool.wait_ge(added, STEPS * g + k - 1)
                    elif not is_first(g, 0):
                        pool.wait_ge(added, STEPS * g)
                    pool.sem_inc(pool_go, 1)
                    cols = bass.ds(base, width)
                    pool.tensor_tensor(acc[:, cols], acc[:, cols], term, op).then_inc(added, 1)

            pool.memset(sb["acc"][:], 0.0).then_inc(acc_clear, 1)
            pool.memset(sb["den"][:], 0.0).then_inc(acc_clear, 1)
            def make_mask(g, n, p, first):
                pool.wait_ge(dst_in[p], 16 * (n + 1))
                if not first:
                    pool.wait_ge(topped, g - 1)
                pool.tensor_tensor(mask[p][:, 0:GE], dst[p][:, 0:GE], dst[p][:, 1:GE + 1], ALU.subtract).then_inc(masked, 1)

            def weigh(g, p):
                pool.wait_ge(ex_sb, g + 1)
                pool.wait_ge(vw_ready, g + 1)
                if not is_first(g, 0):
                    pool.wait_ge(vt_ps, g)
                pool.tensor_tensor(vx[:], ex[p][:, 0:GE], vw[p][:], ALU.mult).then_inc(vx_ready, 1)

            for p in two:
                gather(p, 0, p, True)
            make_mask(0, 0, 0, True)
            pool.wait_ge(acc_clear, 2)
            gather(2, 1, 0, False)
            make_mask(1, 0, 1, True)
            weigh(0, 0)
            gather(3, 1, 1, False)
            make_mask(2, 1, 0, False)
            weigh(1, 1)
            gather(4, 2, 0, False)
            make_mask(3, 1, 1, False)
            add(0, 0)
            with pool.Fori(1, G // 2 - 2) as n:
                weigh(2 * n, 0)
                gather(2 * n + 3, n + 1, 1, False)
                make_mask(2 * n + 2, n + 1, 0, False)
                add(2 * n - 1, 1)
                weigh(2 * n + 1, 1)
                gather(2 * n + 4, n + 2, 0, False)
                make_mask(2 * n + 3, n + 1, 1, False)
                add(2 * n, 0)
            weigh(G - 4, 0)
            gather(G - 1, G // 2 - 1, 1, False)
            make_mask(G - 2, G // 2 - 1, 0, False)
            add(G - 5, 1)
            weigh(G - 3, 1)
            make_mask(G - 1, G // 2 - 1, 1, False)
            add(G - 4, 0)
            weigh(G - 2, 0)
            add(G - 3, 1)
            weigh(G - 1, 1)
            add(G - 2, 0)
            add(G - 1, 1)

        @block.sync
        def _(sp):
            def load(g, n, p, first):
                edges = bass.ds(g * GE, GE)
                if not first:
                    sp.wait_ge(feat_low_ready, g - 1)
                for k in two:
                    sp.dma_start(feat[p][k * D:(k + 1) * D, :], dram["edge_feat"][:, edges]).then_inc(feat_in[p], 16)
                bases = window_bases(nc, mybir.EngineType.SP, sb, TG * g)
                if not first:
                    sp.wait_ge(z_ready, KC * (g - 1))
                for k in two:
                    sp.dma_start(sh[p][k * D:(k + 1) * D, :, :], dram["edge_sh"][k::2, edges].partition_broadcast(D)
                                 ).then_inc(sh_in[p], 16)
                if not first:
                    sp.wait_ge(masked, g - 1)
                    sp.wait_ge(pick_ready, g - 1)
                sp.dma_start(dst[p][:], dram["dst_scaled"][bass.ds(g * GE, GE + 1)].partition_broadcast(P)
                             ).then_inc(dst_in[p], 16)
                if not first:
                    sp.wait_ge(q_ps, g - 1)
                for t in range(TG):
                    sp.dma_start(qwin[p][:, t, :], dram["q_rows"][bass.ds(bases[t], P), :]).then_inc(qwin_in[p], 16)

            for p in two:
                load(p, 0, p, True)
            with sp.Fori(1, G // 2) as n:
                for p in two:
                    load(2 * n + p, n, p, False)

        @block.tensor
        def _(pe):
            def prepare(g, n, p):
                pe.wait_ge(rows_in[p], 64 * (n + 1))
                if not is_first(g, 0):
                    pe.wait_ge(xt_sb, g)
                for t in range(TG):
                    mm = nc.tensor.transpose(b_xt[:, t * P:(t + 1) * P], rows[p][:, t, :], sb["ident"][:])
                mm.then_inc(xt_ps, 1)
                pe.wait_ge(feat_low_ready, g + 1)
                if is_first(g, 1) or is_first(g, 2):
                    pe.wait_ge(hid_sb, g)
                nc.tensor.matmul(b_hid_vt[:], sb["L2_w1_hi"][:], feat_split[p][:], start=True, stop=False)
                nc.tensor.matmul(b_hid_vt[:], sb["L2_w1_lo"][:], feat_split[p][0:D, :], start=False, stop=True
                                 ).then_inc(hid_ps, 1)

            def pick_q(g, n, p):
                pe.wait_ge(qwin_in[p], 64 * (n + 1))
                pe.wait_ge(pick_ready, g + 1)
                for t in range(TG):
                    mm = nc.tensor.matmul(b_q[:, t * P:(t + 1) * P], qwin[p][:, t, :], pick[:, t, :],
                                          start=True, stop=True)
                mm.then_inc(q_ps, 1)

            def split_product(bank, name, g, p, waits):
                hi, lo = sb[name + "_hi"], sb[name + "_lo"]
                for c in range(KC - 1):
                    if waits:
                        pe.wait_ge(low_ready, KC * g + c + 1)
                    nc.tensor.matmul(bank[:], hi[:, c, :], z_hi[p][:, c, :], start=(c == 0), stop=False)
                    nc.tensor.matmul(bank[:], lo[:, c, :], z_hi[p][:, c, :], start=False, stop=False)
                    nc.tensor.matmul(bank[:], hi[:, c, :], z_lo[p][:, c, :], start=False, stop=False)
                if waits:
                    pe.wait_ge(low_ready, KC * (g + 1))
                nc.tensor.matmul(bank[:], hi[:, KC - 1, :], z_hi[p][:, KC - 1, :], start=False, stop=False)
                return nc.tensor.matmul(bank[:], lo[0:D, KC - 1, :], z_hi[p][0:D, KC - 1, :], start=False, stop=True)

            def body(g, n, p, next, front, back):
                q = 1 - p
                if next:
                    prepare(*after(g, n, p))
                if front:
                    split_product(b_k, "L2_Cqk", g, p, True).then_inc(k_ps, 1)
                    pe.wait_ge(hid_sb, g + 1)
                    if is_first(g, 1):
                        pe.wait_ge(w_sb, 2)
                    elif back:
                        pe.wait_ge(sum_sb, 2 * (g - 1))
                        pe.sem_inc(pe_go, 1)
                    nc.tensor.matmul(b_wk_sum[:], sb["L2_w2"][0:D, :], hid[p][0:D, :], start=True, stop=True)
                    nc.tensor.matmul(b_wv_den[:], sb["L2_w2"][D:P, :], hid[p][D:P, :], start=True,
                                     stop=True).then_inc(w_ps, 1)
                    if back:
                        pe.wait_ge(vw_ready, g)
                    split_product(b_v, "L2_Cv", g, p, False).then_inc(v_ps, 1)
                if back:
                    pe.wait_ge(vx_ready, g)
                    if front:
                        pe.wait_ge(w_sb, 2 * (g + 1))
                    else:
                        pe.wait_ge(sum_sb, 2 * (g - 1))
                    if next:
                        pe.wait_ge(hid_sb, g + 2)
                    for t in range(TG):
                        nc.tensor.transpose(b_hid_vt[:, t * P:(t + 1) * P], vx[:, t * P:(t + 1) * P], sb["ident"][:])
                    for t in range(TG):
                        mm = nc.tensor.transpose(b_wv_den[:, t * P:(t + 1) * P], ex[q][:, t * P:(t + 1) * P],
                                                 sb["ident"][:])
                    mm.then_inc(vt_ps, 1)
                if front:
                    pe.wait_ge(u_ready, g + 1)
                    nc.tensor.matmul(b_attn[:], sb["head_sum"][:], u[:], start=True, stop=True).then_inc(attn_ps, 1)
                if next:
                    pick_q(*after(g, n, p))
                if back:
                    pe.wait_ge(vt_sb, 2 * g)
                    pe.wait_ge(onehot_ready, g)
                    for t in range(TG):
                        nc.tensor.matmul(b_wk_sum[:, t * P:(t + 1) * P], vt[:, t, :], onehot[:, t, :],
                                         start=True, stop=True)
                    for t in range(TG):
                        mm = nc.tensor.matmul(b_wv_den[:, t * P:(t + 1) * P], et[:, t, :], onehot[:, t, :],
                                              start=True, stop=True)
                    mm.then_inc(sum_ps, 1)

            def first(g, n, p):
                prepare(g, n, p)
                pick_q(g, n, p)

            run_rounds(pe, first, body)

        @block.vector
        def _(dve):
            dve.memset(run[1][:], LOWEST).then_inc(dve_set, 1)
            dve.memset(mask[0][:, GE:GE + 1], 0.0).then_inc(dve_set, 1)
            dve.memset(mask[1][:, GE:GE + 1], 0.0).then_inc(dve_set, 1)
            dve.memset(zero[:], 0.0).then_inc(dve_set, 1)

            def backward(t, n):
                a = t[:]
                return bass.AP(a.tensor, a.offset + n - 1, [list(a.ap[0]), [-1, GE]])

            def make_pick(g, n, p):
                dve.wait_ge(dst_in[p], 16 * (n + 1))
                if not is_first(g, 0):
                    dve.wait_ge(q_ps, g)
                dve.tensor_tensor(pick[:], dst[p][:, 1:GE + 1].rearrange("p (t e) -> p t e", t=TG),
                                  sb["node_of_part"][:, bass.ds(TG * g, TG)].unsqueeze(2).to_broadcast([P, TG, P]),
                                  ALU.is_equal).then_inc(pick_ready, 1)

            def feat_low(g, p):
                dve.wait_ge(feat_high_sb, g + 1)
                dve.tensor_tensor(feat_split[p][D:P, :], feat[p][D:P, :], feat_split[p][D:P, :].bitcast(F32),
                                  ALU.subtract).then_inc(feat_low_ready, 1)

            def make(g, n, p, c):
                if c == 0:
                    dve.wait_ge(sh_in[p], 32 * (n + 1))
                    dve.wait_ge(xt_sb, g + 1)
                if c >= 2:
                    dve.wait_ge(low_ready, KC * g + c - 1)
                elif not is_first(g, 0):
                    dve.wait_ge(low_ready, KC * g)
                dve.tensor_tensor(z[:, c % 2, :], xt[p][:], sh[p][:, c, :], ALU.mult).then_inc(z_ready, 1)

            def low(g, n, p, c):
                dve.wait_ge(high_sb, KC * g + c + 1)
                if c < KC - 1:
                    dve.tensor_tensor(z_lo[p][:, c, :], z[:, c % 2, :], z_hi[p][:, c, :].bitcast(F32),
                                      ALU.subtract).then_inc(low_ready, 1)
                else:
                    dve.tensor_tensor(z_hi[p][D:P, c, :], z[D:P, c % 2, :], z_hi[p][D:P, c, :].bitcast(F32),
                                      ALU.subtract).then_inc(low_ready, 1)

            def split_begin(*group):
                make(*group, 0)
                make(*group, 1)
                low(*group, 0)
                make(*group, 2)
                low(*group, 1)
                make(*group, 3)
                low(*group, 2)

            def split_end(*group):
                make(*group, 4)
                low(*group, 3)
                low(*group, 4)

            def maxima(g, n, p):
                q = 1 - p
                dve.wait_ge(attn_ps, g + 1)
                dve.wait_ge(masked, g + 1)
                dve.tensor_tensor_scan(run[p][:], mask[p][:, 0:GE], b_attn[:], run[q][:, GE - 1:GE],
                                       ALU.add, ALU.max).then_inc(ran, 1)
                dve.wait_ge(ran, g + 1)
                dve.tensor_tensor_scan(backward(top, GE), backward(mask[p], GE + 1), backward(run[p], GE), LOWEST,
                                       ALU.add, ALU.max).then_inc(topped, 1)
                dve.wait_ge(topped, g + 1)
                if not (is_first(g, 0) or is_first(g, 1)):
                    dve.wait_ge(added, STEPS * (g - 2) + 2)
                dve.tensor_tensor(ex[p][:, 0:GE], b_attn[:], top[:], ALU.subtract).then_inc(shifted, 1)
                dve.scalar_tensor_tensor(out=ex[p][:, GE:GE + 1], in0=run[q][:, GE - 1:GE], scalar=top[:, 0:1],
                                         in1=zero[:], op0=ALU.subtract, op1=ALU.min).then_inc(shifted, 1)

            def body(g, n, p, next, front, back):
                if next:
                    make_pick(*after(g, n, p))
                if back:
                    if not is_first(g, 1):
                        dve.wait_ge(sum_ps, g - 1)
                    dve.tensor_tensor(onehot[:], sb["iota_row"][:].unsqueeze(1).to_broadcast([P, TG, P]),
                                      sb["dst_local"][:, bass.ds(TG * g - TG, TG)].unsqueeze(2).to_broadcast([P, TG, P]),
                                      ALU.is_equal).then_inc(onehot_ready, 1)
                if next:
                    if not is_first(g, G - 2):
                        feat_low(g + 2, p)
                    split_begin(*after(g, n, p))
                if front:
                    dve.wait_ge(k_ps, g + 1)
                    dve.wait_ge(w_sb, 2 * g + 1)
                    dve.tensor_tensor(u[:], b_k[:], wk[:], ALU.mult).then_inc(kw_ready, 1)
                    dve.wait_ge(q_ps, g + 1)
                    dve.wait_ge(kw_ready, g + 1)
                    dve.tensor_tensor(u[:], b_q[:], u[:], ALU.mult).then_inc(u_ready, 1)
                if next:
                    split_end(*after(g, n, p))
                if front:
                    dve.wait_ge(v_ps, g + 1)
                    dve.wait_ge(w_sb, 2 * g + 2)
                    dve.tensor_tensor(vw[p][:], b_v[:], wv[:], ALU.mult).then_inc(vw_ready, 1)
                if front:
                    maxima(g, n, p)

            def first(g, n, p):
                feat_low(0, 0)
                feat_low(1, 1)
                make_pick(g, n, p)
                split_begin(g, n, p)
                split_end(g, n, p)

            dve.wait_ge(dve_set, 4)
            run_rounds(dve, first, body)


def attention_out(nc, sb, h):
    with ExitStack() as ctx:
        ph = Phase(nc, ctx, "attn_out")
        shifted, inverted, scaled, summed, done = (ph.sem(n) for n in ("shifted", "inverted", "scaled", "summed", "done"))
        rec = ph.sb("rec", [P, NP])
        ps = ph.ps("ps", [P, NC, 512])
        block = ctx.enter_context(nc.Block())

        def cols(t, c):
            return t[:, c * CW:(c + 1) * CW]

        @block.vector
        def _(dve):
            for c in range(NC):
                dve.tensor_scalar(cols(sb["den"], c), cols(sb["den"], c), 1e-16, None, ALU.add).then_inc(shifted, 1)
            for c in range(NC):
                dve.wait_ge(shifted, c + 1)
                dve.reciprocal(cols(rec, c), cols(sb["den"], c)).then_inc(inverted, 1)

        @block.gpsimd
        def _(pool):
            for c in range(NC):
                pool.wait_ge(inverted, c + 1)
                pool.tensor_tensor(cols(sb["acc"], c), cols(sb["acc"], c), cols(rec, c), ALU.mult).then_inc(scaled, 1)

        @block.tensor
        def _(pe):
            for c in range(NC):
                nc.tensor.matmul(ps[0:D, c, 0:CW], sb["L2_W_self"][:], part(sb["x_t"], c), start=True, stop=False)
                pe.wait_ge(scaled, c + 1)
                nc.tensor.matmul(ps[0:D, c, 0:CW], sb["L2_W_out"][:], cols(sb["acc"], c), start=False, stop=True
                                 ).then_inc(summed, 1)

        @block.scalar
        def _(act):
            for c in range(NC):
                act.wait_ge(summed, c + 1)
                nc.scalar.copy(part(h, c), ps[0:D, c, 0:CW]).then_inc(done, 1)


def message_loop(nc, dram, sb):
    with ExitStack() as ctx:
        ph = Phase(nc, ctx, "msg")
        two = range(2)
        idx_ready = [ph.sem(f"idx_ready{p}") for p in two]
        rows_in = [ph.sem(f"rows_in{p}") for p in two]
        dst_in = [ph.sem(f"dst_in{p}") for p in two]
        bwin_in = [ph.sem(f"bwin_in{p}") for p in two]
        pick_ready, onehot_ready, picked, pre_ready, msg_ready, sums_ready, added, pool_go, acc_clear = (
            ph.sem(n) for n in ("pick_ready", "onehot_ready", "picked", "pre_ready", "msg_ready", "sums_ready", "added",
                                "pool_go", "acc_clear"))
        idx = [ph.sb(f"idx{p}", [P, TG], I32) for p in two]
        rows = [ph.sb(f"rows{p}", [P, TG, D]) for p in two]
        dst = [ph.sb(f"dst{p}", [P, TG, P]) for p in two]
        bwin = [ph.sb(f"bwin{p}", [P, TG, D]) for p in two]
        pick = [ph.sb(f"pick{p}", [P, TG, P]) for p in two]
        onehot = [ph.sb(f"onehot{p}", [P, TG, P]) for p in two]
        pre = [ph.sb(f"pre{p}", [P, TG, D]) for p in two]
        msg = [ph.sb(f"msg{p}", [P, TG, D]) for p in two]
        at_dst = [ph.ps(f"at_dst{p}", [P, 512]) for p in two]
        sums = [ph.ps(f"sums{p}", [P, TG, P]) for p in two]
        block = ctx.enter_context(nc.Block())

        def is_first(g, k):
            return isinstance(g, int) and g == k

        def run_steps(eng, step):
            for g in range(4):
                step(g, g // 2, g % 2)
            with eng.Fori(2, G // 2 - 1) as n:
                for p in two:
                    step(2 * n + p, n, p)
            step(G - 2, G // 2 - 1, 0)
            step(G - 1, G // 2 - 1, 1, last=True)

        @block.scalar
        def _(act):
            def stage(g, p):
                nc.scalar.copy(idx[p][:], sb["src_i"][:, bass.ds(TG * g, TG)]).then_inc(idx_ready[p], 1)

            def relu(g, p, first):
                act.wait_ge(pre_ready, g + 1)
                if not first:
                    act.wait_ge(sums_ready, g - 1)
                nc.scalar.activation(msg[p][:], pre[p][:], ACT.Relu).then_inc(msg_ready, 1)

            for p in two:
                stage(p, p)
            for p in two:
                relu(p, p, True)
                stage(p + 2, p)
            with act.Fori(1, G // 2 - 1) as n:
                for p in two:
                    relu(2 * n + p, p, False)
                    stage(2 * n + p + 2, p)
            for p in two:
                relu(G - 2 + p, p, False)

        @block.gpsimd
        def _(pool):
            def gather(g, n, p, first):
                pool.wait_ge(idx_ready[p], n + 1)
                if not first:
                    pool.wait_ge(pre_ready, g - 1)
                pool.sem_inc(pool_go, 1)
                for t in range(TG):
                    pool.indirect_dma_start(
                        rows[p][:, t, :], None, dram["a_rows"],
                        bass.IndirectOffsetOnAxis(ap=idx[p][:, t:t + 1], axis=0)).then_inc(rows_in[p], 16)

            for p in two:
                gather(p, 0, p, True)
            with pool.Fori(1, G // 2) as n:
                for p in two:
                    gather(2 * n + p, n, p, False)

        @block.sync
        def _(sp):
            def load(g, p, first):
                if not first:
                    sp.wait_ge(pick_ready, g - 1)
                sp.dma_start(dst[p][:].rearrange("p t e -> p (t e)"),
                             dram["dst_scaled"][bass.ds(g * GE + 1, GE)].partition_broadcast(P)).then_inc(dst_in[p], 16)
                if not first:
                    sp.wait_ge(picked, g - 1)
                bases = window_bases(nc, mybir.EngineType.SP, sb, TG * g)
                for t in range(TG):
                    sp.dma_start(bwin[p][:, t, :], dram["b_rows"][bass.ds(bases[t], P), :]).then_inc(bwin_in[p], 16)

            for p in two:
                load(p, p, True)
            with sp.Fori(1, G // 2) as n:
                for p in two:
                    load(2 * n + p, p, False)

        @block.tensor
        def _(pe):
            def choose(g, n, p):
                pe.wait_ge(bwin_in[p], 64 * (n + 1))
                pe.wait_ge(pick_ready, g + 1)
                if not (is_first(g, 0) or is_first(g, 1)):
                    pe.wait_ge(pre_ready, g - 1)
                for t in range(TG):
                    mm = nc.tensor.matmul(at_dst[p][:, t * D:(t + 1) * D], pick[p][:, t, :], bwin[p][:, t, :],
                                          start=True, stop=True)
                mm.then_inc(picked, 1)

            def total(g, p):
                pe.wait_ge(msg_ready, g + 1)
                pe.wait_ge(onehot_ready, g + 1)
                if not (is_first(g, 0) or is_first(g, 1)):
                    pe.wait_ge(added, TG * (g - 1))
                for t in range(TG):
                    mm = nc.tensor.matmul(sums[p][0:D, t, :], msg[p][:, t, :], onehot[p][:, t, :], start=True, stop=True)
                mm.then_inc(sums_ready, 1)

            def step(g, n, p, last=False):
                if not last:
                    choose(g + 1, n + p, 1 - p)
                total(g, p)

            choose(0, 0, 0)
            run_steps(pe, step)

        @block.vector
        def _(dve):
            def make_pick(g, n, p):
                dve.wait_ge(dst_in[p], 16 * (n + 1))
                dve.tensor_tensor(pick[p][:], dst[p][:],
                                  sb["node_of_part"][:, bass.ds(TG * g, TG)].unsqueeze(2).to_broadcast([P, TG, P]),
                                  ALU.is_equal).then_inc(pick_ready, 1)

            def make_onehot(g, p):
                dve.tensor_tensor(onehot[p][:], sb["iota_row"][:].unsqueeze(1).to_broadcast([P, TG, P]),
                                  sb["dst_local"][:, bass.ds(TG * g, TG)].unsqueeze(2).to_broadcast([P, TG, P]),
                                  ALU.is_equal).then_inc(onehot_ready, 1)

            def join(g, n, p):
                dve.wait_ge(rows_in[p], 64 * (n + 1))
                dve.wait_ge(picked, g + 1)
                if not (is_first(g, 0) or is_first(g, 1)):
                    dve.wait_ge(msg_ready, g - 1)
                dve.tensor_tensor(pre[p][:], rows[p][:], at_dst[p][:, 0:TG * D].rearrange("p (t d) -> p t d", t=TG),
                                  ALU.add).then_inc(pre_ready, 1)

            def add(g, p):
                bases = window_bases(nc, mybir.EngineType.DVE, sb, TG * g)
                for t in range(TG):
                    base = bases[t]
                    if t == 0:
                        dve.wait_ge(sums_ready, g + 1)
                    if not (is_first(g, 0) and t == 0):
                        dve.wait_ge(added, TG * g + t)
                    cols = bass.ds(base, P)
                    dve.tensor_tensor(sb["acc"][0:D, cols], sb["acc"][0:D, cols], sums[p][0:D, t, :],
                                      ALU.add).then_inc(added, 1)

            def step(g, n, p, last=False):
                join(g, n, p)
                if not last:
                    make_pick(g + 1, n + p, 1 - p)
                if not is_first(g, 0):
                    add(g - 1, 1 - p)
                if not last:
                    make_onehot(g + 1, 1 - p)

            dve.memset(sb["acc"][:], 0.0).then_inc(acc_clear, 1)
            dve.wait_ge(acc_clear, 1)
            make_pick(0, 0, 0)
            make_onehot(0, 0)
            run_steps(dve, step)
            add(G - 1, 1)


def program(nc, dram, out):
    Phase.sems.clear()
    with ExitStack() as ctx:
        sb = {}

        def table(name, shape, dt=F32):
            sb[name] = ctx.enter_context(nc.sbuf_tensor(name, shape, dt))

        table("src_i", [P, T + 2 * TG], I32)
        table("dst_i", [P, T], I32)
        for name in ("dst_local", "node_of_part"):
            table(name, [P, T])
        table("iota_row", [P, P])
        table("iota_col", [P, 1])
        table("ident", [P, P])
        table("mean_mat", [D, 3 * D])
        table("eps_col", [P, 1])
        table("cnt_spread", [D + 1, D])
        table("head_sum", [HD, HD])
        for name in ("L0_W_l", "L0_W_r", "L1_W", "L2_W_self", "L3_W_upd_x", "L3_W_upd_a"):
            table(name, [D, D])
        table("L2_W_out", [HD, D])
        table("L2_Wq", [D, HD])
        for name in ("L0_b_l", "L0_gamma", "L0_beta", "L1_b", "L2_gamma", "L2_beta", "L3_b_upd"):
            table(name, [D, 1])
        table("L2_w1_hi", [P, 2 * D], F32R)
        table("L2_w1_lo", [D, 2 * D], F32R)
        table("L2_b1", [2 * D, 1])
        table("L2_w2", [2 * D, HD])
        table("L2_k_b2", [HD, 1])
        table("L2_v_b2", [HD, 1])
        for name in ("L2_Cqk_hi", "L2_Cqk_lo", "L2_Cv_hi", "L2_Cv_lo"):
            table(name, [P, KC, HD], F32R)
        table("L3_W_msg", [D, 2 * D])
        table("L3_b_msg", [P, D])
        table("x_t", [D, NP])
        table("acc", [P, NP])
        table("den", [HD, NP])
        sb["deg_out_sem"] = ctx.enter_context(nc.semaphore("deg_out"))

        def scratch(name, shape):
            dram[name] = nc.dram_tensor(name, shape, F32, kind="Internal").ap()

        scratch("dst_scaled", (EP + 1,))
        scratch("out_deg_line", (NP,))
        scratch("rec_in_kept", (D, NP))
        scratch("x1_rows", (NP, D))
        scratch("x_twice", (NP, 2 * D))
        scratch("q_rows", (NP, HD))
        scratch("a_rows", (NP, D))
        scratch("b_rows", (NP, D))
        sb["dram_out_deg"] = dram["out_deg_line"]

        with ExitStack() as early:
            for name in ("src_hi", "src_lo"):
                sb[name] = early.enter_context(nc.sbuf_tensor(name, [P, T], F32))
            sb["out_deg"] = early.enter_context(nc.sbuf_tensor("out_deg", [NB, P], F32))
            setup(nc, dram, sb)
            for name in ("h", "rsqrt_in", "rsqrt_out", "rec_in"):
                sb[name] = early.enter_context(nc.sbuf_tensor(name, [D, NP], F32))
            sum_loop(nc, "sum0", dram["x"], sb, sb["acc"], True)
            count_reciprocals(nc, sb)
            node_linear(nc, "lin0", sb, sb["acc"], sb["rec_in"],
                        [(sb["L0_W_l"][:], None), (sb["L0_W_r"][:], sb["x_t"])], sb["L0_b_l"], sb["h"])
            batch_norm(nc, "bn0", sb, sb["h"], sb["L0_gamma"], sb["L0_beta"], True)
            add_layer_norm(nc, "ln0", sb, sb["x_t"], sb["h"])
            write_rows(nc, "rows1", sb, sb["x_t"], [(0, None)], D, [(dram["x1_rows"], 0, D)], factor=sb["rsqrt_out"])
            sum_loop(nc, "sum1", dram["x1_rows"], sb, sb["acc"], False)
            node_linear(nc, "lin1", sb, sb["acc"], sb["rsqrt_in"], [(sb["L1_W"][:], None)], sb["L1_b"], sb["h"])
            add_layer_norm(nc, "ln1", sb, sb["x_t"], sb["h"])
            move(nc, "rec_out", dram["rec_in_kept"], sb["rec_in"][:])
        write_rows(nc, "rows2", sb, sb["x_t"], [(0, None), (D, None), (2 * D, sb["L2_Wq"][:])], 4 * D,
                   [(dram["x_twice"], 0, 2 * D), (dram["q_rows"], 2 * D, HD)])
        recycle(nc)
        attention_loop(nc, dram, sb)
        sb["h"] = ctx.enter_context(nc.sbuf_tensor("h_late", [D, NP], F32))
        attention_out(nc, sb, sb["h"])
        batch_norm(nc, "bn2", sb, sb["h"], sb["L2_gamma"], sb["L2_beta"], False)
        add_layer_norm(nc, "ln2", sb, sb["x_t"], sb["h"])
        sb["rec_in"] = ctx.enter_context(nc.sbuf_tensor("rec_in_late", [D, NP], F32))
        move(nc, "rec_back", sb["rec_in"][:], dram["rec_in_kept"])
        write_rows(nc, "rows3", sb, sb["x_t"], [(0, sb["L3_W_msg"][:])], 2 * D,
                   [(dram["a_rows"], 0, D), (dram["b_rows"], D, D)], bias=sb["L3_b_msg"])
        message_loop(nc, dram, sb)
        node_linear(nc, "lin3", sb, sb["acc"], sb["rec_in"],
                    [(sb["L3_W_upd_x"][:], sb["x_t"]), (sb["L3_W_upd_a"][:], None)], sb["L3_b_upd"], sb["h"], relu=True)
        add_layer_norm(nc, "ln3", sb, sb["x_t"], sb["h"])
        write_rows(nc, "rows4", sb, sb["x_t"], [(0, None)], D, [(out, 0, D)])


def kernel(**inputs):
    import numpy as np
    import concourse.bacc as bacc
    from concourse.bass_utils import run_bass_kernel_spmd

    nc = bacc.Bacc("TRN2", target_bir_lowering=False, num_devices=1)
    a = {k: np.asarray(v) for k, v in inputs.items()}
    pad = EP - E
    src = np.concatenate([a["src"], np.full(pad, PADN, a["src"].dtype)])
    dst = np.concatenate([a["dst"], np.full(pad, PADN, a["dst"].dtype)])
    arrays = {
        "x": np.concatenate([a["x"], np.zeros((NP - N, D), a["x"].dtype)]),
        "x_t": np.concatenate([a["x"].T, np.zeros((D, NP - N), a["x"].dtype)], axis=1),
        "src_tab": src.reshape(T, P).T,
        "dst_tab": dst.reshape(T, P).T,
        "dst_line": dst,
        "edge_feat": np.concatenate([a["edge_attr_64"].T, np.zeros((D, pad), a["edge_attr_64"].dtype)], axis=1),
        "edge_sh": np.concatenate([a["edge_attr_9"].T[[*range(S_SH), S_SH - 1]],
                                   np.zeros((S_SH + 1, pad), a["edge_attr_9"].dtype)], axis=1),
        "L2_Cqk": a["L2_gnn_Cqk"].transpose(1, 0, 2).reshape(S_SH * D, HD),
        "L2_Cv": a["L2_gnn_Cv"].transpose(1, 0, 2).reshape(S_SH * D, HD),
    }
    for name, value in a.items():
        short = name.replace("_gnn_", "_")
        if name[0] == "L" and short not in arrays:
            arrays[short] = value
    arrays = {k: np.ascontiguousarray(v) for k, v in arrays.items()}
    dram = {k: nc.dram_tensor("in_" + k, v.shape, mybir.dt.from_np(v.dtype), kind="ExternalInput").ap()
            for k, v in arrays.items()}
    out = nc.dram_tensor("out", (N, D), F32, kind="ExternalOutput").ap()
    program(nc, dram, out)
    r = run_bass_kernel_spmd(nc, [{"in_" + k: v for k, v in arrays.items()}], core_ids=[0])
    return r.results[0]["out"]
```
